# Optimizing a Trainium2 kernel written in Bass

```python
import numpy as np
import jax
import jax.numpy as jnp

def _softmax(x, axis=-1):
    return jax.nn.softmax(x, axis=axis)

def _gelu(x):
    return jax.nn.gelu(x, approximate=True)

def _silu(x):
    return jax.nn.silu(x)

def _sigmoid(x):
    return jax.nn.sigmoid(x)

def _layernorm(x, axis=-1, eps=1e-05):
    m = jnp.mean(x, axis=axis, keepdims=True)
    v = jnp.var(x, axis=axis, keepdims=True)
    return (x - m) / jnp.sqrt(v + eps)

def _scatter_add(tgt, idx, src, axis=0):
    return tgt.at[idx].add(src)

def _segment_sum(src, seg, n):
    return jax.ops.segment_sum(src, seg, n)
kernel_name = 'mk_gnn_resnorm_d1_gnn_r8_ec00a8'

def setup_inputs(seed: int=0):
    np.random.seed(seed)
    _w = jnp.asarray

    def _rec_inputs():
        import jax
        import jax.numpy as jnp
        _gk = jax.random.key(seed)
        x = -0.000202 + 1 * jax.random.normal(jax.random.fold_in(_gk, 1), (6250, 128), jnp.float32)
        src = jax.random.randint(jax.random.fold_in(_gk, 2), (200000,), 0, 6250, jnp.int32)
        dst = jnp.minimum((6250 * jax.random.uniform(jax.random.fold_in(_gk, 3), (200000,)) ** 2.0).astype(jnp.int32), 49999)
        _o = jnp.argsort(dst, stable=True)
        src = src[_o]
        dst = dst[_o]
        edge_attr_128 = -4.21973e-05 + 0.999841 * jax.random.normal(jax.random.fold_in(_gk, 12), (200000, 128), jnp.float32)
        return (x, src, dst, edge_attr_128)
    x, src, dst, edge_attr_128 = _rec_inputs()

    def _L0_gnn_setup():
        import jax, jax.numpy as jnp
        import numpy as np
        EPS = 1e-05

        def layer_norm(x, g, b):
            m = x.mean(-1, keepdims=True)
            v = ((x - m) ** 2).mean(-1, keepdims=True)
            return (x - m) * jax.lax.rsqrt(v + EPS) * g + b
        H, N, E, F = (8, 6250, 75000, 128)
        D = F // H
        key = jax.random.key(seed)
        ks = jax.random.split(key, 16)
        f32 = jnp.float32
        sF = 1.0 / np.sqrt(F)
        s2D = 1.0 / np.sqrt(2 * D)
        sD = 1.0 / np.sqrt(D)
        inp = {'x_node': jax.random.normal(ks[0], (N, F), f32), 'x_edge': jax.random.normal(ks[1], (E, F), f32), 'src': jax.random.randint(ks[2], (E,), 0, N, jnp.int32), 'dst': jax.random.randint(ks[3], (E,), 0, N, jnp.int32), 'Wq': jax.random.normal(ks[4], (H, F, D), f32) * sF, 'Wk': jax.random.normal(ks[5], (H, F, D), f32) * sF, 'Wv': jax.random.normal(ks[6], (H, F, D), f32) * sF, 'Wke': jax.random.normal(ks[7], (H, F, D), f32) * sF, 'Wve': jax.random.normal(ks[8], (H, F, D), f32) * sF, 'gq': jnp.ones((H, D), f32), 'bq': jnp.zeros((H, D), f32), 'gk': jnp.ones((H, D), f32), 'bk': jnp.zeros((H, D), f32), 'gv': jnp.ones((H, D), f32), 'bv': jnp.zeros((H, D), f32), 'gke': jnp.ones((H, D), f32), 'bke': jnp.zeros((H, D), f32), 'gve': jnp.ones((H, D), f32), 'bve': jnp.zeros((H, D), f32), 'relk_W': jax.random.normal(ks[9], (2 * D, D), f32) * s2D, 'relk_b': jnp.zeros((D,), f32), 'relk_g': jnp.ones((D,), f32), 'relk_beta': jnp.zeros((D,), f32), 'relv_W': jax.random.normal(ks[10], (2 * D, D), f32) * s2D, 'relv_b': jnp.zeros((D,), f32), 'relv_g': jnp.ones((D,), f32), 'relv_beta': jnp.zeros((D,), f32), 'z_W': jax.random.normal(ks[11], (D, D), f32) * sD, 'z_b': jnp.zeros((D,), f32), 'z_g': jnp.ones((D,), f32), 'z_beta': jnp.zeros((D,), f32)}
        return inp
    _L0_gnn_all = _L0_gnn_setup()
    _L0_gnn_in = {k: v for k, v in _L0_gnn_all.items() if k in ('Wq', 'Wk', 'Wv', 'Wke', 'Wve', 'gq', 'bq', 'gk', 'bk', 'gv', 'bv', 'gke', 'bke', 'gve', 'bve', 'relk_W', 'relk_b', 'relk_g', 'relk_beta', 'relv_W', 'relv_b', 'relv_g', 'relv_beta', 'z_W', 'z_b', 'z_g', 'z_beta')}
    del _L0_gnn_all
    return {'x': x, 'src': src, 'dst': dst, 'edge_attr_128': edge_attr_128, 'L0_gnn_Wq': _L0_gnn_in['Wq'], 'L0_gnn_Wk': _L0_gnn_in['Wk'], 'L0_gnn_Wv': _L0_gnn_in['Wv'], 'L0_gnn_Wke': _L0_gnn_in['Wke'], 'L0_gnn_Wve': _L0_gnn_in['Wve'], 'L0_gnn_gq': _L0_gnn_in['gq'], 'L0_gnn_bq': _L0_gnn_in['bq'], 'L0_gnn_gk': _L0_gnn_in['gk'], 'L0_gnn_bk': _L0_gnn_in['bk'], 'L0_gnn_gv': _L0_gnn_in['gv'], 'L0_gnn_bv': _L0_gnn_in['bv'], 'L0_gnn_gke': _L0_gnn_in['gke'], 'L0_gnn_bke': _L0_gnn_in['bke'], 'L0_gnn_gve': _L0_gnn_in['gve'], 'L0_gnn_bve': _L0_gnn_in['bve'], 'L0_gnn_relk_W': _L0_gnn_in['relk_W'], 'L0_gnn_relk_b': _L0_gnn_in['relk_b'], 'L0_gnn_relk_g': _L0_gnn_in['relk_g'], 'L0_gnn_relk_beta': _L0_gnn_in['relk_beta'], 'L0_gnn_relv_W': _L0_gnn_in['relv_W'], 'L0_gnn_relv_b': _L0_gnn_in['relv_b'], 'L0_gnn_relv_g': _L0_gnn_in['relv_g'], 'L0_gnn_relv_beta': _L0_gnn_in['relv_beta'], 'L0_gnn_z_W': _L0_gnn_in['z_W'], 'L0_gnn_z_b': _L0_gnn_in['z_b'], 'L0_gnn_z_g': _L0_gnn_in['z_g'], 'L0_gnn_z_beta': _L0_gnn_in['z_beta']}

def reference(x, src, dst, edge_attr_128, L0_gnn_Wq, L0_gnn_Wk, L0_gnn_Wv, L0_gnn_Wke, L0_gnn_Wve, L0_gnn_gq, L0_gnn_bq, L0_gnn_gk, L0_gnn_bk, L0_gnn_gv, L0_gnn_bv, L0_gnn_gke, L0_gnn_bke, L0_gnn_gve, L0_gnn_bve, L0_gnn_relk_W, L0_gnn_relk_b, L0_gnn_relk_g, L0_gnn_relk_beta, L0_gnn_relv_W, L0_gnn_relv_b, L0_gnn_relv_g, L0_gnn_relv_beta, L0_gnn_z_W, L0_gnn_z_b, L0_gnn_z_g, L0_gnn_z_beta):
    import jax
    import jax.numpy as jnp

    def _L0_gnn_ref(x_node, x_edge, Wq, Wk, Wv, Wke, Wve, gq, bq, gk, bk, gv, bv, gke, bke, gve, bve, relk_W, relk_b, relk_g, relk_beta, relv_W, relv_b, relv_g, relv_beta, z_W, z_b, z_g, z_beta, src, dst):
        import jax, jax.numpy as jnp
        import numpy as np
        EPS = 1e-05

        def layer_norm(x, g, b):
            m = x.mean(-1, keepdims=True)
            v = ((x - m) ** 2).mean(-1, keepdims=True)
            return (x - m) * jax.lax.rsqrt(v + EPS) * g + b
        N = x_node.shape[0]
        q = layer_norm(jnp.einsum('nf,hfd->hnd', x_node, Wq), gq[:, None, :], bq[:, None, :])
        k = layer_norm(jnp.einsum('nf,hfd->hnd', x_node, Wk), gk[:, None, :], bk[:, None, :])
        v = layer_norm(jnp.einsum('nf,hfd->hnd', x_node, Wv), gv[:, None, :], bv[:, None, :])
        ke = layer_norm(jnp.einsum('ef,hfd->hed', x_edge, Wke), gke[:, None, :], bke[:, None, :])
        ve = layer_norm(jnp.einsum('ef,hfd->hed', x_edge, Wve), gve[:, None, :], bve[:, None, :])
        rel_k = layer_norm(jnp.concatenate([ke, k[:, src]], -1) @ relk_W + relk_b, relk_g, relk_beta)
        qk = jnp.sum(q[:, dst] * rel_k, -1) / 4.0
        qkT = qk.T
        m = jax.ops.segment_max(qkT, dst, num_segments=N)
        se = jax.ops.segment_sum(jnp.exp(qkT - m[dst]), dst, num_segments=N)
        lse = jnp.log(se) + m
        rel_v = layer_norm(jnp.concatenate([ve, v[:, src]], -1) @ relv_W + relv_b, relv_g, relv_beta)
        logw = qk - lse.T[:, dst]
        h = jnp.transpose(logw[..., None] * rel_v, (1, 0, 2))
        agg = jax.ops.segment_sum(h, dst, num_segments=N)
        z = jax.nn.relu(agg @ z_W + z_b)
        z = layer_norm(z, z_g, z_beta)
        return z.reshape(N, -1)
    x = _layernorm(x + _L0_gnn_ref(x, edge_attr_128, L0_gnn_Wq, L0_gnn_Wk, L0_gnn_Wv, L0_gnn_Wke, L0_gnn_Wve, L0_gnn_gq, L0_gnn_bq, L0_gnn_gk, L0_gnn_bk, L0_gnn_gv, L0_gnn_bv, L0_gnn_gke, L0_gnn_bke, L0_gnn_gve, L0_gnn_bve, L0_gnn_relk_W, L0_gnn_relk_b, L0_gnn_relk_g, L0_gnn_relk_beta, L0_gnn_relv_W, L0_gnn_relv_b, L0_gnn_relv_g, L0_gnn_relv_beta, L0_gnn_z_W, L0_gnn_z_b, L0_gnn_z_g, L0_gnn_z_beta, src, dst), axis=-1)
    return x

_drawn_inputs = setup_inputs


def setup_inputs(seed=0):
    import zlib

    import numpy as np

    out = dict(_drawn_inputs(seed))
    spreads = {'L0_gnn_gq': (1.0, 0.569),
     'L0_gnn_bq': (0.0, 0.436),
     'L0_gnn_gk': (1.0, 0.6),
     'L0_gnn_bk': (0.0, 0.8),
     'L0_gnn_gv': (1.0, 0.2),
     'L0_gnn_bv': (0.0, 0.1),
     'L0_gnn_gke': (1.0, 0.6),
     'L0_gnn_bke': (0.0, 0.8),
     'L0_gnn_gve': (1.0, 0.2),
     'L0_gnn_bve': (0.0, 0.1),
     'L0_gnn_relk_b': (0.0, 0.8),
     'L0_gnn_relk_g': (1.0, 0.2),
     'L0_gnn_relk_beta': (0.0, 2.0),
     'L0_gnn_relv_b': (0.0, 0.1),
     'L0_gnn_relv_g': (1.0, 0.2),
     'L0_gnn_relv_beta': (0.0, 0.1),
     'L0_gnn_z_b': (0.0, 0.8),
     'L0_gnn_z_g': (1.0, 0.2),
     'L0_gnn_z_beta': (0.0, 0.1)}
    factors = {}
    for name, (base, spread) in spreads.items():
        noise = np.random.default_rng([zlib.crc32(name.encode()), seed]).standard_normal(out[name].shape)
        drawn = base * np.exp(spread * noise) if base else spread * noise
        out[name] = jnp.asarray(drawn.astype(out[name].dtype))
    for name, factor in factors.items():
        out[name] = (out[name] * factor).astype(out[name].dtype)
    return out
```

```python
import numpy as np
import concourse.bass as bass
from concourse import mybir
from contextlib import ExitStack

P = 128
N, E, F, H, D = 6250, 200000, 128, 8, 16
TILES = 4
GE = TILES * P
GROUPS = -(-E // GE)
TAIL0 = E - GE
DUP = GROUPS * GE - E
BLOCKS = -(-N // P)
LAST = N - (BLOCKS - 1) * P
STEPS = GROUPS + BLOCKS - 1
EPS = 1e-5
QW = F + H
AW = 2 * F + H + 1
CHUNKS = P // H
CT = -(-(-(-E // P)) // CHUNKS)
CE = CT * P
BIG = 1.0e30
UNROLL = 6
LAG = 2
R_EA, R_SM, R_META, R_P, R_RUN = 3, 3, 6, 3, 3
STORE_LAG = 6


def edge_attention(nc, a, out):
    f32, bf16, i32, u32 = mybir.dt.float32, mybir.dt.bfloat16, mybir.dt.int32, mybir.dt.uint32
    ALU, ACT, AX = mybir.AluOpType, mybir.ActivationFunctionType, mybir.AxisListType
    ctx = ExitStack()
    with ctx:
        def sb(name, shape, dt=f32):
            return ctx.enter_context(nc.sbuf_tensor(name, shape, dt))

        def sem(name):
            return ctx.enter_context(nc.semaphore(name))

        table = nc.dram_tensor("node_table", [N, 2 * F], f32, kind="Internal").ap()
        sums_d = nc.dram_tensor("node_sums", [BLOCKS, P, AW], f32, kind="Internal").ap()
        qk_d = nc.dram_tensor("edge_qk", [GROUPS, TILES * H, P], f32, kind="Internal").ap()
        lse_d = nc.dram_tensor("edge_lse", [CE, P], f32, kind="Internal").ap()

        banks = ctx.enter_context(nc.psum_tensor("banks", [P, 8, 512], f32))
        bank = [banks[:, i, :] for i in range(8)]

        ident = sb("ident", [P, P])
        iota_p = sb("iota_p", [P, 1])
        z_w = sb("z_w", [P, F])
        z_beta_w = sb("z_beta_w", [P, F])
        rows16 = sb("rows16", [P, 9, D])
        eps_c = sb("eps_c", [P, 1])
        one_c = sb("one_c", [P, 1])

        mid = ctx.enter_context(ExitStack())

        def sb_mid(name, shape, dt=f32):
            return mid.enter_context(nc.sbuf_tensor(name, shape, dt))

        iota_n = sb_mid("iota_n", [P, P])
        w_node = sb_mid("w_node", [P, 5 * F])
        w_edge = sb_mid("w_edge", [P, 4 * F])
        table_bias = sb_mid("table_bias", [P, 2, F])
        gq4 = sb_mid("gq4", [P, F])
        bq4 = sb_mid("bq4", [P, F])
        gqb = sb_mid("gqb", [P, F])
        bqb = sb_mid("bqb", [P, H])
        cols = sb_mid("cols", [P, GROUPS, 2 * TILES])
        step_cols = sb_mid("step_cols", [P, STEPS, 4])
        step_ints = sb_mid("step_ints", [1, 3, STEPS], i32)
        RELKG, RELKB, RELKBIAS, RELVBIAS, ZB, ZG, ZBETA = range(7)

        with ExitStack() as scope:
            def sbp(name, shape, dt=f32):
                return scope.enter_context(nc.sbuf_tensor(name, shape, dt))

            w_all = sbp("w_all", [P, 5, F])
            w_mean = sbp("w_mean", [P, 5 * H])
            w_c = sbp("w_c", [P, 5, F])
            w_ct = sbp("w_ct", [P, 4, F])
            rel4 = sbp("rel4", [P, 4, D])
            rel_mean = sbp("rel_mean", [P, 4])
            rel_c = sbp("rel_c", [P, 4, D])
            z4 = sbp("z4", [P, D])
            mask = sbp("mask", [P, F])
            bd = sbp("bd", [P, 4, F])
            bdg = sbp("bdg", [P, 4, F])
            zbd = sbp("zbd", [P, F])
            col = sbp("col", [P, 10])
            colb = sbp("colb", [P, 5, F])
            qrows = sbp("qrows", [P, 2, F])
            rb_mean = sbp("rb_mean", [P, 2])
            rb_c = sbp("rb_c", [P, 2, D])
            tmp_q = sbp("tmp_q", [P, F])
            src_i = sbp("src_i", [P, 13, P], i32)
            dst_i = sbp("dst_i", [P, 13, P], i32)
            src_f = sbp("src_f", [P, 13, P])
            dst_f = sbp("dst_f", [P, 13, P])
            iota_i = sbp("iota_i", [P, STEPS], i32)
            iota_s = sbp("iota_s", [P, STEPS])
            iota_pi = sbp("iota_pi", [P, 1], i32)
            last_i = sbp("last_i", [1, GROUPS - 1], i32)
            last_f = sbp("last_f", [1, GROUPS - 1])
            below = sbp("below", [P, GROUPS - 1])
            thr = sbp("thr", [P, 1])
            g_of = sbp("g_of", [P, 1])
            s_of = sbp("s_of", [P, 1])
            passed = sbp("passed", [P, STEPS])
            blk = sbp("blk", [P, STEPS + 1])
            grp = sbp("grp", [P, STEPS + 1])
            off_f = sbp("off_f", [1, STEPS])
            ones = sbp("ones", [P, P])
            s_load, s_const, s_chain, s_idx = sem("pro_loads"), sem("pro_consts"), sem("pro_chain"), sem("pro_index_loads")
            s_tp, s_tc, s_u, s_wb, s_step, s_stepv = (sem("pro_wT"), sem("pro_wT_copied"), sem("pro_products"),
                                                      sem("pro_mats"), sem("pro_bcast"), sem("pro_step_in"))
            s_it, s_ic_s, s_ic_d = sem("pro_idx_transposed"), sem("pro_src_copied"), sem("pro_dst_copied")
            s_conv = sem("pro_idx_floats")
            FULL = (GROUPS - 1) * TILES
            KB, KR = FULL // P, FULL % P

            loads, idx_loads = [], []

            with nc.allow_non_contiguous_dma(reason="small weight and index layouts"), nc.Block() as block:
                @block.sync
                def _(sp):
                    n = [0, 0]

                    def load(dst, src_ap, which=0):
                        sp.dma_start(dst, src_ap).then_inc((s_load, s_idx)[which], 16)
                        n[which] += 1

                    for i, name in enumerate(("Wq", "Wk", "Wv", "Wke", "Wve")):
                        load(w_all[:, i, :].rearrange("f (h d) -> f h d", h=H), a[name].rearrange("h f d -> f h d"))
                    for h in range(H):
                        rows = slice(D * h, D * h + D)
                        load(rel4[rows, 0:2, :], a["relk_W"].rearrange("(t d) e -> d t e", t=2))
                        load(rel4[rows, 2:4, :], a["relv_W"].rearrange("(t d) e -> d t e", t=2))
                        load(z4[rows, :], a["z_W"])
                        load(col[rows, 8:9], a["relv_g"].rearrange("(d o) -> d o", o=1))
                        load(col[rows, 9:10], a["relv_beta"].rearrange("(d o) -> d o", o=1))
                    for i, name in enumerate(("gke", "gk", "gve", "gv", "bke", "bk", "bve", "bv")):
                        load(col[:, i:i + 1], a[name].rearrange("h (d o) -> (h d) o", o=1))
                    for i, name in enumerate(("gq", "bq")):
                        load(qrows[:, i, :], a[name].rearrange("h d -> (h d)").partition_broadcast(P))
                    for i, name in enumerate(("relk_g", "relk_beta", "relk_b", "relv_b", "z_b", "z_g", "z_beta")):
                        load(rows16[:, i, :], a[name].partition_broadcast(P))
                    for i, (dst_t, name) in enumerate(((src_i, "src"), (dst_i, "dst"))):
                        load(dst_t[:, 0:KB, :], a[name][0:KB * P * P].rearrange("(k t e) -> t k e", t=P, e=P), 1)
                        load(dst_t[0:KR, KB, :], a[name][KB * P * P:FULL * P].rearrange("(t e) -> t e", e=P), 1)
                        load(dst_t[KR:KR + TILES, KB, :], a[name][TAIL0:E].rearrange("(t e) -> t e", e=P), 1)
                    load(last_i[0:1, :], a["dst"][0:(GROUPS - 1) * GE].rearrange("(g e) -> g e", e=GE)[:, GE - 1:GE]
                         .rearrange("g o -> o g"), 1)
                    loads.append(n[0])
                    idx_loads.append(n[1])

                @block.gpsimd
                def _(pool):
                    nc.gpsimd.memset(ident[:], 0.0).then_inc(s_const, 1)
                    nc.gpsimd.memset(mask[:], 1.0).then_inc(s_const, 1)
                    nc.gpsimd.memset(ones[:], 1.0).then_inc(s_const, 1)
                    nc.gpsimd.memset(eps_c[:], EPS).then_inc(s_const, 1)
                    nc.gpsimd.memset(one_c[:], 1.0).then_inc(s_const, 1)
                    nc.gpsimd.iota(iota_i[:], pattern=[[1, STEPS]], base=0, channel_multiplier=0).then_inc(s_const, 1)
                    nc.gpsimd.iota(iota_pi[:], pattern=[[0, 1]], base=0, channel_multiplier=1).then_inc(s_const, 1)
                    pool.wait_ge(s_const, 7)
                    nc.gpsimd.affine_select(out=ident[:], in_=ident[:], compare_op=ALU.not_equal, fill=1.0, base=0,
                                            pattern=[[-1, P]], channel_multiplier=1).then_inc(s_const, 1)
                    m3 = mask[:].rearrange("p (h d) -> p h d", d=D)
                    nc.gpsimd.affine_select(out=m3, in_=m3, compare_op=ALU.is_ge, fill=0.0, base=0,
                                            pattern=[[-D, H], [0, D]], channel_multiplier=1).then_inc(s_const, 1)
                    pool.wait_ge(s_const, 9)
                    nc.gpsimd.affine_select(out=m3, in_=m3, compare_op=ALU.is_ge, fill=0.0, base=D - 1,
                                            pattern=[[D, H], [0, D]], channel_multiplier=-1).then_inc(s_const, 1)

                CONSTS = 10

                @block.vector
                def _(dve):
                    v = nc.vector
                    done = [0]

                    def link(ins):
                        done[0] += 1
                        ins.then_inc(s_chain, 1)
                        dve.wait_ge(s_chain, done[0])

                    dve.wait_ge(s_const, CONSTS)
                    dve.wait_ge(s_load, 16 * loads[0])
                    link(v.tensor_reduce(out=w_mean[:], in_=w_all[:].rearrange("p i (h d) -> p (i h) d", d=D), axis=AX.X, op=ALU.add))
                    link(v.tensor_scalar(out=w_mean[:], in0=w_mean[:], scalar1=1.0 / D, scalar2=None, op0=ALU.mult))
                    link(v.tensor_tensor(out=w_c[:].rearrange("p i (h d) -> p (i h) d", d=D),
                                         in0=w_all[:].rearrange("p i (h d) -> p (i h) d", d=D),
                                         in1=w_mean[:].unsqueeze(2).to_broadcast([P, 5 * H, D]), op=ALU.subtract))
                    link(v.tensor_reduce(out=rel_mean[:], in_=rel4[:], axis=AX.X, op=ALU.add))
                    link(v.tensor_scalar(out=rel_mean[:], in0=rel_mean[:], scalar1=1.0 / D, scalar2=None, op0=ALU.mult))
                    link(v.tensor_tensor(out=rel_c[:], in0=rel4[:], in1=rel_mean[:].unsqueeze(2).to_broadcast([P, 4, D]), op=ALU.subtract))
                    m3 = mask[:].rearrange("p (h d) -> p h d", d=D)
                    for i in range(4):
                        link(v.tensor_tensor(out=bd[:, i, :].rearrange("p (h d) -> p h d", d=D), in0=m3,
                                             in1=rel_c[:, i, :].unsqueeze(1).to_broadcast([P, H, D]), op=ALU.mult))
                        link(v.tensor_scalar(out=bdg[:, i, :], in0=bd[:, i, :], scalar1=col[:, i:i + 1], scalar2=None, op0=ALU.mult))
                        link(v.tensor_copy(out=colb[:, i, :], in_=col[:, 4 + i:5 + i].to_broadcast([P, F])))
                    link(v.tensor_tensor(out=zbd[:].rearrange("p (h d) -> p h d", d=D), in0=m3,
                                         in1=z4[:].unsqueeze(1).to_broadcast([P, H, D]), op=ALU.mult))
                    link(v.tensor_scalar(out=z_w[:], in0=zbd[:], scalar1=col[:, 8:9], scalar2=None, op0=ALU.mult))
                    link(v.tensor_copy(out=colb[:, 4, :], in_=col[:, 9:10].to_broadcast([P, F])))
                    v.tensor_copy(out=w_node[:, 0:3 * F], in_=w_c[:, 0:3, :].rearrange("p i n -> p (i n)")).then_inc(s_wb, 1)
                    v.tensor_copy(out=w_edge[:, 0:2 * F], in_=w_c[:, 3:5, :].rearrange("p i n -> p (i n)")).then_inc(s_wb, 1)
                    for dst_t, row, r16 in ((gq4, 0, RELKG), (bq4, 1, RELKG), (gqb, 0, RELKB), (tmp_q, 1, RELKB)):
                        link(v.tensor_tensor(out=dst_t[:].rearrange("p (h d) -> p h d", d=D),
                                             in0=qrows[:, row, :].rearrange("p (h d) -> p h d", d=D),
                                             in1=rows16[:, r16, :].unsqueeze(1).to_broadcast([P, H, D]), op=ALU.mult))
                        link(v.tensor_scalar(out=dst_t[:], in0=dst_t[:], scalar1=0.25, scalar2=None, op0=ALU.mult))
                    link(v.tensor_reduce(out=bqb[:], in_=tmp_q[:].rearrange("p (h d) -> p h d", d=D), axis=AX.X, op=ALU.add))
                    link(v.tensor_reduce(out=rb_mean[:], in_=rows16[:, RELKBIAS:RELVBIAS + 1, :], axis=AX.X, op=ALU.add))
                    link(v.tensor_scalar(out=rb_mean[:], in0=rb_mean[:], scalar1=1.0 / D, scalar2=None, op0=ALU.mult))
                    link(v.tensor_tensor(out=rb_c[:], in0=rows16[:, RELKBIAS:RELVBIAS + 1, :],
                                         in1=rb_mean[:].unsqueeze(2).to_broadcast([P, 2, D]), op=ALU.subtract))
                    dve.wait_ge(s_u, 2)
                    v.tensor_copy(out=w_node[:, 3 * F:5 * F], in_=bank[1][:, 0:2 * F]).then_inc(s_wb, 1)
                    v.tensor_copy(out=w_edge[:, 2 * F:4 * F], in_=bank[1][:, 2 * F:4 * F]).then_inc(s_wb, 1)
                    for i in range(2):
                        v.tensor_tensor(out=table_bias[:, i, :].rearrange("p (h d) -> p h d", d=D),
                                        in0=bank[2][:, i * F:(i + 1) * F].rearrange("p (h d) -> p h d", d=D),
                                        in1=rb_c[:, i, :].unsqueeze(1).to_broadcast([P, H, D]), op=ALU.add).then_inc(s_wb, 1)
                    v.tensor_copy(out=z_beta_w[:], in_=bank[2][:, 2 * F:3 * F]).then_inc(s_wb, 1)

                    dve.wait_ge(s_idx, 16 * idx_loads[0])
                    for rows_f, rows_i in ((src_f, src_i), (dst_f, dst_i)):
                        v.tensor_copy(out=rows_f[:, 0:KB, :], in_=rows_i[:, 0:KB, :]).then_inc(s_conv, 1)
                        v.tensor_copy(out=rows_f[0:KR + TILES, KB, :], in_=rows_i[0:KR + TILES, KB, :]).then_inc(s_conv, 1)
                    v.tensor_copy(out=last_f[:], in_=last_i[:]).then_inc(s_stepv, 1)
                    v.tensor_copy(out=iota_s[:], in_=iota_i[:]).then_inc(s_wb, 1)
                    v.tensor_copy(out=iota_n[:], in_=iota_i[:, 0:P]).then_inc(s_wb, 1)
                    link(v.tensor_copy(out=iota_p[:], in_=iota_pi[:]))
                    link(v.tensor_scalar(out=thr[:], in0=iota_p[:], scalar1=1.0, scalar2=float(P), op0=ALU.add, op1=ALU.mult))
                    dve.wait_ge(s_step, 1)
                    link(v.tensor_scalar(out=below[:], in0=bank[3][:, 0:GROUPS - 1], scalar1=thr[:, 0:1], scalar2=None, op0=ALU.is_lt))
                    link(v.tensor_reduce(out=g_of[:], in_=below[:], axis=AX.X, op=ALU.add))
                    link(v.tensor_scalar(out=s_of[:], in0=g_of[:], scalar1=iota_p[:, 0:1], scalar2=1.0, op0=ALU.add, op1=ALU.add))
                    v.tensor_scalar(out=passed[:], in0=iota_s[:], scalar1=s_of[:, 0:1], scalar2=None, op0=ALU.is_ge).then_inc(s_stepv, 1)
                    link(v.memset(blk[:, 0:1], -1.0))
                    link(v.memset(grp[:, 0:1], -1.0))
                    dve.wait_ge(s_step, 2)
                    link(v.tensor_copy(out=blk[:, 1:STEPS + 1], in_=bank[4][:, 0:STEPS]))
                    link(v.tensor_tensor(out=grp[:, 1:STEPS + 1], in0=iota_s[:], in1=blk[:, 1:STEPS + 1], op=ALU.subtract))
                    link(v.tensor_scalar(out=step_cols[:, :, 0], in0=blk[:, 1:STEPS + 1], scalar1=float(P), scalar2=None, op0=ALU.mult))
                    link(v.tensor_scalar(out=step_cols[:, :, 1], in0=step_cols[:, :, 0], scalar1=iota_p[:, 0:1], scalar2=-1.0,
                                         op0=ALU.add, op1=ALU.mult))
                    link(v.tensor_tensor(out=step_cols[:, :, 2], in0=blk[:, 1:STEPS + 1], in1=blk[:, 0:STEPS], op=ALU.is_equal))
                    link(v.tensor_tensor(out=step_cols[:, :, 3], in0=grp[:, 1:STEPS + 1], in1=grp[:, 0:STEPS], op=ALU.is_equal))
                    link(v.tensor_copy(out=step_ints[0:1, 0, :], in_=blk[0:1, 1:STEPS + 1]))
                    link(v.tensor_copy(out=step_ints[0:1, 1, :], in_=grp[0:1, 1:STEPS + 1]))
                    link(v.tensor_scalar(out=off_f[:], in0=grp[0:1, 1:STEPS + 1], scalar1=float(GE), scalar2=float(TAIL0),
                                         op0=ALU.mult, op1=ALU.min))
                    link(v.tensor_copy(out=step_ints[0:1, 2, :], in_=off_f[:]))

                    for k in range(KB + 1):
                        n = P if k < KB else KR + TILES
                        dve.wait_ge(s_it, k + 1)
                        v.tensor_copy(out=cols[:].bitcast(i32)[:, k * 32:k * 32 + n // TILES, 0:TILES],
                                      in_=bank[5 + k % 2][:, 0:n].rearrange("p (g j) -> p g j", j=TILES)).then_inc(s_ic_s, 1)
                    dve.wait_ge(s_ic_d, KB + 1)
                    for j in range(DUP // P):
                        link(v.memset(cols[:, GROUPS - 1, TILES + j:TILES + j + 1], 1.0e6))
                    link(v.memset(cols[0:DUP % P, GROUPS - 1, TILES + DUP // P:TILES + DUP // P + 1], 1.0e6))

                @block.scalar
                def _(act):
                    nc.scalar.preload_act_table_set("natural_log_exp_and_others")
                    act.wait_ge(s_tp, 1)
                    nc.scalar.activation(w_ct[:].rearrange("p i n -> p (i n)"), bank[0][:], ACT.Copy).then_inc(s_tc, 1)
                    for k in range(KB + 1):
                        n = P if k < KB else KR + TILES
                        act.wait_ge(s_it, k + 1)
                        nc.scalar.activation(cols[:, k * 32:k * 32 + n // TILES, TILES:2 * TILES],
                                             bank[7 * (k % 2)][:, 0:n].rearrange("p (g j) -> p g j", j=TILES),
                                             ACT.Copy, scale=-1.0).then_inc(s_ic_d, 1)

                @block.tensor
                def _(pe):
                    pe.wait_ge(s_const, CONSTS)
                    pe.wait_ge(s_chain, 3)
                    for i in range(4):
                        last = nc.tensor.transpose(bank[0][:, i * F:(i + 1) * F], w_c[:, 1 + i, :], ident[:])
                    last.then_inc(s_tp, 1)
                    pe.wait_ge(s_tc, 1)
                    pe.wait_ge(s_chain, 3 + 3 + 12 + 3)
                    for i, m in enumerate((1, 3, 0, 2)):
                        last = nc.tensor.matmul(bank[1][:, i * F:(i + 1) * F], w_ct[:, i, :], bdg[:, m, :], start=True, stop=True)
                    last.then_inc(s_u, 1)
                    for i in range(2):
                        nc.tensor.matmul(bank[2][:, i * F:(i + 1) * F], colb[:, 2 * i, :], bd[:, 2 * i, :], start=True, stop=False)
                        nc.tensor.matmul(bank[2][:, i * F:(i + 1) * F], colb[:, 2 * i + 1, :], bd[:, 2 * i + 1, :], start=False, stop=True)
                    nc.tensor.matmul(bank[2][:, 2 * F:3 * F], colb[:, 4, :], zbd[:], start=True, stop=True).then_inc(s_u, 1)
                    pe.wait_ge(s_stepv, 1)
                    nc.tensor.matmul(bank[3][:, 0:GROUPS - 1], ones[0:1, :], last_f[:], start=True, stop=True).then_inc(s_step, 1)
                    pe.wait_ge(s_stepv, 2)
                    nc.tensor.matmul(bank[4][:, 0:STEPS], ones[0:BLOCKS - 1, :], passed[0:BLOCKS - 1, :], start=True, stop=True).then_inc(s_step, 1)
                    pe.wait_ge(s_conv, 4)
                    for k in range(KB + 1):
                        n = P if k < KB else KR + TILES
                        if k >= 2:
                            pe.wait_ge(s_ic_s, k - 1)
                            pe.wait_ge(s_ic_d, k - 1)
                        nc.tensor.transpose(bank[5 + k % 2][:, 0:n], src_f[0:n, k, :], ident[0:n, 0:n])
                        nc.tensor.transpose(bank[7 * (k % 2)][:, 0:n], dst_f[0:n, k, :], ident[0:n, 0:n]).then_inc(s_it, 1)

        q_split = sb_mid("q_split", [P, BLOCKS, 3 * QW], bf16)
        nodes(nc, a, sem, bank, dict(table=table, ident=ident, w_node=w_node, table_bias=table_bias, gq4=gq4, bq4=bq4,
                                     gqb=gqb, bqb=bqb, eps_c=eps_c, q_split=q_split))
        edges(nc, a, sem, banks, dict(table=table, sums_d=sums_d, qk_d=qk_d, ident=ident, iota_n=iota_n, w_edge=w_edge,
                                      cols=cols, step_cols=step_cols, step_ints=step_ints, eps_c=eps_c, q_split=q_split))
        mid.close()
        softmax(nc, a, sem, bank, dict(qk_d=qk_d, lse_d=lse_d, ident=ident, one_c=one_c))
        finish(nc, a, sem, bank, dict(sums_d=sums_d, lse_d=lse_d, ident=ident, z_w=z_w, z_beta_w=z_beta_w,
                                      rows16=rows16, eps_c=eps_c), out)


def nodes(nc, a, sem, bank, t):
    f32, bf16 = mybir.dt.float32, mybir.dt.bfloat16
    ALU, ACT, AX = mybir.AluOpType, mybir.ActivationFunctionType, mybir.AxisListType
    with ExitStack() as scope:
        def sb(name, shape, dt=f32):
            return scope.enter_context(nc.sbuf_tensor(name, shape, dt))

        xb = sb("n_x", [P, 2, 2, F])
        xt = sb("n_xt", [P, 2, F])
        sq = sb("n_sq", [P, 2, 3 * F])
        var = sb("n_var", [P, 2, 3 * H])
        lnv = sb("n_lnv", [P, 2, 3 * H])
        rstd = sb("n_rstd", [P, 2, 3 * H])
        tb = sb("n_tb", [P, 2, 2, 2, F])
        yh = sb("n_yh", [P, 2, F])
        q = sb("n_q", [P, 2, QW])
        qt = sb("n_qt", [P, 2, F])
        q1 = sb("n_q1", [P, 2, QW])
        q2 = sb("n_q2", [P, 2, QW])
        s_x = [sem(f"nodes_x{i}") for i in range(2)]
        s_st = [sem(f"nodes_stored{i}") for i in range(2)]
        s_xt, s_xc, s_pr, s_sq, s_var, s_ln, s_r = (sem("nodes_xT"), sem("nodes_xT_copied"), sem("nodes_projected"),
                                                    sem("nodes_squared"), sem("nodes_var"), sem("nodes_ln"), sem("nodes_rstd"))
        s_u, s_tb, s_yh, s_qg0, s_qg, s_t, s_qb0, s_q = (sem("nodes_scaled"), sem("nodes_table"), sem("nodes_yh"), sem("nodes_qg0"),
                                                         sem("nodes_qg"), sem("nodes_qt"), sem("nodes_qb0"), sem("nodes_q"))
        s_1, s_r1, s_2, s_r2, s_3, s_z = (sem("nodes_part1"), sem("nodes_rest1"), sem("nodes_part2"), sem("nodes_rest2"),
                                          sem("nodes_part3"), sem("nodes_zeroed"))
        q_split, table = t["q_split"], t["table"]
        PAIRS = BLOCKS // 2
        ITER = PAIRS // 2

        assert PAIRS % 2 == 0 and BLOCKS % 2 == 1

        with nc.Block() as block:
            @block.sync
            def _(sp):
                def load(k, slot, b, nb, rows):
                    sp.dma_start(xb[0:rows, slot, 0:nb, :],
                                 a["x"][bass.ds(P * b, nb * rows), :].rearrange("(b p) f -> p b f", p=rows)).then_inc(s_x[slot], 16)

                def body(k, i, slot, b, nb, rows):
                    n = k + 2 * i
                    sp.wait_ge(s_xt, n + 1)
                    sp.wait_ge(s_tb, n + 1)
                    sp.dma_start(table[bass.ds(P * b, nb * rows), :].rearrange("(b p) f -> p b f", p=rows),
                                 tb[0:rows, slot, 0:nb, :, :].rearrange("p b t f -> p b (t f)")).then_inc(s_st[slot], 16)

                load(0, 0, 0, 2, P)
                load(1, 1, 2, 2, P)
                with sp.Fori(0, ITER - 1) as i:
                    for u in range(2):
                        body(u, i, u, 4 * i + 2 * u, 2, P)
                        load(0, u, 4 * i + 2 * u + 4, 2, P)
                for u in range(2):
                    body(2 * (ITER - 1) + u, 0, u, 4 * (ITER - 1) + 2 * u, 2, P)
                    if u == 0:
                        load(0, 0, BLOCKS - 1, 1, LAST)
                body(PAIRS, 0, 0, BLOCKS - 1, 1, LAST)
                sp.wait_ge(s_st[0], 16 * (PAIRS // 2 + 1))
                sp.wait_ge(s_st[1], 16 * (PAIRS // 2))

            @block.tensor
            def _(pe):
                def body(k, i, slot, b, nb, rows):
                    n = k + 2 * i
                    tail = k == PAIRS
                    pe.wait_ge(s_x[slot], 16 * (i + 1) if not tail else 16 * (PAIRS // 2 + 1))
                    pe.wait_ge(s_xc, n)
                    for c in range(nb):
                        last = nc.tensor.transpose(bank[6][:, c * F:c * F + rows], xb[0:rows, slot, c, :], t["ident"][0:rows, 0:rows])
                    last.then_inc(s_xt, 1)
                    pe.wait_ge(s_xc, n + 1)
                    pe.wait_ge(s_u, n)
                    pe.wait_ge(s_yh, n)
                    for c in range(nb):
                        nc.tensor.matmul(bank[c][0:rows, :], xt[:, c, 0:rows], t["w_node"][:, 0:4 * F], start=True, stop=True)
                        last = nc.tensor.matmul(bank[2][0:rows, c * F:(c + 1) * F], xt[:, c, 0:rows], t["w_node"][:, 4 * F:5 * F],
                                                start=True, stop=True)
                    last.then_inc(s_pr, 1)
                each_first(pe, body, ITER, PAIRS)

            @block.scalar
            def _(act):
                def body(k, i, slot, b, nb, rows):
                    n = k + 2 * i
                    act.wait_ge(s_xt, n + 1)
                    act.wait_ge(s_pr, n)
                    nc.scalar.activation(xt[:, 0:nb, 0:rows], bank[6][:, 0:nb * F].rearrange("p (c n) -> p c n", c=nb)[:, :, 0:rows],
                                         ACT.Copy).then_inc(s_xc, 1)
                    act.wait_ge(s_pr, n + 1)
                    for c in range(nb):
                        last = nc.scalar.activation(sq[0:rows, c, :], bank[c][0:rows, 0:3 * F], ACT.Square)
                    last.then_inc(s_sq, 1)
                    act.wait_ge(s_var, n + 1)
                    nc.scalar.activation(lnv[0:rows, 0:nb, :], var[0:rows, 0:nb, :], ACT.Ln, bias=t["eps_c"][0:rows, 0:1], scale=1.0 / D).then_inc(s_ln, 1)
                    act.wait_ge(s_ln, n + 1)
                    nc.scalar.activation(rstd[0:rows, 0:nb, :], lnv[0:rows, 0:nb, :], ACT.Exp, scale=-0.5).then_inc(s_r, 1)
                    qs = q_split[0:rows, bass.ds(b, nb), :]
                    act.wait_ge(s_z, 1)
                    act.wait_ge(s_qg, n + 1)
                    act.wait_ge(s_q, n + 1)
                    nc.scalar.activation(qs[:, :, 0:QW], q[0:rows, 0:nb, :], ACT.Copy).then_inc(s_1, 1)
                    act.wait_ge(s_r1, n + 1)
                    nc.scalar.activation(qs[:, :, QW:2 * QW], q1[0:rows, 0:nb, :], ACT.Copy).then_inc(s_2, 1)
                    act.wait_ge(s_r2, n + 1)
                    nc.scalar.activation(qs[:, :, 2 * QW:3 * QW], q2[0:rows, 0:nb, :], ACT.Copy).then_inc(s_3, 1)
                each_first(act, body, ITER, PAIRS)

            @block.gpsimd
            def _(pool):
                def body(k, i, slot, b, nb, rows):
                    n = k + 2 * i
                    pool.wait_ge(s_u, n + 1)
                    nc.gpsimd.tensor_tensor(out=tb[0:rows, slot, 0:nb, :, :], in0=tb[0:rows, slot, 0:nb, :, :],
                                            in1=t["table_bias"][0:rows].unsqueeze(1).to_broadcast([rows, nb, 2, F]), op=ALU.add).then_inc(s_tb, 1)
                each_first(pool, body, ITER, PAIRS)

            @block.vector
            def _(dve):
                v = nc.vector
                v.memset(q_split[:, BLOCKS - 1, :], 0.0).then_inc(s_z, 1)

                def body(k, i, slot, b, nb, rows):
                    n = k + 2 * i
                    tail = k == PAIRS
                    h3 = lambda ap: ap.rearrange("p (h d) -> p h d", d=D)
                    dve.wait_ge(s_sq, n + 1)
                    v.tensor_reduce(out=var[0:rows, 0:nb, :], in_=sq[0:rows, 0:nb, :].rearrange("p b (h d) -> p b h d", d=D),
                                    axis=AX.X, op=ALU.add).then_inc(s_var, 1)
                    dve.wait_ge(s_r, n + 1)
                    if tail:
                        dve.wait_ge(s_st[slot], 16 * (PAIRS // 2))
                    else:
                        dve.wait_ge(s_st[slot], 16 * i)
                    for c in range(nb):
                        v.tensor_tensor(out=h3(tb[0:rows, slot, c, 0, :]), in0=h3(bank[c][0:rows, 3 * F:4 * F]),
                                        in1=rstd[0:rows, c, H:2 * H].unsqueeze(2).to_broadcast([rows, H, D]), op=ALU.mult)
                        last = v.tensor_tensor(out=h3(tb[0:rows, slot, c, 1, :]), in0=h3(bank[2][0:rows, c * F:(c + 1) * F]),
                                               in1=rstd[0:rows, c, 2 * H:3 * H].unsqueeze(2).to_broadcast([rows, H, D]), op=ALU.mult)
                    last.then_inc(s_u, 1)
                    for c in range(nb):
                        last = v.tensor_tensor(out=h3(yh[0:rows, c, :]), in0=h3(bank[c][0:rows, 0:F]),
                                               in1=rstd[0:rows, c, 0:H].unsqueeze(2).to_broadcast([rows, H, D]), op=ALU.mult)
                    last.then_inc(s_yh, 1)
                    dve.wait_ge(s_yh, n + 1)
                    rep = lambda tt: tt[0:rows, :].unsqueeze(1).to_broadcast([rows, nb, F])
                    v.tensor_tensor(out=qt[0:rows, 0:nb, :], in0=yh[0:rows, 0:nb, :], in1=rep(t["gqb"]), op=ALU.mult).then_inc(s_t, 1)
                    dve.wait_ge(s_3, n)
                    v.tensor_tensor(out=q[0:rows, 0:nb, 0:F], in0=yh[0:rows, 0:nb, :], in1=rep(t["gq4"]), op=ALU.mult).then_inc(s_qg0, 1)
                    dve.wait_ge(s_t, n + 1)
                    v.tensor_reduce(out=q[0:rows, 0:nb, F:QW], in_=qt[0:rows, 0:nb, :].rearrange("p b (h d) -> p b h d", d=D),
                                    axis=AX.X, op=ALU.add).then_inc(s_qb0, 1)
                    dve.wait_ge(s_qg0, n + 1)
                    v.tensor_tensor(out=q[0:rows, 0:nb, 0:F], in0=q[0:rows, 0:nb, 0:F], in1=rep(t["bq4"]), op=ALU.add).then_inc(s_qg, 1)
                    dve.wait_ge(s_qb0, n + 1)
                    v.tensor_tensor(out=q[0:rows, 0:nb, F:QW], in0=q[0:rows, 0:nb, F:QW],
                                    in1=t["bqb"][0:rows, :].unsqueeze(1).to_broadcast([rows, nb, H]), op=ALU.add).then_inc(s_q, 1)
                    dve.wait_ge(s_q, n + 1)
                    dve.wait_ge(s_qg, n + 1)
                    qs = q_split[0:rows, bass.ds(b, nb), :]
                    dve.wait_ge(s_1, n + 1)
                    v.tensor_tensor(out=q1[0:rows, 0:nb, :], in0=q[0:rows, 0:nb, :], in1=qs[:, :, 0:QW], op=ALU.subtract).then_inc(s_r1, 1)
                    dve.wait_ge(s_r1, n + 1)
                    dve.wait_ge(s_2, n + 1)
                    v.tensor_tensor(out=q2[0:rows, 0:nb, :], in0=q1[0:rows, 0:nb, :], in1=qs[:, :, QW:2 * QW], op=ALU.subtract).then_inc(s_r2, 1)
                each_first(dve, body, ITER, PAIRS)


def each_first(eng, body, iters, pairs):
    for u in range(2):
        body(u, 0, u, 2 * u, 2, P)
    with eng.Fori(1, iters) as i:
        for u in range(2):
            body(u, i, u, 4 * i + 2 * u, 2, P)
    body(pairs, 0, pairs % 2, BLOCKS - 1, 1, LAST)


def edges(nc, a, sem, banks, t):
    f32, bf16, i32, u32 = mybir.dt.float32, mybir.dt.bfloat16, mybir.dt.int32, mybir.dt.uint32
    ALU, ACT, AX = mybir.AluOpType, mybir.ActivationFunctionType, mybir.AxisListType
    table, sums_d, qk_d, ident = t["table"], t["sums_d"], t["qk_d"], t["ident"]
    with ExitStack() as scope:
        def sb(name, shape, dt=f32):
            return scope.enter_context(nc.sbuf_tensor(name, shape, dt))

        ea = sb("e_ea", [P, R_EA, TILES, F])
        dstb = sb("e_dstb", [P, R_SM, GE], i32)
        qb = sb("e_q", [P, R_SM, 3 * QW], bf16)
        gcol = sb("e_gcol", [P, R_META, 2 * TILES])
        scol = sb("e_scol", [P, R_META, 4])
        eat = sb("e_eat", [P, 2, GE])
        ysq = sb("e_ysq", [P, 2, 2, 2 * F])
        yvar = sb("e_yvar", [P, 2, 2, 2 * H])
        yln = sb("e_yln", [P, 2, 2, 2 * H])
        yr = sb("e_yr", [P, 2, 2, 2 * H])
        p = sb("e_p", [P, R_P, TILES, 2 * F])
        z = sb("e_z", [P, TILES, 3 * F])
        zs = sb("e_zs", [P, TILES, 3 * H])
        zln = sb("e_zln", [P, TILES, 2 * H])
        zr = sb("e_zr", [P, TILES, 2 * H])
        qk0 = sb("e_qk0", [P, TILES, H])
        w2 = sb("e_w2", [P, TILES, H])
        hh = sb("e_h", [P, 2, TILES, AW])
        oht_a = sb("e_oht_a", [P, GE])
        oht = sb("e_oht", [P, 2, GE], bf16)
        rel = sb("e_rel", [P, TILES])
        oh_a = sb("e_oh_a", [P, TILES, P])
        oh = sb("e_oh", [P, 2, TILES, P])
        run = sb("e_run", [P, R_RUN, AW])
        qkr = sb("e_qkr", [P, R_RUN, TILES * H])
        qkt = sb("e_qkt", [TILES * H, R_RUN, P])
        pair = [banks[:, 0:2, :], banks[:, 2:4, :]]
        eat_ps, qx_ps, agg_ps = banks[:, 4, :], banks[:, 5:7, 0:2 * QW], banks[:, 7, 0:AW]
        qkt_ps = banks[0:TILES * H, 7, AW:AW + P]
        qx4 = qx_ps.rearrange("p b (t c) -> p b t c", c=QW)
        tiles4 = lambda ap: ap.rearrange("p (b t) c -> p b t c", b=2)

        s_ea = [sem(f"ea_loaded{i}") for i in range(R_EA)]
        s_sm = [sem(f"dst_q_loaded{i}") for i in range(R_SM)]
        s_meta = [sem(f"cols_loaded{i}") for i in range(R_META)]
        s_ga = [sem(f"gathered{i}") for i in range(R_P)]
        s_sums_st, s_qk_st = sem("sums_stored"), sem("qk_stored")
        s_tr, s_eat = sem("ea_transposed"), sem("eat_copied")
        s_proj = [sem(f"projected{i}") for i in range(2)]
        s_ysq = [sem(f"y_squared{i}") for i in range(2)]
        s_yv = [sem(f"y_summed{i}") for i in range(2)]
        s_yl = [sem(f"y_ln{i}") for i in range(2)]
        s_yr = [sem(f"y_rstd{i}") for i in range(2)]
        s_p = [sem(f"p_scaled{i}") for i in range(2)]
        s_psq, s_pq, s_z, s_zl, s_zr = sem("p_squared"), sem("pq_ready"), sem("z_summed"), sem("z_ln"), sem("z_rstd")
        s_qk0, s_qk, s_w2, s_qkr = sem("qk_dot"), sem("qk_ready"), sem("w2_ready"), sem("qk_run_ready")
        s_h1, s_h2, s_agg, s_run = sem("h1_ready"), sem("h2_ready"), sem("summed_to_nodes"), sem("run_ready")
        s_qkt, s_qktc = sem("qk_transposed"), sem("qkt_copied")
        s_oha, s_oht, s_qx = sem("oht_abs"), sem("oht_ready"), sem("q_expanded")
        s_rel, s_ohb, s_oh, s_init = sem("rel_ready"), sem("oh_abs"), sem("oh_ready"), sem("edges_init")

        PEEL = UNROLL + 1


        def every(eng, body, first, last):
            for c in range(first):
                body(c, 0, False)
            turns = (STEPS - 1 - first) // UNROLL
            with eng.Fori(0, turns) as i:
                for u in range(UNROLL):
                    body(first + u, i, True)
            for c in range(first + UNROLL * turns, last):
                body(c, 0, False)

        def use(c, i, ring):
            return (UNROLL // ring) * i + (c // ring + 1)

        def is_step(c, loop):
            return loop or 0 <= c < STEPS

        with nc.Block() as block:
            @block.sync
            def _(sp):
                def body(c, i, loop):
                    s = UNROLL * i + c
                    if is_step(c, loop):
                        at = UNROLL * i + c
                        e0 = sp.value_load(t["step_ints"][0:1, 2, bass.ds(at, 1)], min_val=0, max_val=TAIL0)
                        b = sp.value_load(t["step_ints"][0:1, 0, bass.ds(at, 1)], min_val=0, max_val=BLOCKS - 1)
                        g = sp.value_load(t["step_ints"][0:1, 1, bass.ds(at, 1)], min_val=0, max_val=GROUPS - 1)
                        if loop or c >= R_EA:
                            sp.wait_ge(s_tr, s - R_EA + 1)
                        sp.dma_start(ea[:, c % R_EA, :, :],
                                     a["edge_attr_128"][bass.ds(e0, GE), :].rearrange("(j p) f -> p j f", p=P)).then_inc(s_ea[c % R_EA], 16)
                        if loop or c >= R_META:
                            sp.wait_ge(s_run, s - R_META + 1)
                            sp.wait_ge(s_oh, s - R_META + 1)
                        sp.dma_start(gcol[:, c % R_META, :], t["cols"][:, bass.ds(g, 1), :].rearrange("p o c -> p (o c)")).then_inc(s_meta[c % R_META], 16)
                        sp.dma_start(scol[:, c % R_META, :], t["step_cols"][:, bass.ds(at, 1), :].rearrange("p o c -> p (o c)")).then_inc(s_meta[c % R_META], 16)
                        if loop or c >= R_SM:
                            sp.wait_ge(s_qx, s - R_SM + 1)
                        sp.dma_start(qb[:, c % R_SM, :], t["q_split"][:, bass.ds(b, 1), :].rearrange("p o c -> p (o c)")).then_inc(s_sm[c % R_SM], 16)
                        sp.dma_start(dstb[:, c % R_SM, :], a["dst"][bass.ds(e0, GE)].partition_broadcast(P)).then_inc(s_sm[c % R_SM], 16)
                    if loop or 0 <= c - STORE_LAG < STEPS:
                        old = UNROLL * i + (c - STORE_LAG)
                        b = sp.value_load(t["step_ints"][0:1, 0, bass.ds(old, 1)], min_val=0, max_val=BLOCKS - 1)
                        g = sp.value_load(t["step_ints"][0:1, 1, bass.ds(old, 1)], min_val=0, max_val=GROUPS - 1)
                        sp.wait_ge(s_sums_st, 16 * old)
                        sp.wait_ge(s_run, old + 1)
                        sp.dma_start(sums_d[bass.ds(b, 1), :, :].rearrange("o p c -> p (o c)"), run[:, (c - STORE_LAG) % R_RUN, :]).then_inc(s_sums_st, 16)
                        sp.wait_ge(s_qk_st, 16 * old)
                        sp.wait_ge(s_qktc, old + 1)
                        sp.dma_start(qk_d[bass.ds(g, 1), :, :].rearrange("o r e -> r (o e)"), qkt[:, (c - STORE_LAG) % R_RUN, :]).then_inc(s_qk_st, 16)
                every(sp, body, PEEL, STEPS + STORE_LAG)
                sp.wait_ge(s_sums_st, 16 * STEPS)
                sp.wait_ge(s_qk_st, 16 * STEPS)

            @block.tensor
            def _(pe):
                def transpose(c, i):
                    s = UNROLL * i + c
                    pe.wait_ge(s_ea[c % R_EA], 16 * use(c, i, R_EA))
                    if not (isinstance(i, int) and c == 0):
                        pe.wait_ge(s_eat, s)
                    for j in range(TILES):
                        last = nc.tensor.transpose(eat_ps[:, j * P:(j + 1) * P], ea[:, c % R_EA, j, :], ident[:])
                    last.then_inc(s_tr, 1)

                def body(c, i, loop):
                    s = UNROLL * i + c
                    if is_step(c - 3, loop):
                        pe.wait_ge(s_h1, s - 2)
                        pe.wait_ge(s_h2, s - 2)
                        pe.wait_ge(s_oh, s - 2)
                        pe.wait_ge(s_qktc, s - 3)
                        for j in range(TILES):
                            last = nc.tensor.matmul(agg_ps, oh[:, (c - 3) % 2, j, :], hh[:, (c - 3) % 2, j, :],
                                                    start=(j == 0), stop=(j == TILES - 1))
                        last.then_inc(s_agg, 1)
                    if c == 0 and not loop:
                        transpose(0, 0)
                    if is_step(c + 1, loop):
                        transpose(c + 1, i)
                    if is_step(c, loop):
                        pe.wait_ge(s_eat, s + 1)
                        for half in range(2):
                            if loop or c >= 1:
                                pe.wait_ge(s_p[half], s)
                            for k in range(2):
                                last = nc.tensor.matmul(pair[half][:, k, :], eat[:, c % 2, (2 * half + k) * P:(2 * half + k + 1) * P],
                                                        t["w_edge"][:], start=True, stop=True)
                            last.then_inc(s_proj[half], 1)
                    if is_step(c - 3, loop):
                        pe.wait_ge(s_qkr, s - 2)
                        pe.wait_ge(s_run, s - 2)
                        nc.tensor.transpose(qkt_ps, qkr[:, (c - 3) % R_RUN, :], ident[:]).then_inc(s_qkt, 1)
                    if is_step(c - 1, loop):
                        pe.wait_ge(s_oht, s)
                        pe.wait_ge(s_sm[(c - 1) % R_SM], 32 * use(c - 1, i, R_SM))
                        if loop or c >= 2:
                            pe.wait_ge(s_pq, s - 1)
                            pe.wait_ge(s_qk, s - 1)
                        for j in range(TILES):
                            for part in range(3):
                                last = nc.tensor.matmul(qx4[:, j // 2, j % 2, :], oht[:, (c - 1) % 2, j * P:(j + 1) * P],
                                                        qb[:, (c - 1) % R_SM, part * QW:(part + 1) * QW], start=(part == 0), stop=(part == 2))
                        last.then_inc(s_qx, 1)
                every(pe, body, PEEL, STEPS + 3)

            @block.scalar
            def _(act):
                def copy_eat(c, i):
                    s = UNROLL * i + c
                    act.wait_ge(s_tr, s + 1)
                    if not (isinstance(i, int) and c < 2):
                        act.wait_ge(s_proj[1], s - 1)
                    nc.scalar.activation(eat[:, c % 2, :], eat_ps, ACT.Copy).then_inc(s_eat, 1)

                def square_y(half, c, i, loop):
                    s = UNROLL * i + c
                    act.wait_ge(s_proj[half], s + 1)
                    if loop or c >= 1:
                        act.wait_ge(s_yv[half], s)
                    nc.scalar.activation(ysq[:, half, :, :], pair[half][:, :, 0:2 * F], ACT.Square).then_inc(s_ysq[half], 1)

                def rstd_y(half, c, i, loop):
                    s = UNROLL * i + c
                    act.wait_ge(s_yv[half], s + 1)
                    nc.scalar.activation(yln[:, half, :, :], yvar[:, half, :, :], ACT.Ln, bias=t["eps_c"][:, 0:1], scale=1.0 / D).then_inc(s_yl[half], 1)
                    act.wait_ge(s_yl[half], s + 1)
                    if loop or c >= 1:
                        act.wait_ge(s_p[half], s)
                    nc.scalar.activation(yr[:, half, :, :], yln[:, half, :, :], ACT.Exp, scale=-0.5).then_inc(s_yr[half], 1)

                def body(c, i, loop):
                    s = UNROLL * i + c
                    first, second = is_step(c, loop), is_step(c - 2, loop)
                    if c == 0 and not loop:
                        copy_eat(0, 0)
                    if second:
                        act.wait_ge(s_ga[(c - 2) % R_P], 64 * use(c - 2, i, R_P))
                        if loop or c >= 3:
                            act.wait_ge(s_z, s - 2)
                        nc.scalar.activation(z[:, :, 0:2 * F], p[:, (c - 2) % R_P, :, :], ACT.Square).then_inc(s_psq, 1)
                    if first:
                        square_y(0, c, i, loop)
                        rstd_y(0, c, i, loop)
                    if is_step(c + 1, loop):
                        copy_eat(c + 1, i)
                    if first:
                        square_y(1, c, i, loop)
                    if second:
                        act.wait_ge(s_z, s - 1)
                        nc.scalar.activation(zln[:], zs[:, :, 0:2 * H], ACT.Ln, bias=t["eps_c"][:, 0:1], scale=1.0 / D).then_inc(s_zl, 1)
                        act.wait_ge(s_zl, s - 1)
                        if loop or c >= 3:
                            act.wait_ge(s_w2, s - 2)
                            act.wait_ge(s_h1, s - 2)
                        nc.scalar.activation(zr[:], zln[:], ACT.Exp, scale=-0.5).then_inc(s_zr, 1)
                    if first:
                        rstd_y(1, c, i, loop)
                        act.wait_ge(s_sm[c % R_SM], 32 * use(c, i, R_SM))
                        act.wait_ge(s_meta[c % R_META], 32 * use(c, i, R_META))
                        if loop or c >= 1:
                            act.wait_ge(s_oht, s)
                        nc.scalar.activation(oht_a[:], dstb[:, c % R_SM, :], ACT.Abs, bias=scol[:, c % R_META, 1:2]).then_inc(s_oha, 1)
                        act.wait_ge(s_oha, s + 1)
                        if loop or c >= 2:
                            act.wait_ge(s_qx, s - 1)
                        nc.scalar.activation(oht[:, c % 2, :], oht_a[:], ACT.Relu, bias=1.0, scale=-1.0).then_inc(s_oht, 1)
                    if is_step(c - 3, loop):
                        act.wait_ge(s_qkt, s - 2)
                        if loop or c - 3 >= R_RUN:
                            act.wait_ge(s_qk_st, 16 * (s - 3 - R_RUN + 1))
                        nc.scalar.activation(qkt[:, (c - 3) % R_RUN, :], qkt_ps, ACT.Copy).then_inc(s_qktc, 1)
                    if second:
                        if loop or c >= 3:
                            act.wait_ge(s_ohb, TILES * (s - 2))
                        nc.scalar.activation(rel[:], gcol[:, (c - 2) % R_META, TILES:2 * TILES], ACT.Identity,
                                             bias=scol[:, (c - 2) % R_META, 0:1]).then_inc(s_rel, 1)
                        act.wait_ge(s_rel, s - 1)
                        if loop or c >= 3:
                            act.wait_ge(s_oh, s - 2)
                        for j in range(TILES):
                            nc.scalar.activation(oh_a[:, j, :], t["iota_n"][:], ACT.Abs, bias=rel[:, j:j + 1]).then_inc(s_ohb, 1)
                        act.wait_ge(s_ohb, TILES * (s - 1))
                        if loop or c >= 4:
                            act.wait_ge(s_agg, s - 3)
                        nc.scalar.activation(oh[:, (c - 2) % 2, :, :], oh_a[:], ACT.Relu, bias=1.0, scale=-1.0).then_inc(s_oh, 1)
                every(act, body, PEEL, STEPS + 3)

            @block.gpsimd
            def _(pool):
                last_node = pool.alloc_register("last_node")
                nodes_less_2 = pool.to_reg(N - 2)

                def gather(half, c, i, loop):
                    pool.wait_ge(s_p[half], UNROLL * i + c + 1)
                    pool.reg_add(last_node, nodes_less_2, 1)
                    for j in (2 * half, 2 * half + 1):
                        pool.indirect_dma_start(out=p[:, c % R_P, j, :], out_offset=None, in_=table,
                                                in_offset=bass.IndirectOffsetOnAxis(ap=gcol[:, c % R_META, j:j + 1].bitcast(u32), axis=0),
                                                bounds_check=last_node, oob_is_err=True, compute_op=ALU.add).then_inc(s_ga[c % R_P], 16)

                def body(c, i, loop):
                    s = UNROLL * i + c
                    if is_step(c, loop):
                        pool.wait_ge(s_meta[c % R_META], 32 * use(c, i, R_META))
                        gather(0, c, i, loop)
                    if is_step(c - 2, loop):
                        pool.wait_ge(s_ga[(c - 2) % R_P], 64 * use(c - 2, i, R_P))
                        pool.wait_ge(s_zr, s - 1)
                        if loop or c >= 4:
                            pool.wait_ge(s_agg, s - 3)
                        nc.gpsimd.tensor_tensor(out=hh[:, (c - 2) % 2, :, 0:F].rearrange("p t (h d) -> p t h d", d=D),
                                                in0=p[:, (c - 2) % R_P, :, F:2 * F].rearrange("p t (h d) -> p t h d", d=D),
                                                in1=zr[:, :, H:2 * H].unsqueeze(3).to_broadcast([P, TILES, H, D]), op=ALU.mult).then_inc(s_h1, 1)
                    if is_step(c, loop):
                        gather(1, c, i, loop)
                every(pool, body, PEEL, STEPS + 3)

            @block.vector
            def _(dve):
                v = nc.vector
                heads = lambda ap: ap.rearrange("p t (h d) -> p t h d", d=D)
                v.memset(hh[:, :, :, AW - 1:AW], 1.0).then_inc(s_init, 1)
                v.memset(run[:, R_RUN - 1, :], 0.0).then_inc(s_init, 1)
                v.memset(qkr[:, R_RUN - 1, :], 0.0).then_inc(s_init, 1)
                dve.wait_ge(s_init, 3)

                def sum_y(half, c, i, loop):
                    s = UNROLL * i + c
                    dve.wait_ge(s_ysq[half], s + 1)
                    if loop or c >= 1:
                        dve.wait_ge(s_yl[half], s)
                    v.tensor_reduce(out=yvar[:, half, :, :], in_=heads(ysq[:, half, :, :]), axis=AX.X, op=ALU.add).then_inc(s_yv[half], 1)

                def scale(half, c, i, loop):
                    s = UNROLL * i + c
                    dve.wait_ge(s_yr[half], s + 1)
                    if half == 0 and (loop or c >= R_P):
                        dve.wait_ge(s_h1, s - R_P + 1)
                        dve.wait_ge(s_h2, s - R_P + 1)
                        dve.wait_ge(s_psq, s - R_P + 1)
                    v.tensor_tensor(out=heads(p[:, c % R_P, 2 * half:2 * half + 2, :]), in0=heads(pair[half][:, :, 2 * F:4 * F]),
                                    in1=yr[:, half, :, :].unsqueeze(3).to_broadcast([P, 2, 2 * H, D]), op=ALU.mult).then_inc(s_p[half], 1)

                def body(c, i, loop):
                    s = UNROLL * i + c
                    first, second = is_step(c, loop), is_step(c - 2, loop)
                    h = hh[:, (c - 2) % 2, :, :]
                    if first:
                        sum_y(0, c, i, loop)
                    if second:
                        dve.wait_ge(s_ga[(c - 2) % R_P], 64 * use(c - 2, i, R_P))
                        dve.wait_ge(s_qx, s - 1)
                        if loop or c >= 3:
                            dve.wait_ge(s_z, s - 2)
                        v.tensor_tensor(out=tiles4(z[:, :, 2 * F:3 * F]), in0=tiles4(p[:, (c - 2) % R_P, :, 0:F]),
                                        in1=qx4[:, :, :, 0:F], op=ALU.mult).then_inc(s_pq, 1)
                    if is_step(c - 3, loop):
                        dve.wait_ge(s_agg, s - 2)
                        if loop or c >= 4:
                            dve.wait_ge(s_run, s - 3)
                        if loop or c - 3 >= R_RUN:
                            dve.wait_ge(s_sums_st, 16 * (s - 3 - R_RUN + 1))
                        v.scalar_tensor_tensor(out=run[:, (c - 3) % R_RUN, :], in0=run[:, (c - 4) % R_RUN, :],
                                               scalar=scol[:, (c - 3) % R_META, 2:3], in1=agg_ps, op0=ALU.mult, op1=ALU.add).then_inc(s_run, 1)
                    if first:
                        scale(0, c, i, loop)
                    if second:
                        dve.wait_ge(s_psq, s - 1)
                        dve.wait_ge(s_pq, s - 1)
                        if loop or c >= 3:
                            dve.wait_ge(s_zl, s - 2)
                            dve.wait_ge(s_qk0, s - 2)
                        v.tensor_reduce(out=zs[:], in_=heads(z[:]), axis=AX.X, op=ALU.add).then_inc(s_z, 1)
                    if first:
                        sum_y(1, c, i, loop)
                    if second:
                        dve.wait_ge(s_zr, s - 1)
                        dve.wait_ge(s_z, s - 1)
                        if loop or c >= 3:
                            dve.wait_ge(s_qk, s - 2)
                        v.tensor_tensor(out=qk0[:], in0=zs[:, :, 2 * H:3 * H], in1=zr[:, :, 0:H], op=ALU.mult).then_inc(s_qk0, 1)
                        dve.wait_ge(s_qk0, s - 1)
                        if loop or c >= 4:
                            dve.wait_ge(s_agg, s - 3)
                        v.tensor_tensor(out=tiles4(h[:, :, 2 * F:2 * F + H]), in0=tiles4(qk0[:]), in1=qx4[:, :, :, F:QW], op=ALU.add).then_inc(s_qk, 1)
                    if first:
                        scale(1, c, i, loop)
                    if second:
                        dve.wait_ge(s_qk, s - 1)
                        if loop or c >= 3:
                            dve.wait_ge(s_h2, s - 2)
                        v.tensor_tensor(out=w2[:], in0=h[:, :, 2 * F:2 * F + H], in1=zr[:, :, H:2 * H], op=ALU.mult).then_inc(s_w2, 1)
                        if loop or c >= 3:
                            dve.wait_ge(s_qkr, s - 2)
                        if loop or c >= 2 + R_RUN:
                            dve.wait_ge(s_qkt, s - 1 - R_RUN)
                        v.scalar_tensor_tensor(out=qkr[:, (c - 2) % R_RUN, :].rearrange("p (t h) -> p t h", h=H),
                                               in0=qkr[:, (c - 3) % R_RUN, :].rearrange("p (t h) -> p t h", h=H),
                                               scalar=scol[:, (c - 2) % R_META, 3:4], in1=h[:, :, 2 * F:2 * F + H],
                                               op0=ALU.mult, op1=ALU.add).then_inc(s_qkr, 1)
                        dve.wait_ge(s_w2, s - 1)
                        v.tensor_tensor(out=heads(h[:, :, F:2 * F]), in0=heads(p[:, (c - 2) % R_P, :, F:2 * F]),
                                        in1=w2[:].unsqueeze(3).to_broadcast([P, TILES, H, D]), op=ALU.mult).then_inc(s_h2, 1)
                every(dve, body, PEEL, STEPS + 3)


def softmax(nc, a, sem, bank, t):
    f32, bf16, i32 = mybir.dt.float32, mybir.dt.bfloat16, mybir.dt.int32
    ALU, ACT = mybir.AluOpType, mybir.ActivationFunctionType
    qk_t = t["qk_d"].rearrange("g (j h) e -> (g j) h e", h=H)
    with ExitStack() as scope:
        def sb(name, shape, dt=f32):
            return scope.enter_context(nc.sbuf_tensor(name, shape, dt))

        x = sb("m_x", [P, CE])
        m = sb("m_m", [P, CE + 1])
        fresh = sb("m_fresh", [P, CE], bf16)
        ratio = sb("m_ratio", [P, CE])
        junk = sb("m_junk", [P, 2, CE // 7])
        ends = sb("m_ends", [P, 2])
        row = sb("m_row", [1, 2, P])
        row_t = sb("m_row_t", [1, P])
        row_in = sb("m_row_in", [1, P])
        col_in = sb("m_col_in", [P, 2])
        lse_sb = sb("m_lse", [P, 4, 512])
        s_ld, s_pre, s_ch, s_tp, s_ex, s_act = (sem("soft_loads"), sem("soft_pads"), sem("soft_chain"), sem("soft_rows"),
                                                sem("soft_exp"), sem("soft_dve_for_act"))
        s_l, s_lt, s_lc, s_pe = sem("soft_lse"), sem("soft_lse_T"), sem("soft_lse_copied"), sem("soft_for_pe")
        s_ls = [sem(f"soft_lse_stored{i}") for i in range(4)]
        d_i = m[:].bitcast(i32)
        C15 = CHUNKS - 1
        FULL = (GROUPS - 1) * TILES - C15 * CT
        REAL = E - C15 * CE
        SUB, NSUB = CE // 7, 7
        head, sub = E - (GROUPS - 1) * GE, []
        n_loads = []

        with nc.allow_non_contiguous_dma(reason="rows of 512 bytes"), nc.Block() as block:
            @block.gpsimd
            def _(pool):
                nc.gpsimd.memset(x[96:P, REAL:CE], -BIG).then_inc(s_pre, 1)
                nc.gpsimd.memset(d_i[96:P, REAL + 1:CE + 1], -7).then_inc(s_pre, 1)
                nc.gpsimd.memset(d_i[0:32, 0:1], -7).then_inc(s_pre, 1)

            @block.sync
            def _(sp):
                n = [0]

                def load(dst_ap, src_ap):
                    sp.dma_start(dst_ap, src_ap).then_inc(s_ld, 16)
                    n[0] += 1

                sp.wait_ge(s_pre, 3)
                for c in range(CHUNKS):
                    rows = slice(H * c, H * c + H)
                    lo = 0 if c else 1
                    hi = CE + 1 if c < C15 else REAL + 1
                    load(d_i[rows, lo:hi], a["dst"][CE * c - 1 + lo:CE * c - 1 + hi].partition_broadcast(H))
                for c in range(CHUNKS):
                    rows = slice(H * c, H * c + H)
                    k = CT if c < C15 else FULL
                    load(x[rows, 0:k * P].rearrange("h (t e) -> h t e", e=P), qk_t[CT * c:CT * c + k, :, :].rearrange("t h e -> h t e"))
                at, tile0 = FULL * P, (GROUPS - 1) * TILES
                for k in range(DUP // P, TILES):
                    e0 = DUP % P if k == DUP // P else 0
                    load(x[H * C15:P, at:at + P - e0], qk_t[tile0 + k, :, e0:P])
                    at += P - e0
                assert at == REAL
                n_loads.append(n[0])
                for k in range(-(-CT // 4)):
                    tiles = min(4, CT - 4 * k)
                    sp.wait_ge(s_lc, k + 1)
                    sp.dma_start(t["lse_d"][4 * k * P:(4 * k + tiles) * P, :].rearrange("(t p) c -> p t c", p=P),
                                 lse_sb[:, k % 4, 0:tiles * P].rearrange("p (t c) -> p t c", c=P)).then_inc(s_ls[k % 4], 16)
                K = -(-CT // 4)
                for q in range(4):
                    sp.wait_ge(s_ls[q], 16 * len(range(q, K, 4)))

            @block.vector
            def _(dve):
                v = nc.vector
                done = [0]

                def link(ins):
                    done[0] += 1
                    ins.then_inc(s_ch, 1)
                    dve.wait_ge(s_ch, done[0])

                def carry(state, op0, op1, first, part):
                    v.tensor_copy(out=row[:], in_=bank[0][0:1, 0:2 * P].rearrange("o (r c) -> o r c", r=2)).then_inc(s_ch, 1)
                    done[0] += 1
                    dve.wait_ge(s_ch, done[0])
                    for h in range(H):
                        by_c = lambda ap: ap.rearrange("o (c h) -> o c h", h=H)[:, :, h]
                        v.tensor_tensor_scan(out=by_c(row_t[:]), data0=by_c(row[0:1, 1, :]), data1=by_c(row[0:1, 0, :]),
                                             initial=first, op0=op0, op1=op1).then_inc(s_ch, 1)
                        done[0] += 1
                    dve.wait_ge(s_ch, done[0])
                    link(v.memset(row_in[0:1, 0:H], first))
                    v.tensor_copy(out=row_in[0:1, H:P], in_=row_t[0:1, 0:P - H]).then_inc(s_ch, 1)
                    done[0] += 1
                    dve.wait_ge(s_ch, done[0])
                    v.tensor_copy(out=junk[0:1, 0, 0:1], in_=row_in[0:1, 0:1]).then_inc(s_pe, 1)

                dve.wait_ge(s_ld, 16 * n_loads[0])
                link(v.tensor_tensor(out=fresh[:], in0=d_i[:, 1:CE + 1], in1=d_i[:, 0:CE], op=ALU.not_equal))
                link(v.tensor_scalar(out=fresh[:], in0=fresh[:], scalar1=-BIG, scalar2=None, op0=ALU.mult))
                link(v.tensor_tensor(out=ends[:, 1:2], in0=d_i[:, CE:CE + 1], in1=d_i[:, 0:1], op=ALU.not_equal))
                link(v.tensor_scalar(out=ends[:, 1:2], in0=ends[:, 1:2], scalar1=-BIG, scalar2=None, op0=ALU.mult))
                link(v.tensor_tensor_scan(out=m[:, 1:CE + 1], data0=fresh[:], data1=x[:], initial=-BIG, op0=ALU.add, op1=ALU.max))
                v.tensor_copy(out=ends[:, 0:1], in_=m[:, CE:CE + 1]).then_inc(s_pe, 1)
                dve.wait_ge(s_tp, 1)
                carry(0, ALU.add, ALU.max, -BIG, 0)
                dve.wait_ge(s_tp, 2)
                link(v.tensor_copy(out=col_in[:, 0:1], in_=bank[1][:, 0:1]))
                link(v.tensor_copy(out=m[:, 0:1], in_=col_in[:, 0:1]))
                link(v.tensor_tensor_scan(out=m[:, 1:CE + 1], data0=fresh[:], data1=x[:], initial=col_in[:, 0:1], op0=ALU.add, op1=ALU.max))
                for k in range(NSUB):
                    lo, hi = k * SUB, (k + 1) * SUB
                    v.tensor_tensor(out=x[:, lo:hi], in0=x[:, lo:hi], in1=m[:, lo + 1:hi + 1], op=ALU.subtract).then_inc(s_act, 1)
                    link(v.tensor_tensor(out=ratio[:, lo:hi], in0=m[:, lo:hi], in1=m[:, lo + 1:hi + 1], op=ALU.subtract))
                    v.tensor_tensor(out=ratio[:, lo:hi], in0=ratio[:, lo:hi], in1=fresh[:, lo:hi], op=ALU.add).then_inc(s_act, 1)
                link(v.tensor_tensor(out=ends[:, 0:1], in0=col_in[:, 0:1], in1=m[:, CE:CE + 1], op=ALU.subtract))
                v.tensor_tensor(out=ends[:, 1:2], in0=ends[:, 0:1], in1=ends[:, 1:2], op=ALU.add).then_inc(s_act, 1)
                for k in range(NSUB):
                    lo, hi = k * SUB, (k + 1) * SUB
                    dve.wait_ge(s_ex, 2 * (k + 1))
                    link(v.tensor_tensor_scan(out=junk[:, k % 2, :], data0=ratio[:, lo:hi], data1=x[:, lo:hi],
                                              initial=0.0 if k == 0 else junk[:, (k - 1) % 2, SUB - 1:SUB], op0=ALU.mult, op1=ALU.add))
                dve.wait_ge(s_ex, 2 * NSUB + 1)
                v.tensor_copy(out=ends[:, 0:1], in_=junk[:, (NSUB - 1) % 2, SUB - 1:SUB]).then_inc(s_pe, 1)
                dve.wait_ge(s_tp, 3)
                carry(1, ALU.mult, ALU.add, 0.0, 1)
                dve.wait_ge(s_tp, 4)
                link(v.tensor_copy(out=col_in[:, 1:2], in_=bank[1][:, 0:1]))
                for k in range(NSUB):
                    lo, hi = k * SUB, (k + 1) * SUB
                    v.tensor_tensor_scan(out=x[:, lo:hi], data0=ratio[:, lo:hi], data1=x[:, lo:hi],
                                         initial=col_in[:, 1:2] if k == 0 else junk[:, k % 2, 0:1], op0=ALU.mult, op1=ALU.add).then_inc(s_ch, 1)
                    done[0] += 1
                    dve.wait_ge(s_ch, done[0])
                    v.tensor_copy(out=junk[:, (k + 1) % 2, 0:1], in_=x[:, hi - 1:hi]).then_inc(s_act, 1)
                    dve.wait_ge(s_act, 2 * NSUB + 1 + k + 1)
                    if k >= 1:
                        dve.wait_ge(s_ex, 2 * NSUB + 1 + k)
                        v.tensor_tensor(out=x[:, lo - SUB:lo], in0=x[:, lo - SUB:lo], in1=m[:, lo - SUB + 1:lo + 1], op=ALU.add).then_inc(s_l, 1)
                dve.wait_ge(s_ex, 3 * NSUB + 1)
                v.tensor_tensor(out=x[:, CE - SUB:CE], in0=x[:, CE - SUB:CE], in1=m[:, CE - SUB + 1:CE + 1], op=ALU.add).then_inc(s_l, 1)
                for k in range(1, -(-CT // 4), 2):
                    tiles = min(4, CT - 4 * k)
                    dve.wait_ge(s_lt, k + 1)
                    if k >= 4:
                        dve.wait_ge(s_ls[k % 4], 16 * (k // 4))
                    dve.wait_ge(s_lc, k)
                    v.tensor_copy(out=lse_sb[:, k % 4, 0:tiles * P], in_=bank[2 + k % 4][:, 0:tiles * P]).then_inc(s_lc, 1)

            @block.scalar
            def _(act):
                for k in range(NSUB):
                    lo, hi = k * SUB, (k + 1) * SUB
                    act.wait_ge(s_act, 2 * k + 1)
                    nc.scalar.activation(x[:, lo:hi], x[:, lo:hi], ACT.Exp).then_inc(s_ex, 1)
                    act.wait_ge(s_act, 2 * k + 2)
                    nc.scalar.activation(ratio[:, lo:hi], ratio[:, lo:hi], ACT.Exp).then_inc(s_ex, 1)
                act.wait_ge(s_act, 2 * NSUB + 1)
                nc.scalar.activation(ends[:, 1:2], ends[:, 1:2], ACT.Exp).then_inc(s_ex, 1)
                for k in range(NSUB):
                    lo, hi = k * SUB, (k + 1) * SUB
                    act.wait_ge(s_act, 2 * NSUB + 1 + k + 1)
                    nc.scalar.activation(x[:, lo:hi], x[:, lo:hi], ACT.Ln).then_inc(s_ex, 1)
                for k in range(0, -(-CT // 4), 2):
                    tiles = min(4, CT - 4 * k)
                    act.wait_ge(s_lt, k + 1)
                    if k >= 4:
                        act.wait_ge(s_ls[k % 4], 16 * (k // 4))
                    act.wait_ge(s_lc, k)
                    nc.scalar.activation(lse_sb[:, k % 4, 0:tiles * P], bank[2 + k % 4][:, 0:tiles * P], ACT.Copy).then_inc(s_lc, 1)

            @block.tensor
            def _(pe):
                for part in range(2):
                    pe.wait_ge(s_pe, 2 * part + 1)
                    nc.tensor.transpose(bank[0][0:1, 0:P], ends[:, 0:1], t["ident"][:])
                    nc.tensor.transpose(bank[0][0:1, P:2 * P], ends[:, 1:2], t["ident"][:]).then_inc(s_tp, 1)
                    pe.wait_ge(s_pe, 2 * part + 2)
                    nc.tensor.matmul(bank[1][:, 0:1], row_in[0:1, :], t["one_c"][0:1, 0:1], start=True, stop=True).then_inc(s_tp, 1)
                for k in range(-(-CT // 4)):
                    tiles = min(4, CT - 4 * k)
                    pe.wait_ge(s_l, -(-(4 * k + tiles) * P // SUB))
                    if k >= 4:
                        pe.wait_ge(s_lc, k - 3)
                    for j in range(tiles):
                        last = nc.tensor.transpose(bank[2 + k % 4][:, j * P:(j + 1) * P], x[:, (4 * k + j) * P:(4 * k + j + 1) * P], t["ident"][:])
                    last.then_inc(s_lt, 1)


def finish(nc, a, sem, bank, t, out):
    f32, i32, u32 = mybir.dt.float32, mybir.dt.int32, mybir.dt.uint32
    ALU, ACT, AX = mybir.AluOpType, mybir.ActivationFunctionType, mybir.AxisListType
    ident, rows16 = t["ident"], t["rows16"]
    ZB, ZG, ZBETA = 4, 5, 6
    NBK = 4
    TURNS = BLOCKS // NBK
    assert TURNS % 2 == 0 and BLOCKS % NBK == 1
    with ExitStack() as scope:
        def sb(name, shape, dt=f32):
            return scope.enter_context(nc.sbuf_tensor(name, shape, dt))

        cnt = sb("f_cnt", [P, BLOCKS])
        tri = sb("f_tri", [P, P])
        ones = sb("f_ones", [P, P])
        tot = sb("f_tot", [P, BLOCKS])
        pre = sb("f_pre", [P, BLOCKS])
        end = sb("f_end", [P, BLOCKS])
        thr_i = sb("f_thr_i", [P, CHUNKS + 1], i32)
        thr = sb("f_thr", [P, CHUNKS + 1])
        ge = sb("f_ge", [P, BLOCKS, CHUNKS + 1])
        oc = sb("f_oc", [P, BLOCKS, CHUNKS])
        nc_ = sb("f_nc", [P, BLOCKS])
        idx = sb("f_idx", [P, BLOCKS + 3], i32)
        idc = sb("f_idc", [P, 2, NBK], i32)
        sm = sb("f_sm", [P, 2, NBK, AW])
        xb = sb("f_x", [P, 2, NBK, F])
        lg = sb("f_lg", [P, 2, NBK, P])
        lt = sb("f_lt", [P, NBK, P])
        lse = sb("f_lse", [P, NBK, H])
        lc = sb("f_lc", [P, NBK, H])
        tq = sb("f_tq", [P, NBK, H])
        a1 = sb("f_a1", [P, NBK, F])
        ag = sb("f_ag", [P, NBK, F])
        agt = sb("f_agt", [P, NBK, P])
        u = sb("f_u", [P, NBK, F])
        z = sb("f_z", [P, NBK, F])
        zr = sb("f_zr", [P, NBK, F])
        mean = sb("f_mean", [P, NBK, H])
        zc = sb("f_zc", [P, NBK, F])
        zq = sb("f_zq", [P, NBK, F])
        var = sb("f_var", [P, NBK, H])
        lnv = sb("f_lnv", [P, NBK, H])
        r = sb("f_r", [P, NBK, H])
        y = sb("f_y", [P, NBK, F])
        m1 = sb("f_m1", [P, NBK])
        yc = sb("f_yc", [P, NBK, F])
        yq = sb("f_yq", [P, NBK, F])
        v1 = sb("f_v1", [P, NBK])
        l1 = sb("f_l1", [P, NBK])
        r1 = sb("f_r1", [P, NBK])
        o = sb("f_o", [P, 2, NBK, F])
        s_c, s_k, s_ch, s_t = sem("fin_count"), sem("fin_consts"), sem("fin_chain"), sem("fin_prefix")
        with nc.allow_non_contiguous_dma(reason="a count per node"), nc.Block() as block:
            @block.sync
            def _(sp):
                sp.dma_start(cnt[:], t["sums_d"][:, :, AW - 1:AW].rearrange("b p o -> p (b o)")).then_inc(s_c, 16)

            @block.gpsimd
            def _(pool):
                nc.gpsimd.memset(tri[:], 1.0).then_inc(s_k, 1)
                nc.gpsimd.memset(ones[:], 1.0).then_inc(s_k, 1)
                nc.gpsimd.iota(thr_i[:], pattern=[[CE, CHUNKS + 1]], base=0, channel_multiplier=0).then_inc(s_k, 1)
                pool.wait_ge(s_k, 1)
                nc.gpsimd.affine_select(out=tri[:], in_=tri[:], compare_op=ALU.is_ge, fill=0.0, base=0,
                                        pattern=[[1, P]], channel_multiplier=-1).then_inc(s_k, 1)

            @block.tensor
            def _(pe):
                pe.wait_ge(s_c, 16)
                pe.wait_ge(s_k, 4)
                nc.tensor.matmul(bank[0][:, 0:BLOCKS], tri[:], cnt[:], start=True, stop=True)
                nc.tensor.matmul(bank[1][:, 0:BLOCKS], ones[:], cnt[:], start=True, stop=True).then_inc(s_t, 1)

            @block.vector
            def _(dve):
                v = nc.vector
                done = [0]

                def link(ins):
                    done[0] += 1
                    ins.then_inc(s_ch, 1)
                    dve.wait_ge(s_ch, done[0])

                dve.wait_ge(s_k, 4)
                link(v.tensor_copy(out=thr[:], in_=thr_i[:]))
                link(v.memset(idx[:], 0))
                dve.wait_ge(s_t, 1)
                link(v.tensor_copy(out=tot[:], in_=bank[1][:, 0:BLOCKS]))
                link(v.memset(ge[:, :, 0], 0.0))
                link(v.tensor_tensor_scan(out=pre[:], data0=tot[:], data1=ge[:, :, 0], initial=0.0, op0=ALU.add, op1=ALU.add))
                link(v.tensor_tensor(out=pre[:], in0=pre[:], in1=tot[:], op=ALU.subtract))
                link(v.tensor_tensor(out=end[:], in0=pre[:], in1=bank[0][:, 0:BLOCKS], op=ALU.add))
                link(v.tensor_scalar(out=end[:], in0=end[:], scalar1=-1.0, scalar2=0.0, op0=ALU.add, op1=ALU.max))
                link(v.tensor_tensor(out=ge[:], in0=end[:].unsqueeze(2).to_broadcast([P, BLOCKS, CHUNKS + 1]),
                                     in1=thr[:].unsqueeze(1).to_broadcast([P, BLOCKS, CHUNKS + 1]), op=ALU.is_ge))
                link(v.tensor_tensor(out=oc[:], in0=ge[:, :, 0:CHUNKS], in1=ge[:, :, 1:CHUNKS + 1], op=ALU.subtract))
                link(v.tensor_reduce(out=nc_[:], in_=ge[:, :, 1:CHUNKS + 1], axis=AX.X, op=ALU.add))
                link(v.scalar_tensor_tensor(out=end[:], in0=nc_[:], scalar=-float(CE), in1=end[:], op0=ALU.mult, op1=ALU.add))
                link(v.tensor_copy(out=idx[:, 0:BLOCKS], in_=end[:]))

        s_in = [sem(f"fin_loaded{i}") for i in range(2)]
        s_g = [sem(f"fin_lse_gathered{i}") for i in range(2)]
        s_o = [sem(f"fin_stored{i}") for i in range(2)]
        names = ("idc lt lse lc a1 ag tq0 tq agt_ps agt z_ps u z zb relu mean0 mean zc zq var lnv r zn zg zbeta y m0 m1 yc yq v1 l1 r1 o").split()
        s = {n: sem("fin_" + n) for n in names}

        def turns(eng, body):
            for k in range(2):
                body(k, k, 1, NBK * k, NBK, P)
            with eng.Fori(1, TURNS // 2) as i:
                for k in range(2):
                    body(2 * i + k, k, i + 1, NBK * (2 * i + k), NBK, P)
            body(TURNS, 0, TURNS // 2 + 1, BLOCKS - 1, 1, LAST)

        with nc.Block() as block:
            @block.sync
            def _(sp):
                def load(slot, b, nb, rows):
                    sp.dma_start(sm[0:rows, slot, 0:nb, :], t["sums_d"][bass.ds(b, nb), 0:rows, :].rearrange("b p c -> p b c")).then_inc(s_in[slot], 16)
                    sp.dma_start(xb[0:rows, slot, 0:nb, :],
                                 a["x"][bass.ds(P * b, nb * rows), :].rearrange("(b p) f -> p b f", p=rows)).then_inc(s_in[slot], 16)

                def store(n, slot, b, nb, rows):
                    sp.wait_ge(s["o"], n + 1)
                    sp.dma_start(out[bass.ds(P * b, nb * rows), :].rearrange("(b p) f -> p b f", p=rows), o[0:rows, slot, 0:nb, :]).then_inc(s_o[slot], 16)

                load(0, 0, NBK, P)
                load(1, NBK, NBK, P)
                with sp.Fori(0, TURNS // 2 - 1) as i:
                    for k in range(2):
                        store(2 * i + k, k, NBK * (2 * i + k), NBK, P)
                        load(k, NBK * (2 * i + k + 2), NBK, P)
                store(TURNS - 2, 0, NBK * (TURNS - 2), NBK, P)
                load(0, BLOCKS - 1, 1, LAST)
                store(TURNS - 1, 1, NBK * (TURNS - 1), NBK, P)
                store(TURNS, 0, BLOCKS - 1, 1, LAST)
                sp.wait_ge(s_o[0], 16 * (TURNS // 2 + 1))
                sp.wait_ge(s_o[1], 16 * (TURNS // 2))

            @block.gpsimd
            def _(pool):
                g = nc.gpsimd
                last_row = pool.alloc_register("last_row")
                rows_less_2 = pool.to_reg(CE - 2)

                def gather(n, slot, nth, b, nb, rows):
                    g.tensor_copy(out=idc[:, slot, 0:nb], in_=idx[:, bass.ds(b, nb)]).then_inc(s["idc"], 1)
                    pool.wait_ge(s["idc"], n + 1)
                    pool.reg_add(last_row, rows_less_2, 1)
                    for k in range(nb):
                        pool.indirect_dma_start(out=lg[:, slot, k, :], out_offset=None, in_=t["lse_d"],
                                                in_offset=bass.IndirectOffsetOnAxis(ap=idc[:, slot, k:k + 1].bitcast(u32), axis=0),
                                                bounds_check=last_row, oob_is_err=True).then_inc(s_g[slot], 16)

                def body(n, slot, nth, b, nb, rows):
                    pool.wait_ge(s["zn"], n + 1)
                    rr = slice(0, rows)
                    r16 = lambda k: rows16[rr, k, :].unsqueeze(1).to_broadcast([rows, nb * H, D])
                    hd = lambda ap: ap.rearrange("p b (h d) -> p (b h) d", d=D)
                    g.tensor_tensor(out=hd(zc[rr, 0:nb, :]), in0=hd(zc[rr, 0:nb, :]), in1=r16(ZG), op=ALU.mult).then_inc(s["zg"], 1)
                    pool.wait_ge(s["zg"], n + 1)
                    g.tensor_tensor(out=hd(zc[rr, 0:nb, :]), in0=hd(zc[rr, 0:nb, :]), in1=r16(ZBETA), op=ALU.add).then_inc(s["zbeta"], 1)

                gather(0, 0, 1, 0, NBK, P)
                for k in range(2):
                    pool.wait_ge(s["lt"], k)
                    gather(k + 1, 1 - k, 0, NBK * (k + 1), NBK, P)
                    body(k, k, 0, 0, NBK, P)
                with pool.Fori(1, TURNS // 2 - 1) as i:
                    for k in range(2):
                        pool.wait_ge(s["lt"], 2 * i + k)
                        gather(2 * i + k + 1, 1 - k, 0, NBK * (2 * i + k + 1), NBK, P)
                        body(2 * i + k, k, 0, 0, NBK, P)
                for k in range(2):
                    n = TURNS - 2 + k
                    pool.wait_ge(s["lt"], n)
                    if k == 0:
                        gather(n + 1, 1, 0, NBK * (n + 1), NBK, P)
                    else:
                        gather(n + 1, 0, 0, BLOCKS - 1, 1, LAST)
                    body(n, k, 0, 0, NBK, P)
                body(TURNS, 0, 0, 0, 1, LAST)

            @block.tensor
            def _(pe):
                def body(n, slot, nth, b, nb, rows):
                    pe.wait_ge(s["ag"], n + 1)
                    pe.wait_ge(s["agt"], n)
                    for k in range(nb):
                        last = nc.tensor.transpose(bank[0][:, k * P:k * P + rows], ag[0:rows, k, :], ident[0:rows, 0:rows])
                    last.then_inc(s["agt_ps"], 1)
                    pe.wait_ge(s["agt"], n + 1)
                    pe.wait_ge(s["z"], n)
                    for k in range(nb):
                        last = nc.tensor.matmul(bank[1][0:rows, k * F:(k + 1) * F], agt[:, k, 0:rows], t["z_w"][:], start=True, stop=True)
                    last.then_inc(s["z_ps"], 1)
                turns(pe, body)

            @block.scalar
            def _(act):
                def body(n, slot, nth, b, nb, rows):
                    rr = slice(0, rows)
                    act.wait_ge(s["agt_ps"], n + 1)
                    act.wait_ge(s["z_ps"], n)
                    nc.scalar.activation(agt[:, 0:nb, 0:rows], bank[0][:, 0:nb * P].rearrange("p (b n) -> p b n", n=P)[:, :, 0:rows],
                                         ACT.Copy).then_inc(s["agt"], 1)
                    act.wait_ge(s["zb"], n + 1)
                    act.wait_ge(s["zc"], n)
                    nc.scalar.activation(zr[rr, 0:nb, :], z[rr, 0:nb, :], ACT.Relu).then_inc(s["relu"], 1)
                    act.wait_ge(s["zc"], n + 1)
                    act.wait_ge(s["var"], n)
                    nc.scalar.activation(zq[rr, 0:nb, :], zc[rr, 0:nb, :], ACT.Square).then_inc(s["zq"], 1)
                    act.wait_ge(s["var"], n + 1)
                    nc.scalar.activation(lnv[rr, 0:nb, :], var[rr, 0:nb, :], ACT.Ln, bias=t["eps_c"][rr, 0:1], scale=1.0 / D).then_inc(s["lnv"], 1)
                    act.wait_ge(s["lnv"], n + 1)
                    act.wait_ge(s["zn"], n)
                    nc.scalar.activation(r[rr, 0:nb, :], lnv[rr, 0:nb, :], ACT.Exp, scale=-0.5).then_inc(s["r"], 1)
                    act.wait_ge(s["yc"], n + 1)
                    act.wait_ge(s["v1"], n)
                    nc.scalar.activation(yq[rr, 0:nb, :], yc[rr, 0:nb, :], ACT.Square).then_inc(s["yq"], 1)
                    act.wait_ge(s["v1"], n + 1)
                    nc.scalar.activation(l1[rr, 0:nb], v1[rr, 0:nb], ACT.Ln, bias=t["eps_c"][rr, 0:1], scale=1.0 / F).then_inc(s["l1"], 1)
                    act.wait_ge(s["l1"], n + 1)
                    act.wait_ge(s["o"], n)
                    nc.scalar.activation(r1[rr, 0:nb], l1[rr, 0:nb], ACT.Exp, scale=-0.5).then_inc(s["r1"], 1)
                turns(act, body)

            @block.vector
            def _(dve):
                v = nc.vector

                def body(n, slot, nth, b, nb, rows):
                    rr = slice(0, rows)
                    hd = lambda ap: ap.rearrange("p b (h d) -> p b h d", d=D)
                    hf = lambda ap: ap.rearrange("p b (h d) -> p (b h) d", d=D)
                    per_head = lambda ap: ap[rr, 0:nb, :].unsqueeze(3).to_broadcast([rows, nb, H, D])
                    r16 = lambda k: rows16[rr, k, :].unsqueeze(1).to_broadcast([rows, nb * H, D])

                    def step(name, ins, *needs):
                        return ins

                    gathers = 16 * NBK * (nth - 1) + 16 * nb
                    dve.wait_ge(s_g[slot], gathers)
                    v.tensor_tensor(out=lt[rr, 0:nb, :].rearrange("p b (c h) -> p b c h", h=H),
                                    in0=lg[rr, slot, 0:nb, :].rearrange("p b (c h) -> p b c h", h=H),
                                    in1=oc[rr, bass.ds(b, nb), :].unsqueeze(3).to_broadcast([rows, nb, CHUNKS, H]), op=ALU.mult).then_inc(s["lt"], 1)
                    dve.wait_ge(s["lt"], n + 1)
                    v.tensor_reduce(out=lse[rr, 0:nb, :], in_=lt[rr, 0:nb, :].rearrange("p b (c h) -> p b h c", h=H), axis=AX.X, op=ALU.add).then_inc(s["lse"], 1)
                    dve.wait_ge(s["lse"], n + 1)
                    dve.wait_ge(s_in[slot], 32 * nth)
                    v.tensor_tensor(out=lc[rr, 0:nb, :], in0=lse[rr, 0:nb, :],
                                    in1=sm[rr, slot, 0:nb, AW - 1:AW].to_broadcast([rows, nb, H]), op=ALU.mult).then_inc(s["lc"], 1)
                    v.tensor_tensor(out=hd(a1[rr, 0:nb, :]), in0=hd(sm[rr, slot, 0:nb, 0:F]), in1=per_head(lse), op=ALU.mult).then_inc(s["a1"], 1)
                    dve.wait_ge(s["a1"], n + 1)
                    dve.wait_ge(s["agt_ps"], n)
                    v.tensor_tensor(out=ag[rr, 0:nb, :], in0=sm[rr, slot, 0:nb, F:2 * F], in1=a1[rr, 0:nb, :], op=ALU.subtract).then_inc(s["ag"], 1)
                    dve.wait_ge(s["lc"], n + 1)
                    v.tensor_tensor(out=tq[rr, 0:nb, :], in0=sm[rr, slot, 0:nb, 2 * F:2 * F + H], in1=lc[rr, 0:nb, :], op=ALU.subtract).then_inc(s["tq"], 1)
                    dve.wait_ge(s["tq"], n + 1)
                    v.tensor_tensor(out=hd(u[rr, 0:nb, :]), in0=t["z_beta_w"][rr, :].rearrange("p (h d) -> p h d", d=D).unsqueeze(1).to_broadcast([rows, nb, H, D]),
                                    in1=per_head(tq), op=ALU.mult).then_inc(s["u"], 1)
                    dve.wait_ge(s["u"], n + 1)
                    dve.wait_ge(s["z_ps"], n + 1)
                    dve.wait_ge(s["relu"], n)
                    v.tensor_tensor(out=z[rr, 0:nb, :], in0=bank[1][rr, 0:nb * F].rearrange("p (b f) -> p b f", f=F), in1=u[rr, 0:nb, :], op=ALU.add).then_inc(s["z"], 1)
                    dve.wait_ge(s["z"], n + 1)
                    v.tensor_tensor(out=hf(z[rr, 0:nb, :]), in0=hf(z[rr, 0:nb, :]), in1=r16(ZB), op=ALU.add).then_inc(s["zb"], 1)
                    dve.wait_ge(s["relu"], n + 1)
                    v.tensor_reduce(out=mean[rr, 0:nb, :], in_=hd(zr[rr, 0:nb, :]), axis=AX.X, op=ALU.add).then_inc(s["mean0"], 1)
                    dve.wait_ge(s["mean0"], n + 1)
                    v.tensor_scalar(out=mean[rr, 0:nb, :], in0=mean[rr, 0:nb, :], scalar1=1.0 / D, scalar2=None, op0=ALU.mult).then_inc(s["mean"], 1)
                    dve.wait_ge(s["mean"], n + 1)
                    v.tensor_tensor(out=hd(zc[rr, 0:nb, :]), in0=hd(zr[rr, 0:nb, :]), in1=per_head(mean), op=ALU.subtract).then_inc(s["zc"], 1)
                    dve.wait_ge(s["zq"], n + 1)
                    v.tensor_reduce(out=var[rr, 0:nb, :], in_=hd(zq[rr, 0:nb, :]), axis=AX.X, op=ALU.add).then_inc(s["var"], 1)
                    dve.wait_ge(s["r"], n + 1)
                    dve.wait_ge(s["zc"], n + 1)
                    v.tensor_tensor(out=hd(zc[rr, 0:nb, :]), in0=hd(zc[rr, 0:nb, :]), in1=per_head(r), op=ALU.mult).then_inc(s["zn"], 1)
                    dve.wait_ge(s["zbeta"], n + 1)
                    v.tensor_tensor(out=y[rr, 0:nb, :], in0=zc[rr, 0:nb, :], in1=xb[rr, slot, 0:nb, :], op=ALU.add).then_inc(s["y"], 1)
                    dve.wait_ge(s["y"], n + 1)
                    v.tensor_reduce(out=m1[rr, 0:nb], in_=y[rr, 0:nb, :], axis=AX.X, op=ALU.add).then_inc(s["m0"], 1)
                    dve.wait_ge(s["m0"], n + 1)
                    v.tensor_scalar(out=m1[rr, 0:nb], in0=m1[rr, 0:nb], scalar1=1.0 / F, scalar2=None, op0=ALU.mult).then_inc(s["m1"], 1)
                    dve.wait_ge(s["m1"], n + 1)
                    v.tensor_tensor(out=yc[rr, 0:nb, :], in0=y[rr, 0:nb, :], in1=m1[rr, 0:nb].unsqueeze(2).to_broadcast([rows, nb, F]), op=ALU.subtract).then_inc(s["yc"], 1)
                    dve.wait_ge(s["yq"], n + 1)
                    v.tensor_reduce(out=v1[rr, 0:nb], in_=yq[rr, 0:nb, :], axis=AX.X, op=ALU.add).then_inc(s["v1"], 1)
                    dve.wait_ge(s["r1"], n + 1)
                    dve.wait_ge(s["yc"], n + 1)
                    dve.wait_ge(s_o[slot], 16 * (nth - 1))
                    v.tensor_tensor(out=o[rr, slot, 0:nb, :], in0=yc[rr, 0:nb, :], in1=r1[rr, 0:nb].unsqueeze(2).to_broadcast([rows, nb, F]), op=ALU.mult).then_inc(s["o"], 1)
                turns(dve, body)


_WEIGHTS = ["Wq", "Wk", "Wv", "Wke", "Wve", "gq", "bq", "gk", "bk", "gv", "bv", "gke", "bke", "gve", "bve",
            "relk_W", "relk_b", "relk_g", "relk_beta", "relv_W", "relv_b", "relv_g", "relv_beta", "z_W", "z_b", "z_g", "z_beta"]


def kernel(**inputs):
    import concourse.bacc as _bacc
    from concourse.bass_utils import run_bass_kernel_spmd as _run

    nc = _bacc.Bacc("TRN2", target_bir_lowering=False, num_devices=1)
    arrays, aps = {}, {}
    names = {"x": "x", "src": "src", "dst": "dst", "edge_attr_128": "edge_attr_128"}
    names.update({w: "L0_gnn_" + w for w in _WEIGHTS})
    for short, name in names.items():
        arr = np.ascontiguousarray(inputs[name])
        arrays["in_" + short] = arr
        aps[short] = nc.dram_tensor("in_" + short, arr.shape, mybir.dt.from_np(arr.dtype), kind="ExternalInput").ap()
    out = nc.dram_tensor("out_0", (N, F), mybir.dt.float32, kind="ExternalOutput").ap()
    edge_attention(nc, aps, out)
    r = _run(nc, [arrays], core_ids=[0])
    return r.results[0]["out_0"]
```

```python
import numpy as np
import concourse.bass as bass
from concourse import mybir
from contextlib import ExitStack

P = 128
N, E, F, H, D = 6250, 200000, 128, 8, 16
TILES = 4
GE = TILES * P
GROUPS = -(-E // GE)
TAIL0 = E - GE
DUP = GROUPS * GE - E
BLOCKS = -(-N // P)
LAST = N - (BLOCKS - 1) * P
STEPS = GROUPS + BLOCKS - 1
EPS = 1e-5
QW = F + H
AW = 2 * F + H + 1
CHUNKS = P // H
CT = -(-(-(-E // P)) // CHUNKS)
CE = CT * P
BIG = 1.0e30
UNROLL = 6
RING = 6
STORE_LAG = 10
PEEL = 14



def edge_attention(nc, a, out):
    f32, bf16, i32, u32 = mybir.dt.float32, mybir.dt.bfloat16, mybir.dt.int32, mybir.dt.uint32
    ALU, ACT, AX = mybir.AluOpType, mybir.ActivationFunctionType, mybir.AxisListType
    ctx = ExitStack()
    with ctx:
        def sb(name, shape, dt=f32):
            return ctx.enter_context(nc.sbuf_tensor(name, shape, dt))

        def sem(name):
            return ctx.enter_context(nc.semaphore(name))

        table = nc.dram_tensor("node_table", [N, 2 * F], f32, kind="Internal").ap()
        sums_d = nc.dram_tensor("node_sums", [BLOCKS, P, AW], f32, kind="Internal").ap()
        qk_d = nc.dram_tensor("edge_qk", [GROUPS, TILES * H, P], f32, kind="Internal").ap()
        lse_d = nc.dram_tensor("edge_lse", [CE, P], f32, kind="Internal").ap()

        banks = ctx.enter_context(nc.psum_tensor("banks", [P, 8, 512], f32))
        bank = [banks[:, i, :] for i in range(8)]

        ident = sb("ident", [P, P])
        iota_p = sb("iota_p", [P, 1])
        z_w = sb("z_w", [P, F])
        z_beta_w = sb("z_beta_w", [P, F])
        rows16 = sb("rows16", [P, 9, D])
        eps_c = sb("eps_c", [P, 1])
        one_c = sb("one_c", [P, 1])

        mid = ctx.enter_context(ExitStack())

        def sb_mid(name, shape, dt=f32):
            return mid.enter_context(nc.sbuf_tensor(name, shape, dt))

        iota_n = sb_mid("iota_n", [P, P])
        w_node = sb_mid("w_node", [P, 5 * F])
        w_edge = sb_mid("w_edge", [P, 4 * F])
        table_bias = sb_mid("table_bias", [P, 2, F])
        gq4 = sb_mid("gq4", [P, F])
        bq4 = sb_mid("bq4", [P, F])
        gqb = sb_mid("gqb", [P, F])
        bqb = sb_mid("bqb", [P, H])
        cols = sb_mid("cols", [P, GROUPS, 2 * TILES])
        step_cols = sb_mid("step_cols", [P, STEPS, 4])
        step_ints = sb_mid("step_ints", [1, STEPS], i32)
        RELKG, RELKB, RELKBIAS, RELVBIAS, ZB, ZG, ZBETA = range(7)

        with ExitStack() as scope:
            def sbp(name, shape, dt=f32):
                return scope.enter_context(nc.sbuf_tensor(name, shape, dt))

            w_all = sbp("w_all", [P, 5, F])
            w_mean = sbp("w_mean", [P, 5 * H])
            w_c = sbp("w_c", [P, 5, F])
            w_ct = sbp("w_ct", [P, 4, F])
            rel4 = sbp("rel4", [P, 4, D])
            rel_mean = sbp("rel_mean", [P, 4])
            rel_c = sbp("rel_c", [P, 4, D])
            z4 = sbp("z4", [P, D])
            mask = sbp("mask", [P, F])
            bd = sbp("bd", [P, 4, F])
            bdg = sbp("bdg", [P, 4, F])
            zbd = sbp("zbd", [P, F])
            col = sbp("col", [P, 10])
            colb = sbp("colb", [P, 5, F])
            qrows = sbp("qrows", [P, 2, F])
            rb_mean = sbp("rb_mean", [P, 2])
            rb_c = sbp("rb_c", [P, 2, D])
            tmp_q = sbp("tmp_q", [P, F])
            src_i = sbp("src_i", [P, 13, P], i32)
            dst_i = sbp("dst_i", [P, 13, P], i32)
            src_f = sbp("src_f", [P, 13, P])
            dst_f = sbp("dst_f", [P, 13, P])
            iota_i = sbp("iota_i", [P, STEPS], i32)
            iota_s = sbp("iota_s", [P, STEPS])
            iota_pi = sbp("iota_pi", [P, 1], i32)
            last_i = sbp("last_i", [1, GROUPS - 1], i32)
            last_f = sbp("last_f", [1, GROUPS - 1])
            below = sbp("below", [P, GROUPS - 1])
            thr = sbp("thr", [P, 1])
            g_of = sbp("g_of", [P, 1])
            s_of = sbp("s_of", [P, 1])
            passed = sbp("passed", [P, STEPS])
            blk = sbp("blk", [P, STEPS + 1])
            grp = sbp("grp", [P, STEPS + 1])
            off_f = sbp("off_f", [1, STEPS])
            ones = sbp("ones", [P, P])
            s_load, s_const, s_chain, s_idx = sem("pro_loads"), sem("pro_consts"), sem("pro_chain"), sem("pro_index_loads")
            s_tp, s_tc, s_u, s_wb, s_step, s_stepv = (sem("pro_wT"), sem("pro_wT_copied"), sem("pro_products"),
                                                      sem("pro_mats"), sem("pro_bcast"), sem("pro_step_in"))
            s_it, s_ic_s, s_ic_d = sem("pro_idx_transposed"), sem("pro_src_copied"), sem("pro_dst_copied")
            s_conv = sem("pro_idx_floats")
            FULL = (GROUPS - 1) * TILES
            KB, KR = FULL // P, FULL % P

            loads, idx_loads = [], []

            with nc.allow_non_contiguous_dma(reason="small weight and index layouts"), nc.Block() as block:
                @block.sync
                def _(sp):
                    n = [0, 0]

                    def load(dst, src_ap, which=0):
                        sp.dma_start(dst, src_ap).then_inc((s_load, s_idx)[which], 16)
                        n[which] += 1

                    for i, name in enumerate(("Wq", "Wk", "Wv", "Wke", "Wve")):
                        load(w_all[:, i, :].rearrange("f (h d) -> f h d", h=H), a[name].rearrange("h f d -> f h d"))
                    for h in range(H):
                        rows = slice(D * h, D * h + D)
                        load(rel4[rows, 0:2, :], a["relk_W"].rearrange("(t d) e -> d t e", t=2))
                        load(rel4[rows, 2:4, :], a["relv_W"].rearrange("(t d) e -> d t e", t=2))
                        load(z4[rows, :], a["z_W"])
                        load(col[rows, 8:9], a["relv_g"].rearrange("(d o) -> d o", o=1))
                        load(col[rows, 9:10], a["relv_beta"].rearrange("(d o) -> d o", o=1))
                    for i, name in enumerate(("gke", "gk", "gve", "gv", "bke", "bk", "bve", "bv")):
                        load(col[:, i:i + 1], a[name].rearrange("h (d o) -> (h d) o", o=1))
                    for i, name in enumerate(("gq", "bq")):
                        load(qrows[:, i, :], a[name].rearrange("h d -> (h d)").partition_broadcast(P))
                    for i, name in enumerate(("relk_g", "relk_beta", "relk_b", "relv_b", "z_b", "z_g", "z_beta")):
                        load(rows16[:, i, :], a[name].partition_broadcast(P))
                    for i, (dst_t, name) in enumerate(((src_i, "src"), (dst_i, "dst"))):
                        load(dst_t[:, 0:KB, :], a[name][0:KB * P * P].rearrange("(k t e) -> t k e", t=P, e=P), 1)
                        load(dst_t[0:KR, KB, :], a[name][KB * P * P:FULL * P].rearrange("(t e) -> t e", e=P), 1)
                        load(dst_t[KR:KR + TILES, KB, :], a[name][TAIL0:E].rearrange("(t e) -> t e", e=P), 1)
                    load(last_i[0:1, :], a["dst"][0:(GROUPS - 1) * GE].rearrange("(g e) -> g e", e=GE)[:, GE - 1:GE]
                         .rearrange("g o -> o g"), 1)
                    loads.append(n[0])
                    idx_loads.append(n[1])

                @block.gpsimd
                def _(pool):
                    nc.gpsimd.memset(ident[:], 0.0).then_inc(s_const, 1)
                    nc.gpsimd.memset(mask[:], 1.0).then_inc(s_const, 1)
                    nc.gpsimd.memset(ones[:], 1.0).then_inc(s_const, 1)
                    nc.gpsimd.memset(eps_c[:], EPS).then_inc(s_const, 1)
                    nc.gpsimd.memset(one_c[:], 1.0).then_inc(s_const, 1)
                    nc.gpsimd.iota(iota_i[:], pattern=[[1, STEPS]], base=0, channel_multiplier=0).then_inc(s_const, 1)
                    nc.gpsimd.iota(iota_pi[:], pattern=[[0, 1]], base=0, channel_multiplier=1).then_inc(s_const, 1)
                    pool.wait_ge(s_const, 7)
                    nc.gpsimd.affine_select(out=ident[:], in_=ident[:], compare_op=ALU.not_equal, fill=1.0, base=0,
                                            pattern=[[-1, P]], channel_multiplier=1).then_inc(s_const, 1)
                    m3 = mask[:].rearrange("p (h d) -> p h d", d=D)
                    nc.gpsimd.affine_select(out=m3, in_=m3, compare_op=ALU.is_ge, fill=0.0, base=0,
                                            pattern=[[-D, H], [0, D]], channel_multiplier=1).then_inc(s_const, 1)
                    pool.wait_ge(s_const, 9)
                    nc.gpsimd.affine_select(out=m3, in_=m3, compare_op=ALU.is_ge, fill=0.0, base=D - 1,
                                            pattern=[[D, H], [0, D]], channel_multiplier=-1).then_inc(s_const, 1)

                CONSTS = 10

                @block.vector
                def _(dve):
                    v = nc.vector
                    done = [0]

                    def link(ins):
                        done[0] += 1
                        ins.then_inc(s_chain, 1)
                        dve.wait_ge(s_chain, done[0])

                    dve.wait_ge(s_const, CONSTS)
                    dve.wait_ge(s_load, 16 * loads[0])
                    link(v.tensor_reduce(out=w_mean[:], in_=w_all[:].rearrange("p i (h d) -> p (i h) d", d=D), axis=AX.X, op=ALU.add))
                    link(v.tensor_scalar(out=w_mean[:], in0=w_mean[:], scalar1=1.0 / D, scalar2=None, op0=ALU.mult))
                    link(v.tensor_tensor(out=w_c[:].rearrange("p i (h d) -> p (i h) d", d=D),
                                         in0=w_all[:].rearrange("p i (h d) -> p (i h) d", d=D),
                                         in1=w_mean[:].unsqueeze(2).to_broadcast([P, 5 * H, D]), op=ALU.subtract))
                    link(v.tensor_reduce(out=rel_mean[:], in_=rel4[:], axis=AX.X, op=ALU.add))
                    link(v.tensor_scalar(out=rel_mean[:], in0=rel_mean[:], scalar1=1.0 / D, scalar2=None, op0=ALU.mult))
                    link(v.tensor_tensor(out=rel_c[:], in0=rel4[:], in1=rel_mean[:].unsqueeze(2).to_broadcast([P, 4, D]), op=ALU.subtract))
                    m3 = mask[:].rearrange("p (h d) -> p h d", d=D)
                    for i in range(4):
                        link(v.tensor_tensor(out=bd[:, i, :].rearrange("p (h d) -> p h d", d=D), in0=m3,
                                             in1=rel_c[:, i, :].unsqueeze(1).to_broadcast([P, H, D]), op=ALU.mult))
                        link(v.tensor_scalar(out=bdg[:, i, :], in0=bd[:, i, :], scalar1=col[:, i:i + 1], scalar2=None, op0=ALU.mult))
                        link(v.tensor_copy(out=colb[:, i, :], in_=col[:, 4 + i:5 + i].to_broadcast([P, F])))
                    link(v.tensor_tensor(out=zbd[:].rearrange("p (h d) -> p h d", d=D), in0=m3,
                                         in1=z4[:].unsqueeze(1).to_broadcast([P, H, D]), op=ALU.mult))
                    link(v.tensor_scalar(out=z_w[:], in0=zbd[:], scalar1=col[:, 8:9], scalar2=None, op0=ALU.mult))
                    link(v.tensor_copy(out=colb[:, 4, :], in_=col[:, 9:10].to_broadcast([P, F])))
                    v.tensor_copy(out=w_node[:, 0:3 * F], in_=w_c[:, 0:3, :].rearrange("p i n -> p (i n)")).then_inc(s_wb, 1)
                    v.tensor_copy(out=w_edge[:, 0:2 * F], in_=w_c[:, 3:5, :].rearrange("p i n -> p (i n)")).then_inc(s_wb, 1)
                    for dst_t, row, r16 in ((gq4, 0, RELKG), (bq4, 1, RELKG), (gqb, 0, RELKB), (tmp_q, 1, RELKB)):
                        link(v.tensor_tensor(out=dst_t[:].rearrange("p (h d) -> p h d", d=D),
                                             in0=qrows[:, row, :].rearrange("p (h d) -> p h d", d=D),
                                             in1=rows16[:, r16, :].unsqueeze(1).to_broadcast([P, H, D]), op=ALU.mult))
                        link(v.tensor_scalar(out=dst_t[:], in0=dst_t[:], scalar1=0.25, scalar2=None, op0=ALU.mult))
                    link(v.tensor_reduce(out=bqb[:], in_=tmp_q[:].rearrange("p (h d) -> p h d", d=D), axis=AX.X, op=ALU.add))
                    link(v.tensor_reduce(out=rb_mean[:], in_=rows16[:, RELKBIAS:RELVBIAS + 1, :], axis=AX.X, op=ALU.add))
                    link(v.tensor_scalar(out=rb_mean[:], in0=rb_mean[:], scalar1=1.0 / D, scalar2=None, op0=ALU.mult))
                    link(v.tensor_tensor(out=rb_c[:], in0=rows16[:, RELKBIAS:RELVBIAS + 1, :],
                                         in1=rb_mean[:].unsqueeze(2).to_broadcast([P, 2, D]), op=ALU.subtract))
                    dve.wait_ge(s_u, 2)
                    v.tensor_copy(out=w_node[:, 3 * F:5 * F], in_=bank[1][:, 0:2 * F]).then_inc(s_wb, 1)
                    v.tensor_copy(out=w_edge[:, 2 * F:4 * F], in_=bank[1][:, 2 * F:4 * F]).then_inc(s_wb, 1)
                    for i in range(2):
                        v.tensor_tensor(out=table_bias[:, i, :].rearrange("p (h d) -> p h d", d=D),
                                        in0=bank[2][:, i * F:(i + 1) * F].rearrange("p (h d) -> p h d", d=D),
                                        in1=rb_c[:, i, :].unsqueeze(1).to_broadcast([P, H, D]), op=ALU.add).then_inc(s_wb, 1)
                    v.tensor_copy(out=z_beta_w[:], in_=bank[2][:, 2 * F:3 * F]).then_inc(s_wb, 1)

                    dve.wait_ge(s_idx, 16 * idx_loads[0])
                    for rows_f, rows_i in ((src_f, src_i), (dst_f, dst_i)):
                        v.tensor_copy(out=rows_f[:, 0:KB, :], in_=rows_i[:, 0:KB, :]).then_inc(s_conv, 1)
                        v.tensor_copy(out=rows_f[0:KR + TILES, KB, :], in_=rows_i[0:KR + TILES, KB, :]).then_inc(s_conv, 1)
                    v.tensor_copy(out=last_f[:], in_=last_i[:]).then_inc(s_stepv, 1)
                    v.tensor_copy(out=iota_s[:], in_=iota_i[:]).then_inc(s_wb, 1)
                    v.tensor_copy(out=iota_n[:], in_=iota_i[:, 0:P]).then_inc(s_wb, 1)
                    link(v.tensor_copy(out=iota_p[:], in_=iota_pi[:]))
                    link(v.tensor_scalar(out=thr[:], in0=iota_p[:], scalar1=1.0, scalar2=float(P), op0=ALU.add, op1=ALU.mult))
                    dve.wait_ge(s_step, 1)
                    link(v.tensor_scalar(out=below[:], in0=bank[3][:, 0:GROUPS - 1], scalar1=thr[:, 0:1], scalar2=None, op0=ALU.is_lt))
                    link(v.tensor_reduce(out=g_of[:], in_=below[:], axis=AX.X, op=ALU.add))
                    link(v.tensor_scalar(out=s_of[:], in0=g_of[:], scalar1=iota_p[:, 0:1], scalar2=1.0, op0=ALU.add, op1=ALU.add))
                    v.tensor_scalar(out=passed[:], in0=iota_s[:], scalar1=s_of[:, 0:1], scalar2=None, op0=ALU.is_ge).then_inc(s_stepv, 1)
                    link(v.memset(blk[:, 0:1], -1.0))
                    link(v.memset(grp[:, 0:1], -1.0))
                    dve.wait_ge(s_step, 2)
                    link(v.tensor_copy(out=blk[:, 1:STEPS + 1], in_=bank[4][:, 0:STEPS]))
                    link(v.tensor_tensor(out=grp[:, 1:STEPS + 1], in0=iota_s[:], in1=blk[:, 1:STEPS + 1], op=ALU.subtract))
                    link(v.tensor_scalar(out=step_cols[:, :, 0], in0=blk[:, 1:STEPS + 1], scalar1=float(P), scalar2=None, op0=ALU.mult))
                    link(v.tensor_scalar(out=step_cols[:, :, 1], in0=step_cols[:, :, 0], scalar1=iota_p[:, 0:1], scalar2=-1.0,
                                         op0=ALU.add, op1=ALU.mult))
                    link(v.tensor_tensor(out=step_cols[:, :, 2], in0=blk[:, 1:STEPS + 1], in1=blk[:, 0:STEPS], op=ALU.is_equal))
                    link(v.tensor_tensor(out=step_cols[:, :, 3], in0=grp[:, 1:STEPS + 1], in1=grp[:, 0:STEPS], op=ALU.is_equal))
                    link(v.tensor_scalar(out=off_f[:], in0=grp[0:1, 1:STEPS + 1], scalar1=float(GE), scalar2=float(TAIL0),
                                         op0=ALU.mult, op1=ALU.min))
                    link(v.tensor_tensor(out=off_f[:], in0=off_f[:], in1=blk[0:1, 1:STEPS + 1], op=ALU.add))
                    link(v.tensor_copy(out=step_ints[:], in_=off_f[:]))

                    for k in range(KB + 1):
                        n = P if k < KB else KR + TILES
                        dve.wait_ge(s_it, k + 1)
                        v.tensor_copy(out=cols[:].bitcast(i32)[:, k * 32:k * 32 + n // TILES, 0:TILES],
                                      in_=bank[5 + k % 2][:, 0:n].rearrange("p (g j) -> p g j", j=TILES)).then_inc(s_ic_s, 1)
                    dve.wait_ge(s_ic_d, KB + 1)
                    for j in range(DUP // P):
                        link(v.memset(cols[:, GROUPS - 1, TILES + j:TILES + j + 1], 1.0e6))
                    link(v.memset(cols[0:DUP % P, GROUPS - 1, TILES + DUP // P:TILES + DUP // P + 1], 1.0e6))

                @block.scalar
                def _(act):
                    nc.scalar.preload_act_table_set("natural_log_exp_and_others")
                    act.wait_ge(s_tp, 1)
                    nc.scalar.activation(w_ct[:].rearrange("p i n -> p (i n)"), bank[0][:], ACT.Copy).then_inc(s_tc, 1)
                    for k in range(KB + 1):
                        n = P if k < KB else KR + TILES
                        act.wait_ge(s_it, k + 1)
                        nc.scalar.activation(cols[:, k * 32:k * 32 + n // TILES, TILES:2 * TILES],
                                             bank[7 * (k % 2)][:, 0:n].rearrange("p (g j) -> p g j", j=TILES),
                                             ACT.Copy, scale=-1.0).then_inc(s_ic_d, 1)

                @block.tensor
                def _(pe):
                    pe.wait_ge(s_const, CONSTS)
                    pe.wait_ge(s_chain, 3)
                    for i in range(4):
                        last = nc.tensor.transpose(bank[0][:, i * F:(i + 1) * F], w_c[:, 1 + i, :], ident[:])
                    last.then_inc(s_tp, 1)
                    pe.wait_ge(s_tc, 1)
                    pe.wait_ge(s_chain, 3 + 3 + 12 + 3)
                    for i, m in enumerate((1, 3, 0, 2)):
                        last = nc.tensor.matmul(bank[1][:, i * F:(i + 1) * F], w_ct[:, i, :], bdg[:, m, :], start=True, stop=True)
                    last.then_inc(s_u, 1)
                    for i in range(2):
                        nc.tensor.matmul(bank[2][:, i * F:(i + 1) * F], colb[:, 2 * i, :], bd[:, 2 * i, :], start=True, stop=False)
                        nc.tensor.matmul(bank[2][:, i * F:(i + 1) * F], colb[:, 2 * i + 1, :], bd[:, 2 * i + 1, :], start=False, stop=True)
                    nc.tensor.matmul(bank[2][:, 2 * F:3 * F], colb[:, 4, :], zbd[:], start=True, stop=True).then_inc(s_u, 1)
                    pe.wait_ge(s_stepv, 1)
                    nc.tensor.matmul(bank[3][:, 0:GROUPS - 1], ones[0:1, :], last_f[:], start=True, stop=True).then_inc(s_step, 1)
                    pe.wait_ge(s_stepv, 2)
                    nc.tensor.matmul(bank[4][:, 0:STEPS], ones[0:BLOCKS - 1, :], passed[0:BLOCKS - 1, :], start=True, stop=True).then_inc(s_step, 1)
                    pe.wait_ge(s_conv, 4)
                    for k in range(KB + 1):
                        n = P if k < KB else KR + TILES
                        if k >= 2:
                            pe.wait_ge(s_ic_s, k - 1)
                            pe.wait_ge(s_ic_d, k - 1)
                        nc.tensor.transpose(bank[5 + k % 2][:, 0:n], src_f[0:n, k, :], ident[0:n, 0:n])
                        nc.tensor.transpose(bank[7 * (k % 2)][:, 0:n], dst_f[0:n, k, :], ident[0:n, 0:n]).then_inc(s_it, 1)

        q_split = sb_mid("q_split", [P, BLOCKS, 3 * QW], bf16)
        nodes(nc, a, sem, bank, dict(table=table, ident=ident, w_node=w_node, table_bias=table_bias, gq4=gq4, bq4=bq4,
                                     gqb=gqb, bqb=bqb, eps_c=eps_c, q_split=q_split))
        edges(nc, a, sem, banks, dict(table=table, sums_d=sums_d, qk_d=qk_d, ident=ident, iota_n=iota_n, w_edge=w_edge,
                                      cols=cols, step_cols=step_cols, step_ints=step_ints, eps_c=eps_c, q_split=q_split))
        mid.close()
        softmax(nc, a, sem, bank, dict(qk_d=qk_d, lse_d=lse_d, ident=ident, one_c=one_c))
        finish(nc, a, sem, bank, dict(sums_d=sums_d, lse_d=lse_d, ident=ident, z_w=z_w, z_beta_w=z_beta_w,
                                      rows16=rows16, eps_c=eps_c), out)


def nodes(nc, a, sem, bank, t):
    f32, bf16 = mybir.dt.float32, mybir.dt.bfloat16
    ALU, ACT, AX = mybir.AluOpType, mybir.ActivationFunctionType, mybir.AxisListType
    with ExitStack() as scope:
        def sb(name, shape, dt=f32):
            return scope.enter_context(nc.sbuf_tensor(name, shape, dt))

        xb = sb("n_x", [P, 2, 2, F])
        xt = sb("n_xt", [P, 2, F])
        sq = sb("n_sq", [P, 2, 3 * F])
        var = sb("n_var", [P, 2, 3 * H])
        lnv = sb("n_lnv", [P, 2, 3 * H])
        rstd = sb("n_rstd", [P, 2, 3 * H])
        tb = sb("n_tb", [P, 2, 2, 2, F])
        yh = sb("n_yh", [P, 2, F])
        q = sb("n_q", [P, 2, QW])
        qt = sb("n_qt", [P, 2, F])
        q1 = sb("n_q1", [P, 2, QW])
        q2 = sb("n_q2", [P, 2, QW])
        s_x = [sem(f"nodes_x{i}") for i in range(2)]
        s_st = [sem(f"nodes_stored{i}") for i in range(2)]
        s_xt, s_xc, s_pr, s_sq, s_var, s_ln, s_r = (sem("nodes_xT"), sem("nodes_xT_copied"), sem("nodes_projected"),
                                                    sem("nodes_squared"), sem("nodes_var"), sem("nodes_ln"), sem("nodes_rstd"))
        s_u, s_tb, s_yh, s_qg0, s_qg, s_t, s_qb0, s_q = (sem("nodes_scaled"), sem("nodes_table"), sem("nodes_yh"), sem("nodes_qg0"),
                                                         sem("nodes_qg"), sem("nodes_qt"), sem("nodes_qb0"), sem("nodes_q"))
        s_1, s_r1, s_2, s_r2, s_3, s_z = (sem("nodes_part1"), sem("nodes_rest1"), sem("nodes_part2"), sem("nodes_rest2"),
                                          sem("nodes_part3"), sem("nodes_zeroed"))
        q_split, table = t["q_split"], t["table"]
        PAIRS = BLOCKS // 2
        ITER = PAIRS // 2

        assert PAIRS % 2 == 0 and BLOCKS % 2 == 1

        with nc.Block() as block:
            @block.sync
            def _(sp):
                def load(k, slot, b, nb, rows):
                    sp.dma_start(xb[0:rows, slot, 0:nb, :],
                                 a["x"][bass.ds(P * b, nb * rows), :].rearrange("(b p) f -> p b f", p=rows)).then_inc(s_x[slot], 16)

                def body(k, i, slot, b, nb, rows):
                    n = k + 2 * i
                    sp.wait_ge(s_xt, n + 1)
                    sp.wait_ge(s_tb, n + 1)
                    sp.dma_start(table[bass.ds(P * b, nb * rows), :].rearrange("(b p) f -> p b f", p=rows),
                                 tb[0:rows, slot, 0:nb, :, :].rearrange("p b t f -> p b (t f)")).then_inc(s_st[slot], 16)

                load(0, 0, 0, 2, P)
                load(1, 1, 2, 2, P)
                with sp.Fori(0, ITER - 1) as i:
                    for u in range(2):
                        body(u, i, u, 4 * i + 2 * u, 2, P)
                        load(0, u, 4 * i + 2 * u + 4, 2, P)
                for u in range(2):
                    body(2 * (ITER - 1) + u, 0, u, 4 * (ITER - 1) + 2 * u, 2, P)
                    if u == 0:
                        load(0, 0, BLOCKS - 1, 1, LAST)
                body(PAIRS, 0, 0, BLOCKS - 1, 1, LAST)
                sp.wait_ge(s_st[0], 16 * (PAIRS // 2 + 1))
                sp.wait_ge(s_st[1], 16 * (PAIRS // 2))

            @block.tensor
            def _(pe):
                def body(k, i, slot, b, nb, rows):
                    n = k + 2 * i
                    tail = k == PAIRS
                    pe.wait_ge(s_x[slot], 16 * (i + 1) if not tail else 16 * (PAIRS // 2 + 1))
                    pe.wait_ge(s_xc, n)
                    for c in range(nb):
                        last = nc.tensor.transpose(bank[6][:, c * F:c * F + rows], xb[0:rows, slot, c, :], t["ident"][0:rows, 0:rows])
                    last.then_inc(s_xt, 1)
                    pe.wait_ge(s_xc, n + 1)
                    pe.wait_ge(s_u, n)
                    pe.wait_ge(s_yh, n)
                    for c in range(nb):
                        nc.tensor.matmul(bank[c][0:rows, :], xt[:, c, 0:rows], t["w_node"][:, 0:4 * F], start=True, stop=True)
                        last = nc.tensor.matmul(bank[2][0:rows, c * F:(c + 1) * F], xt[:, c, 0:rows], t["w_node"][:, 4 * F:5 * F],
                                                start=True, stop=True)
                    last.then_inc(s_pr, 1)
                each_first(pe, body, ITER, PAIRS)

            @block.scalar
            def _(act):
                def body(k, i, slot, b, nb, rows):
                    n = k + 2 * i
                    act.wait_ge(s_xt, n + 1)
                    act.wait_ge(s_pr, n)
                    nc.scalar.activation(xt[:, 0:nb, 0:rows], bank[6][:, 0:nb * F].rearrange("p (c n) -> p c n", c=nb)[:, :, 0:rows],
                                         ACT.Copy).then_inc(s_xc, 1)
                    act.wait_ge(s_pr, n + 1)
                    for c in range(nb):
                        last = nc.scalar.activation(sq[0:rows, c, :], bank[c][0:rows, 0:3 * F], ACT.Square)
                    last.then_inc(s_sq, 1)
                    act.wait_ge(s_var, n + 1)
                    nc.scalar.activation(lnv[0:rows, 0:nb, :], var[0:rows, 0:nb, :], ACT.Ln, bias=t["eps_c"][0:rows, 0:1], scale=1.0 / D).then_inc(s_ln, 1)
                    act.wait_ge(s_ln, n + 1)
                    nc.scalar.activation(rstd[0:rows, 0:nb, :], lnv[0:rows, 0:nb, :], ACT.Exp, scale=-0.5).then_inc(s_r, 1)
                    qs = q_split[0:rows, bass.ds(b, nb), :]
                    act.wait_ge(s_z, 1)
                    act.wait_ge(s_qg, n + 1)
                    act.wait_ge(s_q, n + 1)
                    nc.scalar.activation(qs[:, :, 0:QW], q[0:rows, 0:nb, :], ACT.Copy).then_inc(s_1, 1)
                    act.wait_ge(s_r1, n + 1)
                    nc.scalar.activation(qs[:, :, QW:2 * QW], q1[0:rows, 0:nb, :], ACT.Copy).then_inc(s_2, 1)
                    act.wait_ge(s_r2, n + 1)
                    nc.scalar.activation(qs[:, :, 2 * QW:3 * QW], q2[0:rows, 0:nb, :], ACT.Copy).then_inc(s_3, 1)
                each_first(act, body, ITER, PAIRS)

            @block.gpsimd
            def _(pool):
                def body(k, i, slot, b, nb, rows):
                    n = k + 2 * i
                    pool.wait_ge(s_u, n + 1)
                    nc.gpsimd.tensor_tensor(out=tb[0:rows, slot, 0:nb, :, :], in0=tb[0:rows, slot, 0:nb, :, :],
                                            in1=t["table_bias"][0:rows].unsqueeze(1).to_broadcast([rows, nb, 2, F]), op=ALU.add).then_inc(s_tb, 1)
                each_first(pool, body, ITER, PAIRS)

            @block.vector
            def _(dve):
                v = nc.vector
                v.memset(q_split[:, BLOCKS - 1, :], 0.0).then_inc(s_z, 1)

                def body(k, i, slot, b, nb, rows):
                    n = k + 2 * i
                    tail = k == PAIRS
                    h3 = lambda ap: ap.rearrange("p (h d) -> p h d", d=D)
                    dve.wait_ge(s_sq, n + 1)
                    v.tensor_reduce(out=var[0:rows, 0:nb, :], in_=sq[0:rows, 0:nb, :].rearrange("p b (h d) -> p b h d", d=D),
                                    axis=AX.X, op=ALU.add).then_inc(s_var, 1)
                    dve.wait_ge(s_r, n + 1)
                    if tail:
                        dve.wait_ge(s_st[slot], 16 * (PAIRS // 2))
                    else:
                        dve.wait_ge(s_st[slot], 16 * i)
                    for c in range(nb):
                        v.tensor_tensor(out=h3(tb[0:rows, slot, c, 0, :]), in0=h3(bank[c][0:rows, 3 * F:4 * F]),
                                        in1=rstd[0:rows, c, H:2 * H].unsqueeze(2).to_broadcast([rows, H, D]), op=ALU.mult)
                        last = v.tensor_tensor(out=h3(tb[0:rows, slot, c, 1, :]), in0=h3(bank[2][0:rows, c * F:(c + 1) * F]),
                                               in1=rstd[0:rows, c, 2 * H:3 * H].unsqueeze(2).to_broadcast([rows, H, D]), op=ALU.mult)
                    last.then_inc(s_u, 1)
                    for c in range(nb):
                        last = v.tensor_tensor(out=h3(yh[0:rows, c, :]), in0=h3(bank[c][0:rows, 0:F]),
                                               in1=rstd[0:rows, c, 0:H].unsqueeze(2).to_broadcast([rows, H, D]), op=ALU.mult)
                    last.then_inc(s_yh, 1)
                    dve.wait_ge(s_yh, n + 1)
                    rep = lambda tt: tt[0:rows, :].unsqueeze(1).to_broadcast([rows, nb, F])
                    v.tensor_tensor(out=qt[0:rows, 0:nb, :], in0=yh[0:rows, 0:nb, :], in1=rep(t["gqb"]), op=ALU.mult).then_inc(s_t, 1)
                    dve.wait_ge(s_3, n)
                    v.tensor_tensor(out=q[0:rows, 0:nb, 0:F], in0=yh[0:rows, 0:nb, :], in1=rep(t["gq4"]), op=ALU.mult).then_inc(s_qg0, 1)
                    dve.wait_ge(s_t, n + 1)
                    v.tensor_reduce(out=q[0:rows, 0:nb, F:QW], in_=qt[0:rows, 0:nb, :].rearrange("p b (h d) -> p b h d", d=D),
                                    axis=AX.X, op=ALU.add).then_inc(s_qb0, 1)
                    dve.wait_ge(s_qg0, n + 1)
                    v.tensor_tensor(out=q[0:rows, 0:nb, 0:F], in0=q[0:rows, 0:nb, 0:F], in1=rep(t["bq4"]), op=ALU.add).then_inc(s_qg, 1)
                    dve.wait_ge(s_qb0, n + 1)
                    v.tensor_tensor(out=q[0:rows, 0:nb, F:QW], in0=q[0:rows, 0:nb, F:QW],
                                    in1=t["bqb"][0:rows, :].unsqueeze(1).to_broadcast([rows, nb, H]), op=ALU.add).then_inc(s_q, 1)
                    dve.wait_ge(s_q, n + 1)
                    dve.wait_ge(s_qg, n + 1)
                    qs = q_split[0:rows, bass.ds(b, nb), :]
                    dve.wait_ge(s_1, n + 1)
                    v.tensor_tensor(out=q1[0:rows, 0:nb, :], in0=q[0:rows, 0:nb, :], in1=qs[:, :, 0:QW], op=ALU.subtract).then_inc(s_r1, 1)
                    dve.wait_ge(s_r1, n + 1)
                    dve.wait_ge(s_2, n + 1)
                    v.tensor_tensor(out=q2[0:rows, 0:nb, :], in0=q1[0:rows, 0:nb, :], in1=qs[:, :, QW:2 * QW], op=ALU.subtract).then_inc(s_r2, 1)
                each_first(dve, body, ITER, PAIRS)


def each_first(eng, body, iters, pairs):
    for u in range(2):
        body(u, 0, u, 2 * u, 2, P)
    with eng.Fori(1, iters) as i:
        for u in range(2):
            body(u, i, u, 4 * i + 2 * u, 2, P)
    body(pairs, 0, pairs % 2, BLOCKS - 1, 1, LAST)


def edges(nc, a, sem, banks, t):
    f32, bf16, i32, u32 = mybir.dt.float32, mybir.dt.bfloat16, mybir.dt.int32, mybir.dt.uint32
    ALU, ACT, AX = mybir.AluOpType, mybir.ActivationFunctionType, mybir.AxisListType
    table, sums_d, qk_d, ident, step_cols = t["table"], t["sums_d"], t["qk_d"], t["ident"], t["step_cols"]
    with ExitStack() as scope:
        def sb(name, shape, dt=f32):
            return scope.enter_context(nc.sbuf_tensor(name, shape, dt))

        ea = sb("e_ea", [P, RING, TILES, F])
        dstb = sb("e_dstb", [P, RING, GE], i32)
        qb = sb("e_q", [P, RING, 3 * QW], bf16)
        gcol = sb("e_gcol", [P, RING, 2 * TILES])
        eat = sb("e_eat", [P, RING, GE])
        ysq = sb("e_ysq", [P, 2, TILES, 2 * F])
        yvar = sb("e_yvar", [P, TILES, 2 * H])
        yln = sb("e_yln", [P, TILES, 2 * H])
        yr = sb("e_yr", [P, 2, TILES, 2 * H])
        p = sb("e_p", [P, RING, TILES, 2 * F])
        z = sb("e_z", [P, 2, TILES, 3 * F])
        zs = sb("e_zs", [P, TILES, 3 * H])
        zln = sb("e_zln", [P, TILES, 2 * H])
        zr = sb("e_zr", [P, 2, TILES, 2 * H])
        qk0 = sb("e_qk0", [P, TILES, H])
        w2 = sb("e_w2", [P, TILES, H])
        hh = sb("e_h", [P, 2, TILES, AW])
        zero_c = sb("e_zero", [P, 1])
        ob = sb("e_ob", [P, 2, 1])
        oht_a = sb("e_oht_a", [P, GE])
        oht = sb("e_oht", [P, 2, GE], bf16)
        rel = sb("e_rel", [P, 2, TILES])
        oh_a = sb("e_oh_a", [P, TILES, P])
        oh = sb("e_oh", [P, 3, TILES, P])
        run = sb("e_run", [P, RING, AW])
        qkr = sb("e_qkr", [P, RING, TILES * H])
        qkt = sb("e_qkt", [TILES * H, RING, P])
        y_ps, u_ps = [banks[:, h, :] for h in range(2)], [banks[:, 2 + h, :] for h in range(2)]
        eat_ps, qx_ps, agg_ps = banks[:, 4, :], banks[:, 5:7, 0:2 * QW], banks[:, 7, 0:AW]
        qkt_ps = banks[0:TILES * H, 7, AW:AW + P]
        qx4 = qx_ps.rearrange("p b (t c) -> p b t c", c=QW)
        tiles4 = lambda ap: ap.rearrange("p (b t) c -> p b t c", b=2)

        s_ea = [sem(f"ea_loaded{i}") for i in range(RING)]
        s_in = [sem(f"cols_q_dst_loaded{i}") for i in range(RING)]
        s_ga = [sem(f"gathered{i}") for i in range(RING)]
        s_sums_st, s_qk_st = sem("sums_stored"), sem("qk_stored")
        s_tr, s_eat = sem("ea_transposed"), sem("eat_copied")
        s_y = [sem(f"y_projected{i}") for i in range(2)]
        s_ysq = [sem(f"y_squared{i}") for i in range(2)]
        s_u = [sem(f"u_projected{i}") for i in range(2)]
        s_p = [sem(f"p_scaled{i}") for i in range(2)]
        s_yv, s_yl, s_yr = sem("y_summed"), sem("y_ln"), sem("y_rstd")
        s_psq, s_pq, s_z, s_zl, s_zr = sem("p_squared"), sem("pq_ready"), sem("z_summed"), sem("z_ln"), sem("z_rstd")
        s_qk0, s_qk, s_w2, s_qkr = sem("qk_dot"), sem("qk_ready"), sem("w2_ready"), sem("qk_run_ready")
        s_h1, s_h2, s_agg, s_run = sem("h1_ready"), sem("h2_ready"), sem("summed_to_nodes"), sem("run_ready")
        s_qkt, s_qktc = sem("qk_transposed"), sem("qkt_copied")
        s_ob, s_oha, s_oht, s_qx = sem("oht_bias"), sem("oht_abs"), sem("oht_ready"), sem("q_expanded")
        s_rel, s_ohb, s_oh, s_init = sem("rel_ready"), sem("oh_abs"), sem("oh_ready"), sem("edges_init")

        def every(eng, body, last):
            for c in range(PEEL):
                body(c, 0, False)
            turns = (STEPS - 1 - PEEL) // UNROLL
            with eng.Fori(0, turns) as i:
                for u in range(UNROLL):
                    body(PEEL + u, i, True)
            for c in range(PEEL + UNROLL * turns, last):
                body(c, 0, False)

        def use(x, i):
            return i + (x // RING + 1)

        def is_step(x, loop):
            return loop or 0 <= x < STEPS

        with nc.Block() as block:
            @block.sync
            def _(sp):
                r_b, r_e0, r_g, r_n1, r_16n = (sp.alloc_register(f"sp_{name}") for name in ("block", "edge", "group", "n1", "n16"))

                def entry(n, edge):
                    bounded = lambda reg, top: sp.snap(reg, min_val=0, max_val=top)
                    v = sp.value_load(t["step_ints"][0:1, bass.ds(n, 1)], min_val=0, max_val=TAIL0 + 63)
                    sp.reg_alu(r_b, v, 63, ALU.bitwise_and)
                    sp.reg_alu(r_g, v, GE - 64, ALU.add)
                    sp.reg_alu(r_g, r_g, 9, ALU.logical_shift_right)
                    if edge:
                        sp.reg_alu(r_e0, v, r_b, ALU.subtract)
                    return bounded(r_b, BLOCKS - 1), bounded(r_g, GROUPS - 1), bounded(r_e0, TAIL0) if edge else None

                def body(c, i, loop):
                    if is_step(c, loop):
                        n, k = UNROLL * i + c, c % RING
                        again = loop or c >= RING
                        b, g, e0 = entry(n, True)
                        if again:
                            sp.wait_ge(s_tr, n - RING + 1)
                        sp.dma_start(ea[:, k, :, :],
                                     a["edge_attr_128"][bass.ds(e0, GE), :].rearrange("(j p) f -> p j f", p=P)).then_inc(s_ea[k], 16)
                        if again:
                            sp.wait_ge(s_ga[k], 64 * use(c - RING, i))
                            sp.wait_ge(s_rel, n - RING + 1)
                        sp.dma_start(gcol[:, k, :], t["cols"][:, bass.ds(g, 1), :].rearrange("p o c -> p (o c)")).then_inc(s_in[k], 16)
                        if again:
                            sp.wait_ge(s_qx, n - RING + 1)
                        sp.dma_start(qb[:, k, :], t["q_split"][:, bass.ds(b, 1), :].rearrange("p o c -> p (o c)")).then_inc(s_in[k], 16)
                        sp.dma_start(dstb[:, k, :], a["dst"][bass.ds(e0, GE)].partition_broadcast(P)).then_inc(s_in[k], 16)
                    x = c - STORE_LAG
                    if is_step(x, loop):
                        n, k = UNROLL * i + x, x % RING
                        b, g, _ = entry(n, False)
                        if loop:
                            sp.reg_alu(r_n1, n, 1, ALU.add)
                            sp.reg_alu(r_16n, n, 16, ALU.mult)
                        sp.wait_ge(s_sums_st, r_16n if loop else 16 * n)
                        sp.wait_ge(s_run, r_n1 if loop else n + 1)
                        sp.dma_start(sums_d[bass.ds(b, 1), :, :].rearrange("o p c -> p (o c)"), run[:, k, :]).then_inc(s_sums_st, 16)
                        sp.wait_ge(s_qk_st, r_16n if loop else 16 * n)
                        sp.wait_ge(s_qktc, r_n1 if loop else n + 1)
                        sp.dma_start(qk_d[bass.ds(g, 1), :, :].rearrange("o r e -> r (o e)"), qkt[:, k, :]).then_inc(s_qk_st, 16)
                every(sp, body, STEPS + STORE_LAG)
                sp.wait_ge(s_sums_st, 16 * STEPS)
                sp.wait_ge(s_qk_st, 16 * STEPS)

            @block.tensor
            def _(pe):
                def project(x, i, loop, cols, out_ps, s_out, s_used):
                    n = UNROLL * i + x
                    for half in range(2):
                        if loop or x >= 1:
                            pe.wait_ge(s_used[half], n)
                        for k in range(2):
                            last = nc.tensor.matmul(out_ps[half][:, k * 2 * F:(k + 1) * 2 * F], eat[:, x % RING, (2 * half + k) * P:(2 * half + k + 1) * P],
                                                    t["w_edge"][:, cols], start=True, stop=True)
                        last.then_inc(s_out[half], 1)

                def body(c, i, loop):
                    if is_step(c - 1, loop):
                        pe.wait_ge(s_eat, UNROLL * i + c)
                        project(c - 1, i, loop, slice(0, 2 * F), y_ps, s_y, s_ysq)
                    x = c - 7
                    if is_step(x, loop):
                        n = UNROLL * i + x
                        pe.wait_ge(s_h1, n + 1)
                        pe.wait_ge(s_h2, n + 1)
                        pe.wait_ge(s_oh, n + 1)
                        if loop or x >= 1:
                            pe.wait_ge(s_qktc, n)
                        for j in range(TILES):
                            last = nc.tensor.matmul(agg_ps, oh[:, x % 3, j, :], hh[:, x % 2, j, :], start=(j == 0), stop=(j == TILES - 1))
                        last.then_inc(s_agg, 1)
                    if is_step(c - 3, loop):
                        project(c - 3, i, loop, slice(2 * F, 4 * F), u_ps, s_u, s_p)
                    x = c - 5
                    if is_step(x, loop):
                        n, k = UNROLL * i + x, x % RING
                        pe.wait_ge(s_oht, n + 1)
                        pe.wait_ge(s_in[k], 48 * use(x, i))
                        if loop or x >= 1:
                            pe.wait_ge(s_qk, n)
                        for j in range(TILES):
                            for part in range(3):
                                last = nc.tensor.matmul(qx4[:, j // 2, j % 2, :], oht[:, x % 2, j * P:(j + 1) * P],
                                                        qb[:, k, part * QW:(part + 1) * QW], start=(part == 0), stop=(part == 2))
                        last.then_inc(s_qx, 1)
                    if is_step(c, loop):
                        n, k = UNROLL * i + c, c % RING
                        pe.wait_ge(s_ea[k], 16 * use(c, i))
                        if loop or c >= 1:
                            pe.wait_ge(s_eat, n)
                        for j in range(TILES):
                            last = nc.tensor.transpose(eat_ps[:, j * P:(j + 1) * P], ea[:, k, j, :], ident[:])
                        last.then_inc(s_tr, 1)
                    x = c - 7
                    if is_step(x, loop):
                        n = UNROLL * i + x
                        pe.wait_ge(s_qkr, n + 1)
                        pe.wait_ge(s_run, n + 1)
                        nc.tensor.transpose(qkt_ps, qkr[:, x % RING, :], ident[:]).then_inc(s_qkt, 1)
                every(pe, body, STEPS + 7)

            @block.scalar
            def _(act):
                def body(c, i, loop):
                    x = c - 8
                    if is_step(x, loop):
                        n = UNROLL * i + x
                        act.wait_ge(s_qkt, n + 1)
                        if loop or x >= RING:
                            act.wait_ge(s_qk_st, 16 * (n - RING + 1))
                        nc.scalar.activation(qkt[:, x % RING, :], qkt_ps, ACT.Copy).then_inc(s_qktc, 1)
                    x = c - 6
                    if is_step(x, loop):
                        n = UNROLL * i + x
                        act.wait_ge(s_z, n + 1)
                        nc.scalar.activation(zln[:], zs[:, :, 0:2 * H], ACT.Ln, bias=t["eps_c"][:, 0:1], scale=1.0 / D).then_inc(s_zl, 1)
                        act.wait_ge(s_zl, n + 1)
                        if loop or x >= 2:
                            act.wait_ge(s_w2, n - 1)
                            act.wait_ge(s_h1, n - 1)
                        nc.scalar.activation(zr[:, x % 2, :, :], zln[:], ACT.Exp, scale=-0.5).then_inc(s_zr, 1)
                    x = c - 1
                    if is_step(x, loop):
                        n = UNROLL * i + x
                        for half in range(2):
                            act.wait_ge(s_y[half], n + 1)
                            if half == 0 and (loop or x >= 2):
                                act.wait_ge(s_yv, n - 1)
                            nc.scalar.activation(ysq[:, x % 2, 2 * half:2 * half + 2, :].rearrange("p t c -> p (t c)"), y_ps[half],
                                                 ACT.Square).then_inc(s_ysq[half], 1)
                    x = c - 4
                    if is_step(x, loop):
                        n, k = UNROLL * i + x, x % RING
                        act.wait_ge(s_in[k], 48 * use(x, i))
                        act.wait_ge(s_ob, n + 1)
                        if loop or x >= 1:
                            act.wait_ge(s_oht, n)
                        nc.scalar.activation(oht_a[:], dstb[:, k, :], ACT.Abs, bias=ob[:, x % 2, :]).then_inc(s_oha, 1)
                        act.wait_ge(s_oha, n + 1)
                        if loop or x >= 2:
                            act.wait_ge(s_qx, n - 1)
                        nc.scalar.activation(oht[:, x % 2, :], oht_a[:], ACT.Relu, bias=1.0, scale=-1.0).then_inc(s_oht, 1)
                    x = c - 2
                    if is_step(x, loop):
                        n = UNROLL * i + x
                        act.wait_ge(s_yv, n + 1)
                        nc.scalar.activation(yln[:], yvar[:], ACT.Ln, bias=t["eps_c"][:, 0:1], scale=1.0 / D).then_inc(s_yl, 1)
                        act.wait_ge(s_yl, n + 1)
                        if loop or x >= 2:
                            act.wait_ge(s_p[1], n - 1)
                        nc.scalar.activation(yr[:, x % 2, :, :], yln[:], ACT.Exp, scale=-0.5).then_inc(s_yr, 1)
                    x = c - 5
                    if is_step(x, loop):
                        n, k = UNROLL * i + x, x % RING
                        act.wait_ge(s_ga[k], 64 * use(x, i))
                        if loop or x >= 2:
                            act.wait_ge(s_z, n - 1)
                        nc.scalar.activation(z[:, x % 2, :, 0:2 * F], p[:, k, :, :], ACT.Square).then_inc(s_psq, 1)
                        act.wait_ge(s_rel, n + 1)
                        if loop or x >= 1:
                            act.wait_ge(s_oh, n)
                        for j in range(TILES):
                            nc.scalar.activation(oh_a[:, j, :], t["iota_n"][:], ACT.Abs, bias=rel[:, x % 2, j:j + 1]).then_inc(s_ohb, 1)
                        act.wait_ge(s_ohb, TILES * (n + 1))
                        if loop or x >= 3:
                            act.wait_ge(s_agg, n - 2)
                        nc.scalar.activation(oh[:, x % 3, :, :], oh_a[:], ACT.Relu, bias=1.0, scale=-1.0).then_inc(s_oh, 1)
                    if is_step(c, loop):
                        n = UNROLL * i + c
                        act.wait_ge(s_tr, n + 1)
                        if loop or c >= RING:
                            act.wait_ge(s_u[1], n - RING + 1)
                        nc.scalar.activation(eat[:, c % RING, :], eat_ps, ACT.Copy).then_inc(s_eat, 1)
                every(act, body, STEPS + 8)

            @block.gpsimd
            def _(pool):
                last_node = pool.alloc_register("last_node")
                nodes_less_2 = pool.to_reg(N - 2)

                def gather(half, x, i):
                    k = x % RING
                    pool.wait_ge(s_p[half], UNROLL * i + x + 1)
                    pool.reg_add(last_node, nodes_less_2, 1)
                    for j in (2 * half, 2 * half + 1):
                        pool.indirect_dma_start(out=p[:, k, j, :], out_offset=None, in_=table,
                                                in_offset=bass.IndirectOffsetOnAxis(ap=gcol[:, k, j:j + 1].bitcast(u32), axis=0),
                                                bounds_check=last_node, oob_is_err=True, compute_op=ALU.add).then_inc(s_ga[k], 16)

                def body(c, i, loop):
                    x = c - 4
                    if is_step(x, loop):
                        pool.wait_ge(s_in[x % RING], 48 * use(x, i))
                        gather(0, x, i)
                    x = c - 6
                    if is_step(x, loop):
                        n, k = UNROLL * i + x, x % RING
                        pool.wait_ge(s_ga[k], 64 * use(x, i))
                        pool.wait_ge(s_zr, n + 1)
                        if loop or x >= 2:
                            pool.wait_ge(s_agg, n - 1)
                        nc.gpsimd.tensor_tensor(out=hh[:, x % 2, :, 0:F].rearrange("p t (h d) -> p t h d", d=D),
                                                in0=p[:, k, :, F:2 * F].rearrange("p t (h d) -> p t h d", d=D),
                                                in1=zr[:, x % 2, :, H:2 * H].unsqueeze(3).to_broadcast([P, TILES, H, D]), op=ALU.mult).then_inc(s_h1, 1)
                    if is_step(c - 4, loop):
                        gather(1, c - 4, i)
                every(pool, body, STEPS + 6)

            @block.vector
            def _(dve):
                v = nc.vector
                heads = lambda ap: ap.rearrange("p t (h d) -> p t h d", d=D)
                v.memset(hh[:, :, :, AW - 1:AW], 1.0).then_inc(s_init, 1)
                v.memset(run[:, RING - 1, :], 0.0).then_inc(s_init, 1)
                v.memset(qkr[:, RING - 1, :], 0.0).then_inc(s_init, 1)
                v.memset(zero_c[:], 0.0).then_inc(s_init, 1)
                dve.wait_ge(s_init, 4)

                def step_col(n, k):
                    return step_cols[:, bass.ds(n, 1), k]

                def body(c, i, loop):
                    x = c - 2
                    if is_step(x, loop):
                        n = UNROLL * i + x
                        dve.wait_ge(s_ysq[0], n + 1)
                        dve.wait_ge(s_ysq[1], n + 1)
                        if loop or x >= 1:
                            dve.wait_ge(s_yl, n)
                        v.tensor_reduce(out=yvar[:], in_=heads(ysq[:, x % 2, :, :]), axis=AX.X, op=ALU.add).then_inc(s_yv, 1)
                    x = c - 6
                    if is_step(x, loop):
                        n = UNROLL * i + x
                        h = hh[:, x % 2, :, :]
                        dve.wait_ge(s_zr, n + 1)
                        dve.wait_ge(s_z, n + 1)
                        if loop or x >= 1:
                            dve.wait_ge(s_qk, n)
                        v.tensor_tensor(out=qk0[:], in0=zs[:, :, 2 * H:3 * H], in1=zr[:, x % 2, :, 0:H], op=ALU.mult).then_inc(s_qk0, 1)
                        dve.wait_ge(s_qk0, n + 1)
                        if loop or x >= 2:
                            dve.wait_ge(s_agg, n - 1)
                        v.tensor_tensor(out=tiles4(h[:, :, 2 * F:2 * F + H]), in0=tiles4(qk0[:]), in1=qx4[:, :, :, F:QW], op=ALU.add).then_inc(s_qk, 1)
                    x = c - 4
                    if is_step(x, loop):
                        n, k = UNROLL * i + x, x % RING
                        dve.wait_ge(s_in[k], 48 * use(x, i))
                        if loop or x >= 2:
                            dve.wait_ge(s_ohb, TILES * (n - 1))
                        v.tensor_scalar(out=rel[:, x % 2, :], in0=gcol[:, k, TILES:2 * TILES], scalar1=step_col(n, 0),
                                        scalar2=None, op0=ALU.add).then_inc(s_rel, 1)
                    x = c - 6
                    if is_step(x, loop):
                        n = UNROLL * i + x
                        h = hh[:, x % 2, :, :]
                        dve.wait_ge(s_qk, n + 1)
                        if loop or x >= 1:
                            dve.wait_ge(s_h2, n)
                        v.tensor_tensor(out=w2[:], in0=h[:, :, 2 * F:2 * F + H], in1=zr[:, x % 2, :, H:2 * H], op=ALU.mult).then_inc(s_w2, 1)
                        if loop or x >= 1:
                            dve.wait_ge(s_qkr, n)
                        if loop or x >= RING:
                            dve.wait_ge(s_qkt, n - RING + 1)
                        v.scalar_tensor_tensor(out=qkr[:, x % RING, :].rearrange("p (t h) -> p t h", h=H),
                                               in0=qkr[:, (x - 1) % RING, :].rearrange("p (t h) -> p t h", h=H),
                                               scalar=step_col(n, 3), in1=h[:, :, 2 * F:2 * F + H],
                                               op0=ALU.mult, op1=ALU.add).then_inc(s_qkr, 1)
                        dve.wait_ge(s_w2, n + 1)
                        v.tensor_tensor(out=heads(h[:, :, F:2 * F]), in0=heads(p[:, x % RING, :, F:2 * F]),
                                        in1=w2[:].unsqueeze(3).to_broadcast([P, TILES, H, D]), op=ALU.mult).then_inc(s_h2, 1)
                    x = c - 3
                    if is_step(x, loop):
                        n = UNROLL * i + x
                        if loop or x >= 2:
                            dve.wait_ge(s_oha, n - 1)
                        v.tensor_scalar(out=ob[:, x % 2, :], in0=zero_c[:], scalar1=step_col(n, 1), scalar2=None, op0=ALU.add).then_inc(s_ob, 1)
                        dve.wait_ge(s_yr, n + 1)
                        for half in range(2):
                            dve.wait_ge(s_u[half], n + 1)
                            if half == 0 and (loop or x >= RING):
                                dve.wait_ge(s_h1, n - RING + 1)
                                dve.wait_ge(s_h2, n - RING + 1)
                                dve.wait_ge(s_psq, n - RING + 1)
                            v.tensor_tensor(out=heads(p[:, x % RING, 2 * half:2 * half + 2, :]),
                                            in0=u_ps[half].rearrange("p (t h d) -> p t h d", t=2, d=D),
                                            in1=yr[:, x % 2, 2 * half:2 * half + 2, :].unsqueeze(3).to_broadcast([P, 2, 2 * H, D]),
                                            op=ALU.mult).then_inc(s_p[half], 1)
                    x = c - 7
                    if is_step(x, loop):
                        n = UNROLL * i + x
                        dve.wait_ge(s_agg, n + 1)
                        if loop or x >= 1:
                            dve.wait_ge(s_run, n)
                        if loop or x >= RING:
                            dve.wait_ge(s_sums_st, 16 * (n - RING + 1))
                        v.scalar_tensor_tensor(out=run[:, x % RING, :], in0=run[:, (x - 1) % RING, :],
                                               scalar=step_col(n, 2), in1=agg_ps, op0=ALU.mult, op1=ALU.add).then_inc(s_run, 1)
                    x = c - 5
                    if is_step(x, loop):
                        n, k = UNROLL * i + x, x % RING
                        dve.wait_ge(s_ga[k], 64 * use(x, i))
                        dve.wait_ge(s_qx, n + 1)
                        if loop or x >= 2:
                            dve.wait_ge(s_z, n - 1)
                        v.tensor_tensor(out=tiles4(z[:, x % 2, :, 2 * F:3 * F]), in0=tiles4(p[:, k, :, 0:F]),
                                        in1=qx4[:, :, :, 0:F], op=ALU.mult).then_inc(s_pq, 1)
                        dve.wait_ge(s_psq, n + 1)
                        dve.wait_ge(s_pq, n + 1)
                        if loop or x >= 1:
                            dve.wait_ge(s_zl, n)
                            dve.wait_ge(s_qk0, n)
                        v.tensor_reduce(out=zs[:], in_=heads(z[:, x % 2, :, :]), axis=AX.X, op=ALU.add).then_inc(s_z, 1)
                every(dve, body, STEPS + 7)


def softmax(nc, a, sem, bank, t):
    f32, bf16, i32 = mybir.dt.float32, mybir.dt.bfloat16, mybir.dt.int32
    ALU, ACT = mybir.AluOpType, mybir.ActivationFunctionType
    qk_t = t["qk_d"].rearrange("g (j h) e -> (g j) h e", h=H)
    with ExitStack() as scope:
        def sb(name, shape, dt=f32):
            return scope.enter_context(nc.sbuf_tensor(name, shape, dt))

        x = sb("m_x", [P, CE])
        m = sb("m_m", [P, CE + 1])
        fresh = sb("m_fresh", [P, CE], bf16)
        ratio = sb("m_ratio", [P, CE])
        junk = sb("m_junk", [P, 2, CE // 7])
        ends = sb("m_ends", [P, 2])
        row = sb("m_row", [1, 2, P])
        row_t = sb("m_row_t", [1, P])
        row_in = sb("m_row_in", [1, P])
        col_in = sb("m_col_in", [P, 2])
        lse_sb = sb("m_lse", [P, 4, 512])
        s_ld, s_pre, s_ch, s_tp, s_ex, s_act = (sem("soft_loads"), sem("soft_pads"), sem("soft_chain"), sem("soft_rows"),
                                                sem("soft_exp"), sem("soft_dve_for_act"))
        s_l, s_lt, s_lc, s_pe = sem("soft_lse"), sem("soft_lse_T"), sem("soft_lse_copied"), sem("soft_for_pe")
        s_ls = [sem(f"soft_lse_stored{i}") for i in range(4)]
        d_i = m[:].bitcast(i32)
        C15 = CHUNKS - 1
        FULL = (GROUPS - 1) * TILES - C15 * CT
        REAL = E - C15 * CE
        SUB, NSUB = CE // 7, 7
        head, sub = E - (GROUPS - 1) * GE, []
        n_loads = []

        with nc.allow_non_contiguous_dma(reason="rows of 512 bytes"), nc.Block() as block:
            @block.gpsimd
            def _(pool):
                nc.gpsimd.memset(x[96:P, REAL:CE], -BIG).then_inc(s_pre, 1)
                nc.gpsimd.memset(d_i[96:P, REAL + 1:CE + 1], -7).then_inc(s_pre, 1)
                nc.gpsimd.memset(d_i[0:32, 0:1], -7).then_inc(s_pre, 1)

            @block.sync
            def _(sp):
                n = [0]

                def load(dst_ap, src_ap):
                    sp.dma_start(dst_ap, src_ap).then_inc(s_ld, 16)
                    n[0] += 1

                sp.wait_ge(s_pre, 3)
                for c in range(CHUNKS):
                    rows = slice(H * c, H * c + H)
                    lo = 0 if c else 1
                    hi = CE + 1 if c < C15 else REAL + 1
                    load(d_i[rows, lo:hi], a["dst"][CE * c - 1 + lo:CE * c - 1 + hi].partition_broadcast(H))
                for c in range(CHUNKS):
                    rows = slice(H * c, H * c + H)
                    k = CT if c < C15 else FULL
                    load(x[rows, 0:k * P].rearrange("h (t e) -> h t e", e=P), qk_t[CT * c:CT * c + k, :, :].rearrange("t h e -> h t e"))
                at, tile0 = FULL * P, (GROUPS - 1) * TILES
                for k in range(DUP // P, TILES):
                    e0 = DUP % P if k == DUP // P else 0
                    load(x[H * C15:P, at:at + P - e0], qk_t[tile0 + k, :, e0:P])
                    at += P - e0
                assert at == REAL
                n_loads.append(n[0])
                for k in range(-(-CT // 4)):
                    tiles = min(4, CT - 4 * k)
                    sp.wait_ge(s_lc, k + 1)
                    sp.dma_start(t["lse_d"][4 * k * P:(4 * k + tiles) * P, :].rearrange("(t p) c -> p t c", p=P),
                                 lse_sb[:, k % 4, 0:tiles * P].rearrange("p (t c) -> p t c", c=P)).then_inc(s_ls[k % 4], 16)
                K = -(-CT // 4)
                for q in range(4):
                    sp.wait_ge(s_ls[q], 16 * len(range(q, K, 4)))

            @block.vector
            def _(dve):
                v = nc.vector
                done = [0]

                def link(ins):
                    done[0] += 1
                    ins.then_inc(s_ch, 1)
                    dve.wait_ge(s_ch, done[0])

                def carry(state, op0, op1, first, part):
                    v.tensor_copy(out=row[:], in_=bank[0][0:1, 0:2 * P].rearrange("o (r c) -> o r c", r=2)).then_inc(s_ch, 1)
                    done[0] += 1
                    dve.wait_ge(s_ch, done[0])
                    for h in range(H):
                        by_c = lambda ap: ap.rearrange("o (c h) -> o c h", h=H)[:, :, h]
                        v.tensor_tensor_scan(out=by_c(row_t[:]), data0=by_c(row[0:1, 1, :]), data1=by_c(row[0:1, 0, :]),
                                             initial=first, op0=op0, op1=op1).then_inc(s_ch, 1)
                        done[0] += 1
                    dve.wait_ge(s_ch, done[0])
                    link(v.memset(row_in[0:1, 0:H], first))
                    v.tensor_copy(out=row_in[0:1, H:P], in_=row_t[0:1, 0:P - H]).then_inc(s_ch, 1)
                    done[0] += 1
                    dve.wait_ge(s_ch, done[0])
                    v.tensor_copy(out=junk[0:1, 0, 0:1], in_=row_in[0:1, 0:1]).then_inc(s_pe, 1)

                dve.wait_ge(s_ld, 16 * n_loads[0])
                link(v.tensor_tensor(out=fresh[:], in0=d_i[:, 1:CE + 1], in1=d_i[:, 0:CE], op=ALU.not_equal))
                link(v.tensor_scalar(out=fresh[:], in0=fresh[:], scalar1=-BIG, scalar2=None, op0=ALU.mult))
                link(v.tensor_tensor(out=ends[:, 1:2], in0=d_i[:, CE:CE + 1], in1=d_i[:, 0:1], op=ALU.not_equal))
                link(v.tensor_scalar(out=ends[:, 1:2], in0=ends[:, 1:2], scalar1=-BIG, scalar2=None, op0=ALU.mult))
                link(v.tensor_tensor_scan(out=m[:, 1:CE + 1], data0=fresh[:], data1=x[:], initial=-BIG, op0=ALU.add, op1=ALU.max))
                v.tensor_copy(out=ends[:, 0:1], in_=m[:, CE:CE + 1]).then_inc(s_pe, 1)
                dve.wait_ge(s_tp, 1)
                carry(0, ALU.add, ALU.max, -BIG, 0)
                dve.wait_ge(s_tp, 2)
                link(v.tensor_copy(out=col_in[:, 0:1], in_=bank[1][:, 0:1]))
                link(v.tensor_copy(out=m[:, 0:1], in_=col_in[:, 0:1]))
                link(v.tensor_tensor_scan(out=m[:, 1:CE + 1], data0=fresh[:], data1=x[:], initial=col_in[:, 0:1], op0=ALU.add, op1=ALU.max))
                for k in range(NSUB):
                    lo, hi = k * SUB, (k + 1) * SUB
                    v.tensor_tensor(out=x[:, lo:hi], in0=x[:, lo:hi], in1=m[:, lo + 1:hi + 1], op=ALU.subtract).then_inc(s_act, 1)
                    link(v.tensor_tensor(out=ratio[:, lo:hi], in0=m[:, lo:hi], in1=m[:, lo + 1:hi + 1], op=ALU.subtract))
                    v.tensor_tensor(out=ratio[:, lo:hi], in0=ratio[:, lo:hi], in1=fresh[:, lo:hi], op=ALU.add).then_inc(s_act, 1)
                link(v.tensor_tensor(out=ends[:, 0:1], in0=col_in[:, 0:1], in1=m[:, CE:CE + 1], op=ALU.subtract))
                v.tensor_tensor(out=ends[:, 1:2], in0=ends[:, 0:1], in1=ends[:, 1:2], op=ALU.add).then_inc(s_act, 1)
                for k in range(NSUB):
                    lo, hi = k * SUB, (k + 1) * SUB
                    dve.wait_ge(s_ex, 2 * (k + 1))
                    link(v.tensor_tensor_scan(out=junk[:, k % 2, :], data0=ratio[:, lo:hi], data1=x[:, lo:hi],
                                              initial=0.0 if k == 0 else junk[:, (k - 1) % 2, SUB - 1:SUB], op0=ALU.mult, op1=ALU.add))
                dve.wait_ge(s_ex, 2 * NSUB + 1)
                v.tensor_copy(out=ends[:, 0:1], in_=junk[:, (NSUB - 1) % 2, SUB - 1:SUB]).then_inc(s_pe, 1)
                dve.wait_ge(s_tp, 3)
                carry(1, ALU.mult, ALU.add, 0.0, 1)
                dve.wait_ge(s_tp, 4)
                link(v.tensor_copy(out=col_in[:, 1:2], in_=bank[1][:, 0:1]))
                for k in range(NSUB):
                    lo, hi = k * SUB, (k + 1) * SUB
                    v.tensor_tensor_scan(out=x[:, lo:hi], data0=ratio[:, lo:hi], data1=x[:, lo:hi],
                                         initial=col_in[:, 1:2] if k == 0 else junk[:, k % 2, 0:1], op0=ALU.mult, op1=ALU.add).then_inc(s_ch, 1)
                    done[0] += 1
                    dve.wait_ge(s_ch, done[0])
                    v.tensor_copy(out=junk[:, (k + 1) % 2, 0:1], in_=x[:, hi - 1:hi]).then_inc(s_act, 1)
                    dve.wait_ge(s_act, 2 * NSUB + 1 + k + 1)
                    if k >= 1:
                        dve.wait_ge(s_ex, 2 * NSUB + 1 + k)
                        v.tensor_tensor(out=x[:, lo - SUB:lo], in0=x[:, lo - SUB:lo], in1=m[:, lo - SUB + 1:lo + 1], op=ALU.add).then_inc(s_l, 1)
                dve.wait_ge(s_ex, 3 * NSUB + 1)
                v.tensor_tensor(out=x[:, CE - SUB:CE], in0=x[:, CE - SUB:CE], in1=m[:, CE - SUB + 1:CE + 1], op=ALU.add).then_inc(s_l, 1)
                for k in range(1, -(-CT // 4), 2):
                    tiles = min(4, CT - 4 * k)
                    dve.wait_ge(s_lt, k + 1)
                    if k >= 4:
                        dve.wait_ge(s_ls[k % 4], 16 * (k // 4))
                    dve.wait_ge(s_lc, k)
                    v.tensor_copy(out=lse_sb[:, k % 4, 0:tiles * P], in_=bank[2 + k % 4][:, 0:tiles * P]).then_inc(s_lc, 1)

            @block.scalar
            def _(act):
                for k in range(NSUB):
                    lo, hi = k * SUB, (k + 1) * SUB
                    act.wait_ge(s_act, 2 * k + 1)
                    nc.scalar.activation(x[:, lo:hi], x[:, lo:hi], ACT.Exp).then_inc(s_ex, 1)
                    act.wait_ge(s_act, 2 * k + 2)
                    nc.scalar.activation(ratio[:, lo:hi], ratio[:, lo:hi], ACT.Exp).then_inc(s_ex, 1)
                act.wait_ge(s_act, 2 * NSUB + 1)
                nc.scalar.activation(ends[:, 1:2], ends[:, 1:2], ACT.Exp).then_inc(s_ex, 1)
                for k in range(NSUB):
                    lo, hi = k * SUB, (k + 1) * SUB
                    act.wait_ge(s_act, 2 * NSUB + 1 + k + 1)
                    nc.scalar.activation(x[:, lo:hi], x[:, lo:hi], ACT.Ln).then_inc(s_ex, 1)
                for k in range(0, -(-CT // 4), 2):
                    tiles = min(4, CT - 4 * k)
                    act.wait_ge(s_lt, k + 1)
                    if k >= 4:
                        act.wait_ge(s_ls[k % 4], 16 * (k // 4))
                    act.wait_ge(s_lc, k)
                    nc.scalar.activation(lse_sb[:, k % 4, 0:tiles * P], bank[2 + k % 4][:, 0:tiles * P], ACT.Copy).then_inc(s_lc, 1)

            @block.tensor
            def _(pe):
                for part in range(2):
                    pe.wait_ge(s_pe, 2 * part + 1)
                    nc.tensor.transpose(bank[0][0:1, 0:P], ends[:, 0:1], t["ident"][:])
                    nc.tensor.transpose(bank[0][0:1, P:2 * P], ends[:, 1:2], t["ident"][:]).then_inc(s_tp, 1)
                    pe.wait_ge(s_pe, 2 * part + 2)
                    nc.tensor.matmul(bank[1][:, 0:1], row_in[0:1, :], t["one_c"][0:1, 0:1], start=True, stop=True).then_inc(s_tp, 1)
                for k in range(-(-CT // 4)):
                    tiles = min(4, CT - 4 * k)
                    pe.wait_ge(s_l, -(-(4 * k + tiles) * P // SUB))
                    if k >= 4:
                        pe.wait_ge(s_lc, k - 3)
                    for j in range(tiles):
                        last = nc.tensor.transpose(bank[2 + k % 4][:, j * P:(j + 1) * P], x[:, (4 * k + j) * P:(4 * k + j + 1) * P], t["ident"][:])
                    last.then_inc(s_lt, 1)


def finish(nc, a, sem, bank, t, out):
    f32, i32, u32 = mybir.dt.float32, mybir.dt.int32, mybir.dt.uint32
    ALU, ACT, AX = mybir.AluOpType, mybir.ActivationFunctionType, mybir.AxisListType
    ident, rows16 = t["ident"], t["rows16"]
    ZB, ZG, ZBETA = 4, 5, 6
    NBK = 4
    TURNS = BLOCKS // NBK
    assert TURNS % 2 == 0 and BLOCKS % NBK == 1
    with ExitStack() as scope:
        def sb(name, shape, dt=f32):
            return scope.enter_context(nc.sbuf_tensor(name, shape, dt))

        cnt = sb("f_cnt", [P, BLOCKS])
        tri = sb("f_tri", [P, P])
        ones = sb("f_ones", [P, P])
        tot = sb("f_tot", [P, BLOCKS])
        pre = sb("f_pre", [P, BLOCKS])
        end = sb("f_end", [P, BLOCKS])
        thr_i = sb("f_thr_i", [P, CHUNKS + 1], i32)
        thr = sb("f_thr", [P, CHUNKS + 1])
        ge = sb("f_ge", [P, BLOCKS, CHUNKS + 1])
        oc = sb("f_oc", [P, BLOCKS, CHUNKS])
        nc_ = sb("f_nc", [P, BLOCKS])
        idx = sb("f_idx", [P, BLOCKS + 3], i32)
        idc = sb("f_idc", [P, 2, NBK], i32)
        sm = sb("f_sm", [P, 2, NBK, AW])
        xb = sb("f_x", [P, 2, NBK, F])
        lg = sb("f_lg", [P, 2, NBK, P])
        lt = sb("f_lt", [P, NBK, P])
        lse = sb("f_lse", [P, NBK, H])
        lc = sb("f_lc", [P, NBK, H])
        tq = sb("f_tq", [P, NBK, H])
        a1 = sb("f_a1", [P, NBK, F])
        ag = sb("f_ag", [P, NBK, F])
        agt = sb("f_agt", [P, NBK, P])
        u = sb("f_u", [P, NBK, F])
        z = sb("f_z", [P, NBK, F])
        zr = sb("f_zr", [P, NBK, F])
        mean = sb("f_mean", [P, NBK, H])
        zc = sb("f_zc", [P, NBK, F])
        zq = sb("f_zq", [P, NBK, F])
        var = sb("f_var", [P, NBK, H])
        lnv = sb("f_lnv", [P, NBK, H])
        r = sb("f_r", [P, NBK, H])
        y = sb("f_y", [P, NBK, F])
        m1 = sb("f_m1", [P, NBK])
        yc = sb("f_yc", [P, NBK, F])
        yq = sb("f_yq", [P, NBK, F])
        v1 = sb("f_v1", [P, NBK])
        l1 = sb("f_l1", [P, NBK])
        r1 = sb("f_r1", [P, NBK])
        o = sb("f_o", [P, 2, NBK, F])
        s_c, s_k, s_ch, s_t = sem("fin_count"), sem("fin_consts"), sem("fin_chain"), sem("fin_prefix")
        with nc.allow_non_contiguous_dma(reason="a count per node"), nc.Block() as block:
            @block.sync
            def _(sp):
                sp.dma_start(cnt[:], t["sums_d"][:, :, AW - 1:AW].rearrange("b p o -> p (b o)")).then_inc(s_c, 16)

            @block.gpsimd
            def _(pool):
                nc.gpsimd.memset(tri[:], 1.0).then_inc(s_k, 1)
                nc.gpsimd.memset(ones[:], 1.0).then_inc(s_k, 1)
                nc.gpsimd.iota(thr_i[:], pattern=[[CE, CHUNKS + 1]], base=0, channel_multiplier=0).then_inc(s_k, 1)
                pool.wait_ge(s_k, 1)
                nc.gpsimd.affine_select(out=tri[:], in_=tri[:], compare_op=ALU.is_ge, fill=0.0, base=0,
                                        pattern=[[1, P]], channel_multiplier=-1).then_inc(s_k, 1)

            @block.tensor
            def _(pe):
                pe.wait_ge(s_c, 16)
                pe.wait_ge(s_k, 4)
                nc.tensor.matmul(bank[0][:, 0:BLOCKS], tri[:], cnt[:], start=True, stop=True)
                nc.tensor.matmul(bank[1][:, 0:BLOCKS], ones[:], cnt[:], start=True, stop=True).then_inc(s_t, 1)

            @block.vector
            def _(dve):
                v = nc.vector
                done = [0]

                def link(ins):
                    done[0] += 1
                    ins.then_inc(s_ch, 1)
                    dve.wait_ge(s_ch, done[0])

                dve.wait_ge(s_k, 4)
                link(v.tensor_copy(out=thr[:], in_=thr_i[:]))
                link(v.memset(idx[:], 0))
                dve.wait_ge(s_t, 1)
                link(v.tensor_copy(out=tot[:], in_=bank[1][:, 0:BLOCKS]))
                link(v.memset(ge[:, :, 0], 0.0))
                link(v.tensor_tensor_scan(out=pre[:], data0=tot[:], data1=ge[:, :, 0], initial=0.0, op0=ALU.add, op1=ALU.add))
                link(v.tensor_tensor(out=pre[:], in0=pre[:], in1=tot[:], op=ALU.subtract))
                link(v.tensor_tensor(out=end[:], in0=pre[:], in1=bank[0][:, 0:BLOCKS], op=ALU.add))
                link(v.tensor_scalar(out=end[:], in0=end[:], scalar1=-1.0, scalar2=0.0, op0=ALU.add, op1=ALU.max))
                link(v.tensor_tensor(out=ge[:], in0=end[:].unsqueeze(2).to_broadcast([P, BLOCKS, CHUNKS + 1]),
                                     in1=thr[:].unsqueeze(1).to_broadcast([P, BLOCKS, CHUNKS + 1]), op=ALU.is_ge))
                link(v.tensor_tensor(out=oc[:], in0=ge[:, :, 0:CHUNKS], in1=ge[:, :, 1:CHUNKS + 1], op=ALU.subtract))
                link(v.tensor_reduce(out=nc_[:], in_=ge[:, :, 1:CHUNKS + 1], axis=AX.X, op=ALU.add))
                link(v.scalar_tensor_tensor(out=end[:], in0=nc_[:], scalar=-float(CE), in1=end[:], op0=ALU.mult, op1=ALU.add))
                link(v.tensor_copy(out=idx[:, 0:BLOCKS], in_=end[:]))

        s_in = [sem(f"fin_loaded{i}") for i in range(2)]
        s_g = [sem(f"fin_lse_gathered{i}") for i in range(2)]
        s_o = [sem(f"fin_stored{i}") for i in range(2)]
        names = ("idc lt lse lc a1 ag tq agt_ps agt z_ps u z zb relu mean zc zq var lnv r zn zg zbeta y m1 yc yq v1 l1 r1 o").split()
        s = {n: sem("fin_" + n) for n in names}

        def turns(eng, body):
            for k in range(2):
                body(k, k, 1, NBK * k, NBK, P)
            with eng.Fori(1, TURNS // 2) as i:
                for k in range(2):
                    body(2 * i + k, k, i + 1, NBK * (2 * i + k), NBK, P)
            body(TURNS, 0, TURNS // 2 + 1, BLOCKS - 1, 1, LAST)

        with nc.Block() as block:
            @block.sync
            def _(sp):
                def load(slot, b, nb, rows):
                    sp.dma_start(sm[0:rows, slot, 0:nb, :], t["sums_d"][bass.ds(b, nb), 0:rows, :].rearrange("b p c -> p b c")).then_inc(s_in[slot], 16)
                    sp.dma_start(xb[0:rows, slot, 0:nb, :],
                                 a["x"][bass.ds(P * b, nb * rows), :].rearrange("(b p) f -> p b f", p=rows)).then_inc(s_in[slot], 16)

                def store(n, slot, b, nb, rows):
                    sp.wait_ge(s["o"], n + 1)
                    sp.dma_start(out[bass.ds(P * b, nb * rows), :].rearrange("(b p) f -> p b f", p=rows), o[0:rows, slot, 0:nb, :]).then_inc(s_o[slot], 16)

                load(0, 0, NBK, P)
                load(1, NBK, NBK, P)
                with sp.Fori(0, TURNS // 2 - 1) as i:
                    for k in range(2):
                        store(2 * i + k, k, NBK * (2 * i + k), NBK, P)
                        load(k, NBK * (2 * i + k + 2), NBK, P)
                store(TURNS - 2, 0, NBK * (TURNS - 2), NBK, P)
                load(0, BLOCKS - 1, 1, LAST)
                store(TURNS - 1, 1, NBK * (TURNS - 1), NBK, P)
                store(TURNS, 0, BLOCKS - 1, 1, LAST)
                sp.wait_ge(s_o[0], 16 * (TURNS // 2 + 1))
                sp.wait_ge(s_o[1], 16 * (TURNS // 2))

            @block.gpsimd
            def _(pool):
                g = nc.gpsimd
                last_row = pool.alloc_register("last_row")
                rows_less_2 = pool.to_reg(CE - 2)

                def gather(n, slot, nth, b, nb, rows):
                    g.tensor_copy(out=idc[:, slot, 0:nb], in_=idx[:, bass.ds(b, nb)]).then_inc(s["idc"], 1)
                    pool.wait_ge(s["idc"], n + 1)
                    pool.reg_add(last_row, rows_less_2, 1)
                    for k in range(nb):
                        pool.indirect_dma_start(out=lg[:, slot, k, :], out_offset=None, in_=t["lse_d"],
                                                in_offset=bass.IndirectOffsetOnAxis(ap=idc[:, slot, k:k + 1].bitcast(u32), axis=0),
                                                bounds_check=last_row, oob_is_err=True).then_inc(s_g[slot], 16)

                def body(n, slot, nth, b, nb, rows):
                    pool.wait_ge(s["zn"], n + 1)
                    rr = slice(0, rows)
                    r16 = lambda k: rows16[rr, k, :].unsqueeze(1).to_broadcast([rows, nb * H, D])
                    hd = lambda ap: ap.rearrange("p b (h d) -> p (b h) d", d=D)
                    g.tensor_tensor(out=hd(zc[rr, 0:nb, :]), in0=hd(zc[rr, 0:nb, :]), in1=r16(ZG), op=ALU.mult).then_inc(s["zg"], 1)
                    pool.wait_ge(s["zg"], n + 1)
                    g.tensor_tensor(out=hd(zc[rr, 0:nb, :]), in0=hd(zc[rr, 0:nb, :]), in1=r16(ZBETA), op=ALU.add).then_inc(s["zbeta"], 1)

                gather(0, 0, 1, 0, NBK, P)
                for k in range(2):
                    pool.wait_ge(s["lt"], k)
                    gather(k + 1, 1 - k, 0, NBK * (k + 1), NBK, P)
                    body(k, k, 0, 0, NBK, P)
                with pool.Fori(1, TURNS // 2 - 1) as i:
                    for k in range(2):
                        pool.wait_ge(s["lt"], 2 * i + k)
                        gather(2 * i + k + 1, 1 - k, 0, NBK * (2 * i + k + 1), NBK, P)
                        body(2 * i + k, k, 0, 0, NBK, P)
                for k in range(2):
                    n = TURNS - 2 + k
                    pool.wait_ge(s["lt"], n)
                    if k == 0:
                        gather(n + 1, 1, 0, NBK * (n + 1), NBK, P)
                    else:
                        gather(n + 1, 0, 0, BLOCKS - 1, 1, LAST)
                    body(n, k, 0, 0, NBK, P)
                body(TURNS, 0, 0, 0, 1, LAST)

            @block.tensor
            def _(pe):
                def body(n, slot, nth, b, nb, rows):
                    pe.wait_ge(s["ag"], n + 1)
                    pe.wait_ge(s["agt"], n)
                    for k in range(nb):
                        last = nc.tensor.transpose(bank[0][:, k * P:k * P + rows], ag[0:rows, k, :], ident[0:rows, 0:rows])
                    last.then_inc(s["agt_ps"], 1)
                    pe.wait_ge(s["agt"], n + 1)
                    pe.wait_ge(s["z"], n)
                    for k in range(nb):
                        last = nc.tensor.matmul(bank[1][0:rows, k * F:(k + 1) * F], agt[:, k, 0:rows], t["z_w"][:], start=True, stop=True)
                    last.then_inc(s["z_ps"], 1)
                turns(pe, body)

            @block.scalar
            def _(act):
                def body(n, slot, nth, b, nb, rows):
                    rr = slice(0, rows)
                    act.wait_ge(s["agt_ps"], n + 1)
                    act.wait_ge(s["z_ps"], n)
                    nc.scalar.activation(agt[:, 0:nb, 0:rows], bank[0][:, 0:nb * P].rearrange("p (b n) -> p b n", n=P)[:, :, 0:rows],
                                         ACT.Copy).then_inc(s["agt"], 1)
                    act.wait_ge(s["zb"], n + 1)
                    act.wait_ge(s["zc"], n)
                    nc.scalar.activation(zr[rr, 0:nb, :], z[rr, 0:nb, :], ACT.Relu).then_inc(s["relu"], 1)
                    act.wait_ge(s["zc"], n + 1)
                    act.wait_ge(s["var"], n)
                    nc.scalar.activation(zq[rr, 0:nb, :], zc[rr, 0:nb, :], ACT.Square).then_inc(s["zq"], 1)
                    act.wait_ge(s["var"], n + 1)
                    nc.scalar.activation(lnv[rr, 0:nb, :], var[rr, 0:nb, :], ACT.Ln, bias=t["eps_c"][rr, 0:1], scale=1.0 / D).then_inc(s["lnv"], 1)
                    act.wait_ge(s["lnv"], n + 1)
                    act.wait_ge(s["zn"], n)
                    nc.scalar.activation(r[rr, 0:nb, :], lnv[rr, 0:nb, :], ACT.Exp, scale=-0.5).then_inc(s["r"], 1)
                    act.wait_ge(s["yc"], n + 1)
                    act.wait_ge(s["v1"], n)
                    nc.scalar.activation(yq[rr, 0:nb, :], yc[rr, 0:nb, :], ACT.Square).then_inc(s["yq"], 1)
                    act.wait_ge(s["v1"], n + 1)
                    nc.scalar.activation(l1[rr, 0:nb], v1[rr, 0:nb], ACT.Ln, bias=t["eps_c"][rr, 0:1], scale=1.0 / F).then_inc(s["l1"], 1)
                    act.wait_ge(s["l1"], n + 1)
                    act.wait_ge(s["o"], n)
                    nc.scalar.activation(r1[rr, 0:nb], l1[rr, 0:nb], ACT.Exp, scale=-0.5).then_inc(s["r1"], 1)
                turns(act, body)

            @block.vector
            def _(dve):
                v = nc.vector

                def body(n, slot, nth, b, nb, rows):
                    rr = slice(0, rows)
                    hd = lambda ap: ap.rearrange("p b (h d) -> p b h d", d=D)
                    hf = lambda ap: ap.rearrange("p b (h d) -> p (b h) d", d=D)
                    per_head = lambda ap: ap[rr, 0:nb, :].unsqueeze(3).to_broadcast([rows, nb, H, D])
                    r16 = lambda k: rows16[rr, k, :].unsqueeze(1).to_broadcast([rows, nb * H, D])

                    def step(name, ins, *needs):
                        return ins

                    gathers = 16 * NBK * (nth - 1) + 16 * nb
                    dve.wait_ge(s_g[slot], gathers)
                    v.tensor_tensor(out=lt[rr, 0:nb, :].rearrange("p b (c h) -> p b c h", h=H),
                                    in0=lg[rr, slot, 0:nb, :].rearrange("p b (c h) -> p b c h", h=H),
                                    in1=oc[rr, bass.ds(b, nb), :].unsqueeze(3).to_broadcast([rows, nb, CHUNKS, H]), op=ALU.mult).then_inc(s["lt"], 1)
                    dve.wait_ge(s["lt"], n + 1)
                    v.tensor_reduce(out=lse[rr, 0:nb, :], in_=lt[rr, 0:nb, :].rearrange("p b (c h) -> p b h c", h=H), axis=AX.X, op=ALU.add).then_inc(s["lse"], 1)
                    dve.wait_ge(s["lse"], n + 1)
                    dve.wait_ge(s_in[slot], 32 * nth)
                    v.tensor_tensor(out=lc[rr, 0:nb, :], in0=lse[rr, 0:nb, :],
                                    in1=sm[rr, slot, 0:nb, AW - 1:AW].to_broadcast([rows, nb, H]), op=ALU.mult).then_inc(s["lc"], 1)
                    v.tensor_tensor(out=hd(a1[rr, 0:nb, :]), in0=hd(sm[rr, slot, 0:nb, 0:F]), in1=per_head(lse), op=ALU.mult).then_inc(s["a1"], 1)
                    dve.wait_ge(s["a1"], n + 1)
                    dve.wait_ge(s["agt_ps"], n)
                    v.tensor_tensor(out=ag[rr, 0:nb, :], in0=sm[rr, slot, 0:nb, F:2 * F], in1=a1[rr, 0:nb, :], op=ALU.subtract).then_inc(s["ag"], 1)
                    dve.wait_ge(s["lc"], n + 1)
                    v.tensor_tensor(out=tq[rr, 0:nb, :], in0=sm[rr, slot, 0:nb, 2 * F:2 * F + H], in1=lc[rr, 0:nb, :], op=ALU.subtract).then_inc(s["tq"], 1)
                    dve.wait_ge(s["tq"], n + 1)
                    v.tensor_tensor(out=hd(u[rr, 0:nb, :]), in0=t["z_beta_w"][rr, :].rearrange("p (h d) -> p h d", d=D).unsqueeze(1).to_broadcast([rows, nb, H, D]),
                                    in1=per_head(tq), op=ALU.mult).then_inc(s["u"], 1)
                    dve.wait_ge(s["u"], n + 1)
                    dve.wait_ge(s["z_ps"], n + 1)
                    dve.wait_ge(s["relu"], n)
                    v.tensor_tensor(out=z[rr, 0:nb, :], in0=bank[1][rr, 0:nb * F].rearrange("p (b f) -> p b f", f=F), in1=u[rr, 0:nb, :], op=ALU.add).then_inc(s["z"], 1)
                    dve.wait_ge(s["z"], n + 1)
                    v.tensor_tensor(out=hf(z[rr, 0:nb, :]), in0=hf(z[rr, 0:nb, :]), in1=r16(ZB), op=ALU.add).then_inc(s["zb"], 1)
                    dve.wait_ge(s["relu"], n + 1)
                    v.tensor_reduce(out=mean[rr, 0:nb, :], in_=hd(zr[rr, 0:nb, :]), axis=AX.X, op=ALU.add).then_inc(s["mean"], 1)
                    dve.wait_ge(s["mean"], n + 1)
                    v.scalar_tensor_tensor(out=hf(zc[rr, 0:nb, :]), in0=mean[rr, 0:nb, :].rearrange("p b h -> p (b h)").unsqueeze(2).to_broadcast([rows, nb * H, D]),
                                           scalar=-1.0 / D, in1=hf(zr[rr, 0:nb, :]), op0=ALU.mult, op1=ALU.add).then_inc(s["zc"], 1)
                    dve.wait_ge(s["zq"], n + 1)
                    v.tensor_reduce(out=var[rr, 0:nb, :], in_=hd(zq[rr, 0:nb, :]), axis=AX.X, op=ALU.add).then_inc(s["var"], 1)
                    dve.wait_ge(s["r"], n + 1)
                    dve.wait_ge(s["zc"], n + 1)
                    v.tensor_tensor(out=hd(zc[rr, 0:nb, :]), in0=hd(zc[rr, 0:nb, :]), in1=per_head(r), op=ALU.mult).then_inc(s["zn"], 1)
                    dve.wait_ge(s["zbeta"], n + 1)
                    v.tensor_tensor(out=y[rr, 0:nb, :], in0=zc[rr, 0:nb, :], in1=xb[rr, slot, 0:nb, :], op=ALU.add).then_inc(s["y"], 1)
                    dve.wait_ge(s["y"], n + 1)
                    v.tensor_reduce(out=m1[rr, 0:nb], in_=y[rr, 0:nb, :], axis=AX.X, op=ALU.add).then_inc(s["m1"], 1)
                    dve.wait_ge(s["m1"], n + 1)
                    v.scalar_tensor_tensor(out=yc[rr, 0:nb, :], in0=m1[rr, 0:nb].unsqueeze(2).to_broadcast([rows, nb, F]), scalar=-1.0 / F,
                                           in1=y[rr, 0:nb, :], op0=ALU.mult, op1=ALU.add).then_inc(s["yc"], 1)
                    dve.wait_ge(s["yq"], n + 1)
                    v.tensor_reduce(out=v1[rr, 0:nb], in_=yq[rr, 0:nb, :], axis=AX.X, op=ALU.add).then_inc(s["v1"], 1)
                    dve.wait_ge(s["r1"], n + 1)
                    dve.wait_ge(s["yc"], n + 1)
                    dve.wait_ge(s_o[slot], 16 * (nth - 1))
                    v.tensor_tensor(out=o[rr, slot, 0:nb, :], in0=yc[rr, 0:nb, :], in1=r1[rr, 0:nb].unsqueeze(2).to_broadcast([rows, nb, F]), op=ALU.mult).then_inc(s["o"], 1)
                turns(dve, body)


_WEIGHTS = ["Wq", "Wk", "Wv", "Wke", "Wve", "gq", "bq", "gk", "bk", "gv", "bv", "gke", "bke", "gve", "bve",
            "relk_W", "relk_b", "relk_g", "relk_beta", "relv_W", "relv_b", "relv_g", "relv_beta", "z_W", "z_b", "z_g", "z_beta"]


def kernel(**inputs):
    import concourse.bacc as _bacc
    from concourse.bass_utils import run_bass_kernel_spmd as _run

    nc = _bacc.Bacc("TRN2", target_bir_lowering=False, num_devices=1)
    arrays, aps = {}, {}
    names = {"x": "x", "src": "src", "dst": "dst", "edge_attr_128": "edge_attr_128"}
    names.update({w: "L0_gnn_" + w for w in _WEIGHTS})
    for short, name in names.items():
        arr = np.ascontiguousarray(inputs[name])
        arrays["in_" + short] = arr
        aps[short] = nc.dram_tensor("in_" + short, arr.shape, mybir.dt.from_np(arr.dtype), kind="ExternalInput").ap()
    out = nc.dram_tensor("out_0", (N, F), mybir.dt.float32, kind="ExternalOutput").ap()
    edge_attention(nc, aps, out)
    r = _run(nc, [arrays], core_ids=[0])
    return r.results[0]["out_0"]
```

```python
import numpy as np
import concourse.bass as bass
from concourse import mybir
from contextlib import ExitStack

P = 128
N, E, F, H, D = 6250, 200000, 128, 8, 16
TILES = 4
GE = TILES * P
GROUPS = -(-E // GE)
TAIL0 = E - GE
DUP = GROUPS * GE - E
BLOCKS = -(-N // P)
LAST = N - (BLOCKS - 1) * P
STEPS = GROUPS + BLOCKS - 1
EPS = 1e-5
QW = F + H
AW = 2 * F + H + 1
CHUNKS = P // H
CT = -(-(-(-E // P)) // CHUNKS)
CE = CT * P
BIG = 1.0e30
UNROLL = 12
RING = 6
STORE_LAG = 12
PEEL = 15



def edge_attention(nc, a, out):
    f32, bf16, i32, u32 = mybir.dt.float32, mybir.dt.bfloat16, mybir.dt.int32, mybir.dt.uint32
    ALU, ACT, AX = mybir.AluOpType, mybir.ActivationFunctionType, mybir.AxisListType
    ctx = ExitStack()
    with ctx:
        def sb(name, shape, dt=f32):
            return ctx.enter_context(nc.sbuf_tensor(name, shape, dt))

        def sem(name):
            return ctx.enter_context(nc.semaphore(name))

        table = nc.dram_tensor("node_table", [N, 2 * F], f32, kind="Internal").ap()
        sums_d = nc.dram_tensor("node_sums", [BLOCKS, P, AW], f32, kind="Internal").ap()
        qk_d = nc.dram_tensor("edge_qk", [GROUPS, TILES * H, P], f32, kind="Internal").ap()
        lse_d = nc.dram_tensor("edge_lse", [CE, P], f32, kind="Internal").ap()

        banks = ctx.enter_context(nc.psum_tensor("banks", [P, 8, 512], f32))
        bank = [banks[:, i, :] for i in range(8)]

        ident = sb("ident", [P, P])
        iota_p = sb("iota_p", [P, 1])
        z_w = sb("z_w", [P, F])
        z_beta_w = sb("z_beta_w", [P, F])
        rows16 = sb("rows16", [P, 9, D])
        eps_c = sb("eps_c", [P, 1])
        one_c = sb("one_c", [P, 1])
        counts = sb("counts", [P, BLOCKS])

        mid = ctx.enter_context(ExitStack())

        def sb_mid(name, shape, dt=f32):
            return mid.enter_context(nc.sbuf_tensor(name, shape, dt))

        iota_n = sb_mid("iota_n", [P, P])
        w_node = sb_mid("w_node", [P, 5 * F])
        w_edge = sb_mid("w_edge", [P, 4 * F])
        table_bias = sb_mid("table_bias", [P, 2, F])
        gq4 = sb_mid("gq4", [P, F])
        bq4 = sb_mid("bq4", [P, F])
        gqb = sb_mid("gqb", [P, F])
        bqb = sb_mid("bqb", [P, H])
        cols = sb_mid("cols", [P, GROUPS, 2 * TILES])
        step_cols = sb_mid("step_cols", [P, STEPS, 4])
        step_ints = sb_mid("step_ints", [1, STEPS], i32)
        RELKG, RELKB, RELKBIAS, RELVBIAS, ZB, ZG, ZBETA = range(7)

        with ExitStack() as scope:
            def sbp(name, shape, dt=f32):
                return scope.enter_context(nc.sbuf_tensor(name, shape, dt))

            w_all = sbp("w_all", [P, 5, F])
            w_mean = sbp("w_mean", [P, 5 * H])
            w_c = sbp("w_c", [P, 5, F])
            w_ct = sbp("w_ct", [P, 4, F])
            rel4 = sbp("rel4", [P, 4, D])
            rel_mean = sbp("rel_mean", [P, 4])
            rel_c = sbp("rel_c", [P, 4, D])
            z4 = sbp("z4", [P, D])
            mask = sbp("mask", [P, F])
            bd = sbp("bd", [P, 4, F])
            bdg = sbp("bdg", [P, 4, F])
            zbd = sbp("zbd", [P, F])
            col = sbp("col", [P, 10])
            colb = sbp("colb", [P, 5, F])
            qrows = sbp("qrows", [P, 2, F])
            rb_mean = sbp("rb_mean", [P, 2])
            rb_c = sbp("rb_c", [P, 2, D])
            tmp_q = sbp("tmp_q", [P, F])
            src_i = sbp("src_i", [P, 13, P], i32)
            dst_i = sbp("dst_i", [P, 13, P], i32)
            src_f = sbp("src_f", [P, 13, P])
            dst_f = sbp("dst_f", [P, 13, P])
            iota_i = sbp("iota_i", [P, STEPS], i32)
            iota_s = sbp("iota_s", [P, STEPS])
            iota_pi = sbp("iota_pi", [P, 1], i32)
            last_i = sbp("last_i", [1, GROUPS - 1], i32)
            last_f = sbp("last_f", [1, GROUPS - 1])
            below = sbp("below", [P, GROUPS - 1])
            thr = sbp("thr", [P, 1])
            g_of = sbp("g_of", [P, 1])
            s_of = sbp("s_of", [P, 1])
            passed = sbp("passed", [P, STEPS])
            blk = sbp("blk", [P, STEPS + 1])
            grp = sbp("grp", [P, STEPS + 1])
            off_f = sbp("off_f", [1, STEPS])
            ones = sbp("ones", [P, P])
            s_load, s_const, s_chain, s_idx = sem("pro_loads"), sem("pro_consts"), sem("pro_chain"), sem("pro_index_loads")
            s_tp, s_tc, s_u, s_wb, s_step, s_stepv = (sem("pro_wT"), sem("pro_wT_copied"), sem("pro_products"),
                                                      sem("pro_mats"), sem("pro_bcast"), sem("pro_step_in"))
            s_it, s_ic_s, s_ic_d = sem("pro_idx_transposed"), sem("pro_src_copied"), sem("pro_dst_copied")
            s_conv = sem("pro_idx_floats")
            FULL = (GROUPS - 1) * TILES
            KB, KR = FULL // P, FULL % P

            loads, idx_loads = [], []

            with nc.allow_non_contiguous_dma(reason="small weight and index layouts"), nc.Block() as block:
                @block.sync
                def _(sp):
                    n = [0, 0]

                    def load(dst, src_ap, which=0):
                        sp.dma_start(dst, src_ap).then_inc((s_load, s_idx)[which], 16)
                        n[which] += 1

                    for i, name in enumerate(("Wq", "Wk", "Wv", "Wke", "Wve")):
                        load(w_all[:, i, :].rearrange("f (h d) -> f h d", h=H), a[name].rearrange("h f d -> f h d"))
                    for h in range(H // 2):
                        rows = slice(D * h, D * h + D)
                        load(rel4[rows, 0:2, :], a["relk_W"].rearrange("(t d) e -> d t e", t=2))
                        load(rel4[rows, 2:4, :], a["relv_W"].rearrange("(t d) e -> d t e", t=2))
                        load(z4[rows, :], a["z_W"])
                        load(col[rows, 8:9], a["relv_g"].rearrange("(d o) -> d o", o=1))
                        load(col[rows, 9:10], a["relv_beta"].rearrange("(d o) -> d o", o=1))
                    for i, name in enumerate(("gke", "gk", "gve", "gv", "bke", "bk", "bve", "bv")):
                        load(col[:, i:i + 1], a[name].rearrange("h (d o) -> (h d) o", o=1))
                    for i, name in enumerate(("gq", "bq")):
                        load(qrows[:, i, :], a[name].rearrange("h d -> (h d)").partition_broadcast(P))
                    for i, name in enumerate(("relk_g", "relk_beta", "relk_b", "relv_b", "z_b", "z_g", "z_beta")):
                        load(rows16[:, i, :], a[name].partition_broadcast(P))
                    for i, (dst_t, name) in enumerate(((src_i, "src"), (dst_i, "dst"))):
                        load(dst_t[:, 0:KB, :], a[name][0:KB * P * P].rearrange("(k t e) -> t k e", t=P, e=P), 1)
                        load(dst_t[0:KR, KB, :], a[name][KB * P * P:FULL * P].rearrange("(t e) -> t e", e=P), 1)
                        load(dst_t[KR:KR + TILES, KB, :], a[name][TAIL0:E].rearrange("(t e) -> t e", e=P), 1)
                    load(last_i[0:1, :], a["dst"][0:(GROUPS - 1) * GE].rearrange("(g e) -> g e", e=GE)[:, GE - 1:GE]
                         .rearrange("g o -> o g"), 1)
                    loads.append(n[0] + 5 * (H // 2))
                    idx_loads.append(n[1])

                @block.gpsimd
                def _(pool):
                    nc.gpsimd.memset(ident[:], 0.0).then_inc(s_const, 1)
                    nc.gpsimd.memset(mask[:], 1.0).then_inc(s_const, 1)
                    nc.gpsimd.memset(ones[:], 1.0).then_inc(s_const, 1)
                    nc.gpsimd.memset(eps_c[:], EPS).then_inc(s_const, 1)
                    nc.gpsimd.memset(one_c[:], 1.0).then_inc(s_const, 1)
                    nc.gpsimd.iota(iota_i[:], pattern=[[1, STEPS]], base=0, channel_multiplier=0).then_inc(s_const, 1)
                    nc.gpsimd.iota(iota_pi[:], pattern=[[0, 1]], base=0, channel_multiplier=1).then_inc(s_const, 1)
                    pool.wait_ge(s_const, 7)
                    nc.gpsimd.affine_select(out=ident[:], in_=ident[:], compare_op=ALU.not_equal, fill=1.0, base=0,
                                            pattern=[[-1, P]], channel_multiplier=1).then_inc(s_const, 1)
                    m3 = mask[:].rearrange("p (h d) -> p h d", d=D)
                    nc.gpsimd.affine_select(out=m3, in_=m3, compare_op=ALU.is_ge, fill=0.0, base=0,
                                            pattern=[[-D, H], [0, D]], channel_multiplier=1).then_inc(s_const, 1)
                    pool.wait_ge(s_const, 9)
                    nc.gpsimd.affine_select(out=m3, in_=m3, compare_op=ALU.is_ge, fill=0.0, base=D - 1,
                                            pattern=[[D, H], [0, D]], channel_multiplier=-1).then_inc(s_const, 1)

                CONSTS = 10

                @block.vector
                def _(dve):
                    v = nc.vector
                    done = [0]

                    def link(ins):
                        done[0] += 1
                        ins.then_inc(s_chain, 1)
                        dve.wait_ge(s_chain, done[0])

                    dve.wait_ge(s_const, CONSTS)
                    dve.wait_ge(s_load, 16 * loads[0])
                    link(v.tensor_reduce(out=w_mean[:], in_=w_all[:].rearrange("p i (h d) -> p (i h) d", d=D), axis=AX.X, op=ALU.add))
                    link(v.tensor_scalar(out=w_mean[:], in0=w_mean[:], scalar1=1.0 / D, scalar2=None, op0=ALU.mult))
                    link(v.tensor_tensor(out=w_c[:].rearrange("p i (h d) -> p (i h) d", d=D),
                                         in0=w_all[:].rearrange("p i (h d) -> p (i h) d", d=D),
                                         in1=w_mean[:].unsqueeze(2).to_broadcast([P, 5 * H, D]), op=ALU.subtract))
                    link(v.tensor_reduce(out=rel_mean[:], in_=rel4[:], axis=AX.X, op=ALU.add))
                    link(v.tensor_scalar(out=rel_mean[:], in0=rel_mean[:], scalar1=1.0 / D, scalar2=None, op0=ALU.mult))
                    link(v.tensor_tensor(out=rel_c[:], in0=rel4[:], in1=rel_mean[:].unsqueeze(2).to_broadcast([P, 4, D]), op=ALU.subtract))
                    m3 = mask[:].rearrange("p (h d) -> p h d", d=D)
                    for i in range(4):
                        link(v.tensor_tensor(out=bd[:, i, :].rearrange("p (h d) -> p h d", d=D), in0=m3,
                                             in1=rel_c[:, i, :].unsqueeze(1).to_broadcast([P, H, D]), op=ALU.mult))
                        link(v.tensor_scalar(out=bdg[:, i, :], in0=bd[:, i, :], scalar1=col[:, i:i + 1], scalar2=None, op0=ALU.mult))
                        link(v.tensor_copy(out=colb[:, i, :], in_=col[:, 4 + i:5 + i].to_broadcast([P, F])))
                    link(v.tensor_tensor(out=zbd[:].rearrange("p (h d) -> p h d", d=D), in0=m3,
                                         in1=z4[:].unsqueeze(1).to_broadcast([P, H, D]), op=ALU.mult))
                    link(v.tensor_scalar(out=z_w[:], in0=zbd[:], scalar1=col[:, 8:9], scalar2=None, op0=ALU.mult))
                    link(v.tensor_copy(out=colb[:, 4, :], in_=col[:, 9:10].to_broadcast([P, F])))
                    v.tensor_copy(out=w_node[:, 0:3 * F], in_=w_c[:, 0:3, :].rearrange("p i n -> p (i n)")).then_inc(s_wb, 1)
                    v.tensor_copy(out=w_edge[:, 0:2 * F], in_=w_c[:, 3:5, :].rearrange("p i n -> p (i n)")).then_inc(s_wb, 1)
                    for dst_t, row, r16 in ((gq4, 0, RELKG), (bq4, 1, RELKG), (gqb, 0, RELKB), (tmp_q, 1, RELKB)):
                        link(v.tensor_tensor(out=dst_t[:].rearrange("p (h d) -> p h d", d=D),
                                             in0=qrows[:, row, :].rearrange("p (h d) -> p h d", d=D),
                                             in1=rows16[:, r16, :].unsqueeze(1).to_broadcast([P, H, D]), op=ALU.mult))
                        link(v.tensor_scalar(out=dst_t[:], in0=dst_t[:], scalar1=0.25, scalar2=None, op0=ALU.mult))
                    link(v.tensor_reduce(out=bqb[:], in_=tmp_q[:].rearrange("p (h d) -> p h d", d=D), axis=AX.X, op=ALU.add))
                    link(v.tensor_reduce(out=rb_mean[:], in_=rows16[:, RELKBIAS:RELVBIAS + 1, :], axis=AX.X, op=ALU.add))
                    link(v.tensor_scalar(out=rb_mean[:], in0=rb_mean[:], scalar1=1.0 / D, scalar2=None, op0=ALU.mult))
                    link(v.tensor_tensor(out=rb_c[:], in0=rows16[:, RELKBIAS:RELVBIAS + 1, :],
                                         in1=rb_mean[:].unsqueeze(2).to_broadcast([P, 2, D]), op=ALU.subtract))
                    dve.wait_ge(s_u, 2)
                    v.tensor_copy(out=w_node[:, 3 * F:5 * F], in_=bank[1][:, 0:2 * F]).then_inc(s_wb, 1)
                    v.tensor_copy(out=w_edge[:, 2 * F:4 * F], in_=bank[1][:, 2 * F:4 * F]).then_inc(s_wb, 1)
                    for i in range(2):
                        v.tensor_tensor(out=table_bias[:, i, :].rearrange("p (h d) -> p h d", d=D),
                                        in0=bank[2][:, i * F:(i + 1) * F].rearrange("p (h d) -> p h d", d=D),
                                        in1=rb_c[:, i, :].unsqueeze(1).to_broadcast([P, H, D]), op=ALU.add).then_inc(s_wb, 1)
                    v.tensor_copy(out=z_beta_w[:], in_=bank[2][:, 2 * F:3 * F]).then_inc(s_wb, 1)

                    dve.wait_ge(s_idx, 16 * idx_loads[0])
                    for rows_f, rows_i in ((src_f, src_i), (dst_f, dst_i)):
                        v.tensor_copy(out=rows_f[:, 0:KB, :], in_=rows_i[:, 0:KB, :]).then_inc(s_conv, 1)
                        v.tensor_copy(out=rows_f[0:KR + TILES, KB, :], in_=rows_i[0:KR + TILES, KB, :]).then_inc(s_conv, 1)
                    v.tensor_copy(out=last_f[:], in_=last_i[:]).then_inc(s_stepv, 1)
                    v.tensor_copy(out=iota_s[:], in_=iota_i[:]).then_inc(s_wb, 1)
                    v.tensor_copy(out=iota_n[:], in_=iota_i[:, 0:P]).then_inc(s_wb, 1)
                    link(v.tensor_copy(out=iota_p[:], in_=iota_pi[:]))
                    link(v.tensor_scalar(out=thr[:], in0=iota_p[:], scalar1=1.0, scalar2=float(P), op0=ALU.add, op1=ALU.mult))
                    dve.wait_ge(s_step, 1)
                    link(v.tensor_scalar(out=below[:], in0=bank[3][:, 0:GROUPS - 1], scalar1=thr[:, 0:1], scalar2=None, op0=ALU.is_lt))
                    link(v.tensor_reduce(out=g_of[:], in_=below[:], axis=AX.X, op=ALU.add))
                    link(v.tensor_scalar(out=s_of[:], in0=g_of[:], scalar1=iota_p[:, 0:1], scalar2=1.0, op0=ALU.add, op1=ALU.add))
                    v.tensor_scalar(out=passed[:], in0=iota_s[:], scalar1=s_of[:, 0:1], scalar2=None, op0=ALU.is_ge).then_inc(s_stepv, 1)
                    link(v.memset(blk[:, 0:1], -1.0))
                    link(v.memset(grp[:, 0:1], -1.0))
                    dve.wait_ge(s_step, 2)
                    link(v.tensor_copy(out=blk[:, 1:STEPS + 1], in_=bank[4][:, 0:STEPS]))
                    link(v.tensor_tensor(out=grp[:, 1:STEPS + 1], in0=iota_s[:], in1=blk[:, 1:STEPS + 1], op=ALU.subtract))
                    link(v.tensor_scalar(out=step_cols[:, :, 0], in0=blk[:, 1:STEPS + 1], scalar1=float(P), scalar2=None, op0=ALU.mult))
                    link(v.tensor_scalar(out=step_cols[:, :, 1], in0=step_cols[:, :, 0], scalar1=iota_p[:, 0:1], scalar2=-1.0,
                                         op0=ALU.add, op1=ALU.mult))
                    link(v.tensor_tensor(out=step_cols[:, :, 2], in0=blk[:, 1:STEPS + 1], in1=blk[:, 0:STEPS], op=ALU.is_equal))
                    link(v.tensor_tensor(out=step_cols[:, :, 3], in0=grp[:, 1:STEPS + 1], in1=grp[:, 0:STEPS], op=ALU.is_equal))
                    link(v.tensor_scalar(out=off_f[:], in0=grp[0:1, 1:STEPS + 1], scalar1=float(GE), scalar2=float(TAIL0),
                                         op0=ALU.mult, op1=ALU.min))
                    link(v.tensor_tensor(out=off_f[:], in0=off_f[:], in1=blk[0:1, 1:STEPS + 1], op=ALU.add))
                    link(v.tensor_copy(out=step_ints[:], in_=off_f[:]))

                    for k in range(KB + 1):
                        n = P if k < KB else KR + TILES
                        dve.wait_ge(s_it, k + 1)
                        v.tensor_copy(out=cols[:].bitcast(i32)[:, k * 32:k * 32 + n // TILES, 0:TILES],
                                      in_=bank[5 + k % 2][:, 0:n].rearrange("p (g j) -> p g j", j=TILES)).then_inc(s_ic_s, 1)
                    dve.wait_ge(s_ic_d, KB + 1)
                    for j in range(DUP // P):
                        link(v.memset(cols[:, GROUPS - 1, TILES + j:TILES + j + 1], 1.0e6))
                    link(v.memset(cols[0:DUP % P, GROUPS - 1, TILES + DUP // P:TILES + DUP // P + 1], 1.0e6))

                @block.scalar
                def _(act):
                    for h in range(H // 2, H):
                        rows = slice(D * h, D * h + D)
                        act.dma_start(rel4[rows, 0:2, :], a["relk_W"].rearrange("(t d) e -> d t e", t=2)).then_inc(s_load, 16)
                        act.dma_start(rel4[rows, 2:4, :], a["relv_W"].rearrange("(t d) e -> d t e", t=2)).then_inc(s_load, 16)
                        act.dma_start(z4[rows, :], a["z_W"]).then_inc(s_load, 16)
                        act.dma_start(col[rows, 8:9], a["relv_g"].rearrange("(d o) -> d o", o=1)).then_inc(s_load, 16)
                        act.dma_start(col[rows, 9:10], a["relv_beta"].rearrange("(d o) -> d o", o=1)).then_inc(s_load, 16)
                    nc.scalar.preload_act_table_set("natural_log_exp_and_others")
                    act.wait_ge(s_tp, 1)
                    nc.scalar.activation(w_ct[:].rearrange("p i n -> p (i n)"), bank[0][:], ACT.Copy).then_inc(s_tc, 1)
                    for k in range(KB + 1):
                        n = P if k < KB else KR + TILES
                        act.wait_ge(s_it, k + 1)
                        nc.scalar.activation(cols[:, k * 32:k * 32 + n // TILES, TILES:2 * TILES],
                                             bank[7 * (k % 2)][:, 0:n].rearrange("p (g j) -> p g j", j=TILES),
                                             ACT.Copy, scale=-1.0).then_inc(s_ic_d, 1)

                @block.tensor
                def _(pe):
                    pe.wait_ge(s_const, CONSTS)
                    pe.wait_ge(s_chain, 3)
                    for i in range(4):
                        last = nc.tensor.transpose(bank[0][:, i * F:(i + 1) * F], w_c[:, 1 + i, :], ident[:])
                    last.then_inc(s_tp, 1)
                    pe.wait_ge(s_tc, 1)
                    pe.wait_ge(s_chain, 3 + 3 + 12 + 3)
                    for i, m in enumerate((1, 3, 0, 2)):
                        last = nc.tensor.matmul(bank[1][:, i * F:(i + 1) * F], w_ct[:, i, :], bdg[:, m, :], start=True, stop=True)
                    last.then_inc(s_u, 1)
                    for i in range(2):
                        nc.tensor.matmul(bank[2][:, i * F:(i + 1) * F], colb[:, 2 * i, :], bd[:, 2 * i, :], start=True, stop=False)
                        nc.tensor.matmul(bank[2][:, i * F:(i + 1) * F], colb[:, 2 * i + 1, :], bd[:, 2 * i + 1, :], start=False, stop=True)
                    nc.tensor.matmul(bank[2][:, 2 * F:3 * F], colb[:, 4, :], zbd[:], start=True, stop=True).then_inc(s_u, 1)
                    pe.wait_ge(s_stepv, 1)
                    nc.tensor.matmul(bank[3][:, 0:GROUPS - 1], ones[0:1, :], last_f[:], start=True, stop=True).then_inc(s_step, 1)
                    pe.wait_ge(s_stepv, 2)
                    nc.tensor.matmul(bank[4][:, 0:STEPS], ones[0:BLOCKS - 1, :], passed[0:BLOCKS - 1, :], start=True, stop=True).then_inc(s_step, 1)
                    pe.wait_ge(s_conv, 4)
                    for k in range(KB + 1):
                        n = P if k < KB else KR + TILES
                        if k >= 2:
                            pe.wait_ge(s_ic_s, k - 1)
                            pe.wait_ge(s_ic_d, k - 1)
                        nc.tensor.transpose(bank[5 + k % 2][:, 0:n], src_f[0:n, k, :], ident[0:n, 0:n])
                        nc.tensor.transpose(bank[7 * (k % 2)][:, 0:n], dst_f[0:n, k, :], ident[0:n, 0:n]).then_inc(s_it, 1)

        q_split = sb_mid("q_split", [P, BLOCKS, 3 * QW], bf16)
        nodes(nc, a, sem, bank, dict(table=table, ident=ident, w_node=w_node, table_bias=table_bias, gq4=gq4, bq4=bq4,
                                     gqb=gqb, bqb=bqb, eps_c=eps_c, q_split=q_split))
        edges(nc, a, sem, banks, dict(table=table, sums_d=sums_d, qk_d=qk_d, ident=ident, iota_n=iota_n, w_edge=w_edge,
                                      cols=cols, step_cols=step_cols, step_ints=step_ints, eps_c=eps_c, q_split=q_split))
        mid.close()
        softmax(nc, a, sem, bank, dict(qk_d=qk_d, lse_d=lse_d, sums_d=sums_d, counts=counts, ident=ident, one_c=one_c))
        finish(nc, a, sem, bank, dict(sums_d=sums_d, lse_d=lse_d, counts=counts, ident=ident, z_w=z_w, z_beta_w=z_beta_w,
                                      rows16=rows16, eps_c=eps_c), out)


def nodes(nc, a, sem, bank, t):
    f32, bf16 = mybir.dt.float32, mybir.dt.bfloat16
    ALU, ACT, AX = mybir.AluOpType, mybir.ActivationFunctionType, mybir.AxisListType
    PAIRS, FIRST = BLOCKS // 2, 8
    assert PAIRS % 2 == 0 and BLOCKS % 2 == 1
    with ExitStack() as scope:
        def sb(name, shape, dt=f32):
            return scope.enter_context(nc.sbuf_tensor(name, shape, dt))

        xb = sb("n_x", [P, 2, 2, F])
        xt = sb("n_xt", [P, 2, 2, F])
        sq = sb("n_sq", [P, 2, 3 * F])
        var = sb("n_var", [P, 2, 3 * H])
        lnv = sb("n_lnv", [P, 2, 3 * H])
        rstd = sb("n_rstd", [P, 2, 2, 3 * H])
        tb = sb("n_tb", [P, 2, 2, 2, F])
        yh = sb("n_yh", [P, 2, 2, F])
        qt = sb("n_qt", [P, 2, F])
        q = sb("n_q", [P, 2, 2, QW])
        q1 = sb("n_q1", [P, 2, 2, QW])
        q2 = sb("n_q2", [P, 2, 2, QW])
        s_x = [sem(f"nodes_x{i}") for i in range(2)]
        s_st = [sem(f"nodes_stored{i}") for i in range(2)]
        s_xt, s_xc, s_pr, s_sq, s_var, s_ln, s_r = (sem("nodes_xT"), sem("nodes_xT_copied"), sem("nodes_projected"),
                                                    sem("nodes_squared"), sem("nodes_var"), sem("nodes_ln"), sem("nodes_rstd"))
        s_u, s_tb, s_yh, s_qg0, s_qg, s_t, s_qb0, s_q = (sem("nodes_scaled"), sem("nodes_table"), sem("nodes_yh"), sem("nodes_qg0"),
                                                         sem("nodes_qg"), sem("nodes_qt"), sem("nodes_qb0"), sem("nodes_q"))
        s_1, s_r1, s_2, s_r2, s_3, s_z = (sem("nodes_part1"), sem("nodes_rest1"), sem("nodes_part2"), sem("nodes_rest2"),
                                          sem("nodes_part3"), sem("nodes_zeroed"))
        q_split, table = t["q_split"], t["table"]
        proj = [[bank[3 * k + c] for c in range(3)] for k in range(2)]

        def every(eng, body, lag):
            for c in range(FIRST):
                body(c, 0, False)
            with eng.Fori(0, (PAIRS - FIRST) // 2) as i:
                for u in range(2):
                    body(FIRST + u, i, True)
            for c in range(PAIRS, PAIRS + 1 + lag):
                body(c, 0, False)

        def pair(x, i, loop):
            if not loop and not 0 <= x <= PAIRS:
                return None
            n = x + 2 * i
            return (n, x % 2, 2 * n, 2, P) if loop or x < PAIRS else (n, x % 2, BLOCKS - 1, 1, LAST)

        def use(x, i):
            return i + (x // 2 + 1)

        with nc.Block() as block:
            @block.sync
            def _(sp):
                def load(x, i, loop):
                    if pair(x, i, loop):
                        n, k, b, nb, rows = pair(x, i, loop)
                        if loop or x >= 2:
                            sp.wait_ge(s_xt, n - 1)
                        sp.dma_start(xb[0:rows, k, 0:nb, :],
                                     a["x"][bass.ds(P * b, nb * rows), :].rearrange("(b p) f -> p b f", p=rows)).then_inc(s_x[k], 16)

                def body(c, i, loop):
                    load(c, i, loop)
                    if pair(c - 3, i, loop):
                        n, k, b, nb, rows = pair(c - 3, i, loop)
                        sp.wait_ge(s_tb, n + 1)
                        sp.dma_start(table[bass.ds(P * b, nb * rows), :].rearrange("(b p) f -> p b f", p=rows),
                                     tb[0:rows, k, 0:nb, :, :].rearrange("p b t f -> p b (t f)")).then_inc(s_st[k], 16)
                every(sp, body, 3)
                sp.wait_ge(s_st[0], 16 * (PAIRS // 2 + 1))
                sp.wait_ge(s_st[1], 16 * (PAIRS // 2))

            @block.tensor
            def _(pe):
                def body(c, i, loop):
                    if pair(c - 1, i, loop):
                        x = c - 1
                        n, k, b, nb, rows = pair(x, i, loop)
                        pe.wait_ge(s_xc, n + 1)
                        if loop or x >= 2:
                            pe.wait_ge(s_u, n - 1)
                            pe.wait_ge(s_yh, n - 1)
                        for c2 in range(nb):
                            nc.tensor.matmul(proj[k][c2][0:rows, :], xt[:, k, c2, 0:rows], t["w_node"][:, 0:4 * F], start=True, stop=True)
                            last = nc.tensor.matmul(proj[k][2][0:rows, c2 * F:(c2 + 1) * F], xt[:, k, c2, 0:rows], t["w_node"][:, 4 * F:5 * F],
                                                    start=True, stop=True)
                        last.then_inc(s_pr, 1)
                    if pair(c, i, loop):
                        n, k, b, nb, rows = pair(c, i, loop)
                        pe.wait_ge(s_x[k], 16 * use(c, i))
                        if loop or c >= 1:
                            pe.wait_ge(s_xc, n)
                        for c2 in range(nb):
                            last = nc.tensor.transpose(bank[6][:, c2 * F:c2 * F + rows], xb[0:rows, k, c2, :], t["ident"][0:rows, 0:rows])
                        last.then_inc(s_xt, 1)
                every(pe, body, 1)

            @block.scalar
            def _(act):
                def part(x, i, loop, s_in, src, col, s_out):
                    if pair(x, i, loop):
                        n, k, b, nb, rows = pair(x, i, loop)
                        act.wait_ge(s_z, 1)
                        act.wait_ge(s_in, n + 1)
                        nc.scalar.activation(q_split[0:rows, bass.ds(b, nb), col * QW:(col + 1) * QW], src[0:rows, k, 0:nb, :],
                                             ACT.Copy).then_inc(s_out, 1)

                def body(c, i, loop):
                    if pair(c - 2, i, loop):
                        x = c - 2
                        n, k, b, nb, rows = pair(x, i, loop)
                        act.wait_ge(s_var, n + 1)
                        if loop or x >= 1:
                            act.wait_ge(s_r, n)
                        nc.scalar.activation(lnv[0:rows, 0:nb, :], var[0:rows, 0:nb, :], ACT.Ln, bias=t["eps_c"][0:rows, 0:1], scale=1.0 / D).then_inc(s_ln, 1)
                        act.wait_ge(s_ln, n + 1)
                        if loop or x >= 2:
                            act.wait_ge(s_u, n - 1)
                            act.wait_ge(s_yh, n - 1)
                        nc.scalar.activation(rstd[0:rows, k, 0:nb, :], lnv[0:rows, 0:nb, :], ACT.Exp, scale=-0.5).then_inc(s_r, 1)
                    if pair(c - 1, i, loop):
                        x = c - 1
                        n, k, b, nb, rows = pair(x, i, loop)
                        act.wait_ge(s_pr, n + 1)
                        if loop or x >= 1:
                            act.wait_ge(s_var, n)
                        for c2 in range(nb):
                            last = nc.scalar.activation(sq[0:rows, c2, :], proj[k][c2][0:rows, 0:3 * F], ACT.Square)
                        last.then_inc(s_sq, 1)
                    if pair(c, i, loop):
                        n, k, b, nb, rows = pair(c, i, loop)
                        act.wait_ge(s_xt, n + 1)
                        if loop or c >= 2:
                            act.wait_ge(s_pr, n - 1)
                        nc.scalar.activation(xt[:, k, 0:nb, 0:rows], bank[6][:, 0:nb * F].rearrange("p (c n) -> p c n", c=nb)[:, :, 0:rows],
                                             ACT.Copy).then_inc(s_xc, 1)
                    part(c - 5, i, loop, s_r2, q2, 2, s_3)
                    part(c - 4, i, loop, s_r1, q1, 1, s_2)
                    part(c - 3, i, loop, s_q, q, 0, s_1)
                every(act, body, 5)

            @block.gpsimd
            def _(pool):
                def body(c, i, loop):
                    if pair(c - 2, i, loop):
                        n, k, b, nb, rows = pair(c - 2, i, loop)
                        pool.wait_ge(s_u, n + 1)
                        nc.gpsimd.tensor_tensor(out=tb[0:rows, k, 0:nb, :, :], in0=tb[0:rows, k, 0:nb, :, :],
                                                in1=t["table_bias"][0:rows].unsqueeze(1).to_broadcast([rows, nb, 2, F]), op=ALU.add).then_inc(s_tb, 1)
                every(pool, body, 2)

            @block.vector
            def _(dve):
                v = nc.vector
                v.memset(q_split[:, BLOCKS - 1, :], 0.0).then_inc(s_z, 1)
                h3 = lambda ap: ap.rearrange("p (h d) -> p h d", d=D)

                def rest(x, i, loop, whole, part, s_part, out, s_out, s_used):
                    if pair(x, i, loop):
                        n, k, b, nb, rows = pair(x, i, loop)
                        dve.wait_ge(s_part, n + 1)
                        if loop or x >= 2:
                            dve.wait_ge(s_used, n - 1)
                        v.tensor_tensor(out=out[0:rows, k, 0:nb, :], in0=whole[0:rows, k, 0:nb, :],
                                        in1=q_split[0:rows, bass.ds(b, nb), part * QW:(part + 1) * QW], op=ALU.subtract).then_inc(s_out, 1)

                def body(c, i, loop):
                    if pair(c - 4, i, loop):
                        dve.wait_ge(s_q, pair(c - 4, i, loop)[0] + 1)
                    rest(c - 4, i, loop, q, 0, s_1, q1, s_r1, s_r2)
                    if pair(c - 5, i, loop):
                        dve.wait_ge(s_r1, pair(c - 5, i, loop)[0] + 1)
                    rest(c - 5, i, loop, q1, 1, s_2, q2, s_r2, s_3)
                    x = c - 3
                    if pair(x, i, loop):
                        n, k, b, nb, rows = pair(x, i, loop)
                        rep = lambda tt: tt[0:rows, :].unsqueeze(1).to_broadcast([rows, nb, F])
                        dve.wait_ge(s_yh, n + 1)
                        if loop or x >= 1:
                            dve.wait_ge(s_qb0, n)
                        v.tensor_tensor(out=qt[0:rows, 0:nb, :], in0=yh[0:rows, k, 0:nb, :], in1=rep(t["gqb"]), op=ALU.mult).then_inc(s_t, 1)
                        if loop or x >= 2:
                            dve.wait_ge(s_1, n - 1)
                            dve.wait_ge(s_r1, n - 1)
                        v.tensor_tensor(out=q[0:rows, k, 0:nb, 0:F], in0=yh[0:rows, k, 0:nb, :], in1=rep(t["gq4"]), op=ALU.mult).then_inc(s_qg0, 1)
                        dve.wait_ge(s_t, n + 1)
                        v.tensor_reduce(out=q[0:rows, k, 0:nb, F:QW], in_=qt[0:rows, 0:nb, :].rearrange("p b (h d) -> p b h d", d=D),
                                        axis=AX.X, op=ALU.add).then_inc(s_qb0, 1)
                        dve.wait_ge(s_qg0, n + 1)
                        v.tensor_tensor(out=q[0:rows, k, 0:nb, 0:F], in0=q[0:rows, k, 0:nb, 0:F], in1=rep(t["bq4"]), op=ALU.add).then_inc(s_qg, 1)
                        dve.wait_ge(s_qb0, n + 1)
                        dve.wait_ge(s_qg, n + 1)
                        v.tensor_tensor(out=q[0:rows, k, 0:nb, F:QW], in0=q[0:rows, k, 0:nb, F:QW],
                                        in1=t["bqb"][0:rows, :].unsqueeze(1).to_broadcast([rows, nb, H]), op=ALU.add).then_inc(s_q, 1)
                    x = c - 2
                    if pair(x, i, loop):
                        n, k, b, nb, rows = pair(x, i, loop)
                        dve.wait_ge(s_r, n + 1)
                        if loop or x >= 2:
                            dve.wait_ge(s_st[k], 16 * (use(x, i) - 1))
                        for c2 in range(nb):
                            v.tensor_tensor(out=h3(tb[0:rows, k, c2, 0, :]), in0=h3(proj[k][c2][0:rows, 3 * F:4 * F]),
                                            in1=rstd[0:rows, k, c2, H:2 * H].unsqueeze(2).to_broadcast([rows, H, D]), op=ALU.mult)
                            last = v.tensor_tensor(out=h3(tb[0:rows, k, c2, 1, :]), in0=h3(proj[k][2][0:rows, c2 * F:(c2 + 1) * F]),
                                                   in1=rstd[0:rows, k, c2, 2 * H:3 * H].unsqueeze(2).to_broadcast([rows, H, D]), op=ALU.mult)
                        last.then_inc(s_u, 1)
                        if loop or x >= 2:
                            dve.wait_ge(s_qg0, n - 1)
                        for c2 in range(nb):
                            last = v.tensor_tensor(out=h3(yh[0:rows, k, c2, :]), in0=h3(proj[k][c2][0:rows, 0:F]),
                                                   in1=rstd[0:rows, k, c2, 0:H].unsqueeze(2).to_broadcast([rows, H, D]), op=ALU.mult)
                        last.then_inc(s_yh, 1)
                    x = c - 1
                    if pair(x, i, loop):
                        n, k, b, nb, rows = pair(x, i, loop)
                        dve.wait_ge(s_sq, n + 1)
                        if loop or x >= 1:
                            dve.wait_ge(s_ln, n)
                        v.tensor_reduce(out=var[0:rows, 0:nb, :], in_=sq[0:rows, 0:nb, :].rearrange("p b (h d) -> p b h d", d=D),
                                        axis=AX.X, op=ALU.add).then_inc(s_var, 1)
                every(dve, body, 5)


def edges(nc, a, sem, banks, t):
    f32, bf16, i32, u32 = mybir.dt.float32, mybir.dt.bfloat16, mybir.dt.int32, mybir.dt.uint32
    ALU, ACT, AX = mybir.AluOpType, mybir.ActivationFunctionType, mybir.AxisListType
    table, sums_d, qk_d, ident, step_cols = t["table"], t["sums_d"], t["qk_d"], t["ident"], t["step_cols"]
    with ExitStack() as scope:
        def sb(name, shape, dt=f32):
            return scope.enter_context(nc.sbuf_tensor(name, shape, dt))

        ea = sb("e_ea", [P, RING, TILES, F])
        dstb = sb("e_dstb", [P, RING, GE], i32)
        qb = sb("e_q", [P, UNROLL, 3 * QW], bf16)
        gcol = sb("e_gcol", [P, UNROLL, 2 * TILES])
        eat = sb("e_eat", [P, RING, GE])
        ysq = sb("e_ysq", [P, 2, TILES, 2 * F])
        yvar = sb("e_yvar", [P, TILES, 2 * H])
        yln = sb("e_yln", [P, TILES, 2 * H])
        yr = sb("e_yr", [P, 2, TILES, 2 * H])
        p = sb("e_p", [P, RING, TILES, 2 * F])
        z = sb("e_z", [P, 2, TILES, 3 * F])
        zs = sb("e_zs", [P, 2, TILES, 3 * H])
        zln = sb("e_zln", [P, TILES, 2 * H])
        zr = sb("e_zr", [P, 2, TILES, 2 * H])
        qk0 = sb("e_qk0", [P, TILES, H])
        w2 = sb("e_w2", [P, TILES, H])
        beta = sb("e_beta", [P, 2, TILES, H])
        hh = sb("e_h", [P, 2, TILES, AW])
        zero_c = sb("e_zero", [P, 1])
        ob = sb("e_ob", [P, 2, 1])
        oht_a = sb("e_oht_a", [P, GE])
        oht = sb("e_oht", [P, 2, GE], bf16)
        rel = sb("e_rel", [P, 2, TILES])
        oh_a = sb("e_oh_a", [P, TILES, P])
        oh = sb("e_oh", [P, RING, TILES, P])
        run = sb("e_run", [P, RING, AW])
        qkr = sb("e_qkr", [P, RING, TILES * H])
        qkt = sb("e_qkt", [TILES * H, RING, P])
        y_ps, u_ps = [banks[:, h, :] for h in range(2)], [banks[:, 2 + h, :] for h in range(2)]
        eat_ps, qx_ps, agg_ps = banks[:, 4, :], banks[:, 5:7, 0:2 * QW], banks[:, 7, 0:AW]
        qkt_ps = banks[0:TILES * H, 7, AW:AW + P]
        qx4 = qx_ps.rearrange("p b (t c) -> p b t c", c=QW)
        tiles4 = lambda ap: ap.rearrange("p (b t) c -> p b t c", b=2)

        s_ea = [sem(f"ea_loaded{i}") for i in range(RING)]
        s_in = [sem(f"cols_q_dst_loaded{i}") for i in range(RING)]
        s_ga = [sem(f"gathered{i}") for i in range(RING)]
        s_sums_st, s_qk_st = sem("sums_stored"), sem("qk_stored")
        s_tr, s_eat = sem("ea_transposed"), sem("eat_copied")
        s_y = [sem(f"y_projected{i}") for i in range(2)]
        s_ysq = [sem(f"y_squared{i}") for i in range(2)]
        s_u = [sem(f"u_projected{i}") for i in range(2)]
        s_p = [sem(f"p_scaled{i}") for i in range(2)]
        s_yv, s_yl, s_yr = sem("y_summed"), sem("y_ln"), sem("y_rstd")
        s_psq, s_pq, s_z, s_zl, s_zr = sem("p_squared"), sem("pq_ready"), sem("z_summed"), sem("z_ln"), sem("z_rstd")
        s_qk0, s_qk, s_w2, s_qkr = sem("qk_dot"), sem("qk_ready"), sem("w2_ready"), sem("qk_run_ready")
        s_h1, s_h2, s_agg, s_run = sem("h1_ready"), sem("h2_ready"), sem("summed_to_nodes"), sem("run_ready")
        s_qkt, s_qktc = sem("qk_transposed"), sem("qkt_copied")
        s_ob, s_oha, s_oht, s_qx = sem("oht_bias"), sem("oht_abs"), sem("oht_ready"), sem("q_expanded")
        s_beta, s_rel, s_ohb, s_oh, s_init = sem("beta_copied"), sem("rel_ready"), sem("oh_abs"), sem("oh_ready"), sem("edges_init")

        def every(eng, body, last):
            for c in range(PEEL):
                body(c, 0, False)
            turns = (STEPS - 1 - PEEL) // UNROLL
            with eng.Fori(0, turns) as i:
                for u in range(UNROLL):
                    body(PEEL + u, i, True)
            for c in range(PEEL + UNROLL * turns, last):
                body(c, 0, False)

        def use(x, i):
            return (UNROLL // RING) * i + (x // RING + 1)

        def is_step(x, loop):
            return loop or 0 <= x < STEPS

        with nc.Block() as block:
            @block.sync
            def _(sp):
                r_b, r_e0, r_g, r_n1, r_16n, r_back = (sp.alloc_register(f"sp_{name}") for name in ("block", "edge", "group", "n1", "n16", "back"))

                def entry(n, edge):
                    bounded = lambda reg, top: sp.snap(reg, min_val=0, max_val=top)
                    v = sp.value_load(t["step_ints"][0:1, bass.ds(n, 1)], min_val=0, max_val=TAIL0 + 63)
                    sp.reg_alu(r_b, v, 63, ALU.bitwise_and)
                    sp.reg_alu(r_g, v, GE - 64, ALU.add)
                    sp.reg_alu(r_g, r_g, 9, ALU.logical_shift_right)
                    if edge:
                        sp.reg_alu(r_e0, v, r_b, ALU.subtract)
                    return bounded(r_b, BLOCKS - 1), bounded(r_g, GROUPS - 1), bounded(r_e0, TAIL0) if edge else None

                def body(c, i, loop):
                    if is_step(c, loop):
                        n, k = UNROLL * i + c, c % RING
                        again = loop or c >= RING
                        b, g, e0 = entry(n, True)
                        if loop:
                            sp.reg_alu(r_back, n, UNROLL - 1, ALU.subtract)
                        back = r_back if loop else n - UNROLL + 1
                        if again:
                            sp.wait_ge(s_tr, n - RING + 1)
                        sp.dma_start(ea[:, k, :, :],
                                     a["edge_attr_128"][bass.ds(e0, GE), :].rearrange("(j p) f -> p j f", p=P)).then_inc(s_ea[k], 16)
                        if again:
                            sp.wait_ge(s_oht, n - RING + 1)
                        if loop or c >= UNROLL:
                            sp.wait_ge(s_ga[k], 64 * use(c - UNROLL, i))
                            sp.wait_ge(s_rel, back)
                        sp.dma_start(gcol[:, c % UNROLL, :], t["cols"][:, bass.ds(g, 1), :].rearrange("p o c -> p (o c)")).then_inc(s_in[k], 16)
                        if loop or c >= UNROLL:
                            sp.wait_ge(s_qx, back)
                        sp.dma_start(qb[:, c % UNROLL, :], t["q_split"][:, bass.ds(b, 1), :].rearrange("p o c -> p (o c)")).then_inc(s_in[k], 16)
                        sp.dma_start(dstb[:, k, :], a["dst"][bass.ds(e0, GE)].partition_broadcast(P)).then_inc(s_in[k], 16)
                    x = c - STORE_LAG
                    if is_step(x, loop):
                        n, k = UNROLL * i + x, x % RING
                        b, g, _ = entry(n, False)
                        if loop:
                            sp.reg_alu(r_n1, n, 1, ALU.add)
                            sp.reg_alu(r_16n, n, 16, ALU.mult)
                        sp.wait_ge(s_sums_st, r_16n if loop else 16 * n)
                        sp.wait_ge(s_run, r_n1 if loop else n + 1)
                        sp.dma_start(sums_d[bass.ds(b, 1), :, :].rearrange("o p c -> p (o c)"), run[:, k, :]).then_inc(s_sums_st, 16)
                        sp.wait_ge(s_qk_st, r_16n if loop else 16 * n)
                        sp.wait_ge(s_qktc, r_n1 if loop else n + 1)
                        sp.dma_start(qk_d[bass.ds(g, 1), :, :].rearrange("o r e -> r (o e)"), qkt[:, k, :]).then_inc(s_qk_st, 16)
                every(sp, body, STEPS + STORE_LAG)
                sp.wait_ge(s_sums_st, 16 * STEPS)
                sp.wait_ge(s_qk_st, 16 * STEPS)

            @block.tensor
            def _(pe):
                def project(x, i, loop, cols, out_ps, s_out, s_used):
                    n = UNROLL * i + x
                    for half in range(2):
                        if loop or x >= 1:
                            pe.wait_ge(s_used[half], n)
                        for k in range(2):
                            last = nc.tensor.matmul(out_ps[half][:, k * 2 * F:(k + 1) * 2 * F], eat[:, x % RING, (2 * half + k) * P:(2 * half + k + 1) * P],
                                                    t["w_edge"][:, cols], start=True, stop=True)
                        last.then_inc(s_out[half], 1)

                def body(c, i, loop):
                    if is_step(c, loop):
                        n, k = UNROLL * i + c, c % RING
                        pe.wait_ge(s_ea[k], 16 * use(c, i))
                        if loop or c >= 1:
                            pe.wait_ge(s_eat, n)
                        for j in range(TILES):
                            last = nc.tensor.transpose(eat_ps[:, j * P:(j + 1) * P], ea[:, k, j, :], ident[:])
                        last.then_inc(s_tr, 1)
                    if is_step(c - 1, loop):
                        pe.wait_ge(s_eat, UNROLL * i + c)
                        project(c - 1, i, loop, slice(0, 2 * F), y_ps, s_y, s_ysq)
                    x = c - 9
                    if is_step(x, loop):
                        n = UNROLL * i + x
                        pe.wait_ge(s_qkr, n + 1)
                        pe.wait_ge(s_run, n + 1)
                        nc.tensor.transpose(qkt_ps, qkr[:, x % RING, :], ident[:]).then_inc(s_qkt, 1)
                    if is_step(c - 3, loop):
                        project(c - 3, i, loop, slice(2 * F, 4 * F), u_ps, s_u, s_p)
                    x = c - 8
                    if is_step(x, loop):
                        n = UNROLL * i + x
                        pe.wait_ge(s_h1, n + 1)
                        pe.wait_ge(s_h2, n + 1)
                        pe.wait_ge(s_oh, n + 1)
                        if loop or x >= 1:
                            pe.wait_ge(s_qktc, n)
                        for j in range(TILES):
                            last = nc.tensor.matmul(agg_ps, oh[:, x % RING, j, :], hh[:, x % 2, j, :], start=(j == 0), stop=(j == TILES - 1))
                        last.then_inc(s_agg, 1)
                    x = c - 5
                    if is_step(x, loop):
                        n, k = UNROLL * i + x, x % RING
                        pe.wait_ge(s_oht, n + 1)
                        pe.wait_ge(s_in[k], 48 * use(x, i))
                        if loop or x >= 1:
                            pe.wait_ge(s_beta, n)
                        for j in range(TILES):
                            for part in range(3):
                                last = nc.tensor.matmul(qx4[:, j // 2, j % 2, :], oht[:, x % 2, j * P:(j + 1) * P],
                                                        qb[:, x % UNROLL, part * QW:(part + 1) * QW], start=(part == 0), stop=(part == 2))
                        last.then_inc(s_qx, 1)
                every(pe, body, STEPS + 9)

            @block.scalar
            def _(act):
                def body(c, i, loop):
                    x = c - 5
                    if is_step(x, loop):
                        n, k = UNROLL * i + x, x % RING
                        act.wait_ge(s_ga[k], 64 * use(x, i))
                        if loop or x >= 2:
                            act.wait_ge(s_z, n - 1)
                        nc.scalar.activation(z[:, x % 2, :, 0:2 * F], p[:, k, :, :], ACT.Square).then_inc(s_psq, 1)
                    x = c - 1
                    if is_step(x, loop):
                        n = UNROLL * i + x
                        for half in range(2):
                            act.wait_ge(s_y[half], n + 1)
                            if half == 0 and (loop or x >= 2):
                                act.wait_ge(s_yv, n - 1)
                            nc.scalar.activation(ysq[:, x % 2, 2 * half:2 * half + 2, :].rearrange("p t c -> p (t c)"), y_ps[half],
                                                 ACT.Square).then_inc(s_ysq[half], 1)
                    if is_step(c, loop):
                        n = UNROLL * i + c
                        act.wait_ge(s_tr, n + 1)
                        if loop or c >= RING:
                            act.wait_ge(s_u[1], n - RING + 1)
                        nc.scalar.activation(eat[:, c % RING, :], eat_ps, ACT.Copy).then_inc(s_eat, 1)
                    x = c - 6
                    if is_step(x, loop):
                        n = UNROLL * i + x
                        act.wait_ge(s_pq, n + 1)
                        if loop or x >= 2:
                            act.wait_ge(s_qk, n - 1)
                        nc.scalar.activation(tiles4(beta[:, x % 2, :, :]), qx4[:, :, :, F:QW], ACT.Copy).then_inc(s_beta, 1)
                    x = c - 9
                    if is_step(x, loop):
                        n = UNROLL * i + x
                        act.wait_ge(s_qkt, n + 1)
                        if loop or x >= RING:
                            act.wait_ge(s_qk_st, 16 * (n - RING + 1))
                        nc.scalar.activation(qkt[:, x % RING, :], qkt_ps, ACT.Copy).then_inc(s_qktc, 1)
                    x2, x4 = c - 2, c - 4
                    if is_step(x4, loop):
                        n, k = UNROLL * i + x4, x4 % RING
                        act.wait_ge(s_in[k], 48 * use(x4, i))
                        act.wait_ge(s_ob, n + 1)
                        if loop or x4 >= 1:
                            act.wait_ge(s_oht, n)
                        nc.scalar.activation(oht_a[:], dstb[:, k, :], ACT.Abs, bias=ob[:, x4 % 2, :]).then_inc(s_oha, 1)
                    if is_step(x2, loop):
                        act.wait_ge(s_yv, UNROLL * i + x2 + 1)
                        if loop or x2 >= 1:
                            act.wait_ge(s_yr, UNROLL * i + x2)
                        nc.scalar.activation(yln[:], yvar[:], ACT.Ln, bias=t["eps_c"][:, 0:1], scale=1.0 / D).then_inc(s_yl, 1)
                    if is_step(x4, loop):
                        n = UNROLL * i + x4
                        act.wait_ge(s_oha, n + 1)
                        if loop or x4 >= 2:
                            act.wait_ge(s_qx, n - 1)
                        nc.scalar.activation(oht[:, x4 % 2, :], oht_a[:], ACT.Relu, bias=1.0, scale=-1.0).then_inc(s_oht, 1)
                    if is_step(x2, loop):
                        n = UNROLL * i + x2
                        act.wait_ge(s_yl, n + 1)
                        if loop or x2 >= 2:
                            act.wait_ge(s_p[1], n - 1)
                        nc.scalar.activation(yr[:, x2 % 2, :, :], yln[:], ACT.Exp, scale=-0.5).then_inc(s_yr, 1)
                    x = c - 5
                    if is_step(x, loop):
                        n = UNROLL * i + x
                        act.wait_ge(s_rel, n + 1)
                        if loop or x >= 1:
                            act.wait_ge(s_oh, n)
                        for j in range(TILES):
                            nc.scalar.activation(oh_a[:, j, :], t["iota_n"][:], ACT.Abs, bias=rel[:, x % 2, j:j + 1]).then_inc(s_ohb, 1)
                    x = c - 6
                    if is_step(x, loop):
                        act.wait_ge(s_z, UNROLL * i + x + 1)
                        if loop or x >= 1:
                            act.wait_ge(s_zr, UNROLL * i + x)
                        nc.scalar.activation(zln[:], zs[:, x % 2, :, 0:2 * H], ACT.Ln, bias=t["eps_c"][:, 0:1], scale=1.0 / D).then_inc(s_zl, 1)
                    x = c - 5
                    if is_step(x, loop):
                        n = UNROLL * i + x
                        act.wait_ge(s_ohb, TILES * (n + 1))
                        if loop or x >= RING:
                            act.wait_ge(s_agg, n - RING + 1)
                        nc.scalar.activation(oh[:, x % RING, :, :], oh_a[:], ACT.Relu, bias=1.0, scale=-1.0).then_inc(s_oh, 1)
                    x = c - 6
                    if is_step(x, loop):
                        n = UNROLL * i + x
                        act.wait_ge(s_zl, n + 1)
                        if loop or x >= 2:
                            act.wait_ge(s_w2, n - 1)
                            act.wait_ge(s_h1, n - 1)
                        nc.scalar.activation(zr[:, x % 2, :, :], zln[:], ACT.Exp, scale=-0.5).then_inc(s_zr, 1)
                every(act, body, STEPS + 9)

            @block.gpsimd
            def _(pool):
                last_node = pool.alloc_register("last_node")
                nodes_less_2 = pool.to_reg(N - 2)

                def gather(half, x, i):
                    k = x % RING
                    pool.wait_ge(s_p[half], UNROLL * i + x + 1)
                    pool.reg_add(last_node, nodes_less_2, 1)
                    for j in (2 * half, 2 * half + 1):
                        pool.indirect_dma_start(out=p[:, k, j, :], out_offset=None, in_=table,
                                                in_offset=bass.IndirectOffsetOnAxis(ap=gcol[:, x % UNROLL, j:j + 1].bitcast(u32), axis=0),
                                                bounds_check=last_node, oob_is_err=True, compute_op=ALU.add).then_inc(s_ga[k], 16)

                def body(c, i, loop):
                    x = c - 4
                    if is_step(x, loop):
                        pool.wait_ge(s_in[x % RING], 48 * use(x, i))
                        gather(0, x, i)
                        gather(1, x, i)
                    x = c - 7
                    if is_step(x, loop):
                        n, k = UNROLL * i + x, x % RING
                        pool.wait_ge(s_ga[k], 64 * use(x, i))
                        pool.wait_ge(s_zr, n + 1)
                        if loop or x >= 2:
                            pool.wait_ge(s_agg, n - 1)
                        nc.gpsimd.tensor_tensor(out=hh[:, x % 2, :, 0:F].rearrange("p t (h d) -> p t h d", d=D),
                                                in0=p[:, k, :, F:2 * F].rearrange("p t (h d) -> p t h d", d=D),
                                                in1=zr[:, x % 2, :, H:2 * H].unsqueeze(3).to_broadcast([P, TILES, H, D]), op=ALU.mult).then_inc(s_h1, 1)
                every(pool, body, STEPS + 7)

            @block.vector
            def _(dve):
                v = nc.vector
                heads = lambda ap: ap.rearrange("p t (h d) -> p t h d", d=D)
                v.memset(hh[:, :, :, AW - 1:AW], 1.0).then_inc(s_init, 1)
                v.memset(run[:, RING - 1, :], 0.0).then_inc(s_init, 1)
                v.memset(qkr[:, RING - 1, :], 0.0).then_inc(s_init, 1)
                v.memset(zero_c[:], 0.0).then_inc(s_init, 1)
                dve.wait_ge(s_init, 4)

                def step_col(n, k):
                    return step_cols[:, bass.ds(n, 1), k]

                def body(c, i, loop):
                    x = c - 9
                    if is_step(x, loop):
                        n = UNROLL * i + x
                        dve.wait_ge(s_agg, n + 1)
                        if loop or x >= 1:
                            dve.wait_ge(s_run, n)
                        if loop or x >= RING:
                            dve.wait_ge(s_sums_st, 16 * (n - RING + 1))
                        v.scalar_tensor_tensor(out=run[:, x % RING, :], in0=run[:, (x - 1) % RING, :],
                                               scalar=step_col(n, 2), in1=agg_ps, op0=ALU.mult, op1=ALU.add).then_inc(s_run, 1)
                    x = c - 6
                    if is_step(x, loop):
                        n, k = UNROLL * i + x, x % RING
                        dve.wait_ge(s_ga[k], 64 * use(x, i))
                        dve.wait_ge(s_qx, n + 1)
                        if loop or x >= 2:
                            dve.wait_ge(s_z, n - 1)
                        v.tensor_tensor(out=tiles4(z[:, x % 2, :, 2 * F:3 * F]), in0=tiles4(p[:, k, :, 0:F]),
                                        in1=qx4[:, :, :, 0:F], op=ALU.mult).then_inc(s_pq, 1)
                    x = c - 2
                    if is_step(x, loop):
                        n = UNROLL * i + x
                        dve.wait_ge(s_ysq[0], n + 1)
                        dve.wait_ge(s_ysq[1], n + 1)
                        if loop or x >= 1:
                            dve.wait_ge(s_yl, n)
                        v.tensor_reduce(out=yvar[:], in_=heads(ysq[:, x % 2, :, :]), axis=AX.X, op=ALU.add).then_inc(s_yv, 1)
                    x = c - 6
                    if is_step(x, loop):
                        n = UNROLL * i + x
                        dve.wait_ge(s_psq, n + 1)
                        dve.wait_ge(s_pq, n + 1)
                        if loop or x >= 2:
                            dve.wait_ge(s_zl, n - 1)
                            dve.wait_ge(s_qk0, n - 1)
                        v.tensor_reduce(out=zs[:, x % 2, :, :], in_=heads(z[:, x % 2, :, :]), axis=AX.X, op=ALU.add).then_inc(s_z, 1)
                    x = c - 7
                    if is_step(x, loop):
                        n = UNROLL * i + x
                        dve.wait_ge(s_zr, n + 1)
                        dve.wait_ge(s_z, n + 1)
                        if loop or x >= 1:
                            dve.wait_ge(s_qk, n)
                        v.tensor_tensor(out=qk0[:], in0=zs[:, x % 2, :, 2 * H:3 * H], in1=zr[:, x % 2, :, 0:H], op=ALU.mult).then_inc(s_qk0, 1)
                    x = c - 4
                    if is_step(x, loop):
                        n, k = UNROLL * i + x, x % RING
                        dve.wait_ge(s_in[k], 48 * use(x, i))
                        if loop or x >= 2:
                            dve.wait_ge(s_ohb, TILES * (n - 1))
                        v.tensor_scalar(out=rel[:, x % 2, :], in0=gcol[:, x % UNROLL, TILES:2 * TILES], scalar1=step_col(n, 0),
                                        scalar2=None, op0=ALU.add).then_inc(s_rel, 1)
                    x = c - 7
                    if is_step(x, loop):
                        n = UNROLL * i + x
                        h = hh[:, x % 2, :, :]
                        dve.wait_ge(s_qk0, n + 1)
                        dve.wait_ge(s_beta, n + 1)
                        if loop or x >= 2:
                            dve.wait_ge(s_agg, n - 1)
                        v.tensor_tensor(out=h[:, :, 2 * F:2 * F + H], in0=qk0[:], in1=beta[:, x % 2, :, :], op=ALU.add).then_inc(s_qk, 1)
                    x = c - 3
                    if is_step(x, loop):
                        n = UNROLL * i + x
                        if loop or x >= 2:
                            dve.wait_ge(s_oha, n - 1)
                        v.tensor_scalar(out=ob[:, x % 2, :], in0=zero_c[:], scalar1=step_col(n, 1), scalar2=None, op0=ALU.add).then_inc(s_ob, 1)
                    x = c - 7
                    if is_step(x, loop):
                        n = UNROLL * i + x
                        h = hh[:, x % 2, :, :]
                        dve.wait_ge(s_qk, n + 1)
                        if loop or x >= 1:
                            dve.wait_ge(s_h2, n)
                        v.tensor_tensor(out=w2[:], in0=h[:, :, 2 * F:2 * F + H], in1=zr[:, x % 2, :, H:2 * H], op=ALU.mult).then_inc(s_w2, 1)
                    x = c - 3
                    if is_step(x, loop):
                        n = UNROLL * i + x
                        dve.wait_ge(s_yr, n + 1)
                        for half in range(2):
                            dve.wait_ge(s_u[half], n + 1)
                            if half == 0 and (loop or x >= RING):
                                dve.wait_ge(s_h1, n - RING + 1)
                                dve.wait_ge(s_h2, n - RING + 1)
                                dve.wait_ge(s_psq, n - RING + 1)
                            v.tensor_tensor(out=heads(p[:, x % RING, 2 * half:2 * half + 2, :]),
                                            in0=u_ps[half].rearrange("p (t h d) -> p t h d", t=2, d=D),
                                            in1=yr[:, x % 2, 2 * half:2 * half + 2, :].unsqueeze(3).to_broadcast([P, 2, 2 * H, D]),
                                            op=ALU.mult).then_inc(s_p[half], 1)
                    x = c - 7
                    if is_step(x, loop):
                        n = UNROLL * i + x
                        h = hh[:, x % 2, :, :]
                        if loop or x >= 1:
                            dve.wait_ge(s_qkr, n)
                        if loop or x >= RING:
                            dve.wait_ge(s_qkt, n - RING + 1)
                        v.scalar_tensor_tensor(out=qkr[:, x % RING, :].rearrange("p (t h) -> p t h", h=H),
                                               in0=qkr[:, (x - 1) % RING, :].rearrange("p (t h) -> p t h", h=H),
                                               scalar=step_col(n, 3), in1=h[:, :, 2 * F:2 * F + H],
                                               op0=ALU.mult, op1=ALU.add).then_inc(s_qkr, 1)
                        dve.wait_ge(s_w2, n + 1)
                        v.tensor_tensor(out=heads(h[:, :, F:2 * F]), in0=heads(p[:, x % RING, :, F:2 * F]),
                                        in1=w2[:].unsqueeze(3).to_broadcast([P, TILES, H, D]), op=ALU.mult).then_inc(s_h2, 1)
                every(dve, body, STEPS + 9)


def softmax(nc, a, sem, bank, t):
    f32, bf16, i32 = mybir.dt.float32, mybir.dt.bfloat16, mybir.dt.int32
    ALU, ACT = mybir.AluOpType, mybir.ActivationFunctionType
    qk_t = t["qk_d"].rearrange("g (j h) e -> (g j) h e", h=H)
    with ExitStack() as scope:
        def sb(name, shape, dt=f32):
            return scope.enter_context(nc.sbuf_tensor(name, shape, dt))

        x = sb("m_x", [P, CE])
        m = sb("m_m", [P, CE + 1])
        fresh = sb("m_fresh", [P, CE], bf16)
        ratio = sb("m_ratio", [P, CE])
        junk = sb("m_junk", [P, 2, CE // 7])
        ends = sb("m_ends", [P, 2])
        row = sb("m_row", [1, 2, P])
        row_t = sb("m_row_t", [1, P])
        row_in = sb("m_row_in", [1, P])
        col_in = sb("m_col_in", [P, 2])
        lse_sb = sb("m_lse", [P, 4, 512])
        s_ld, s_ldx, s_neg, s_pre, s_ch, s_tp, s_ex, s_act = (sem("soft_dst_loads"), sem("soft_qk_loads"), sem("soft_minus_max"), sem("soft_pads"), sem("soft_chain"), sem("soft_rows"),
                                                sem("soft_exp"), sem("soft_dve_for_act"))
        s_l, s_lt, s_lc, s_pe = sem("soft_lse"), sem("soft_lse_T"), sem("soft_lse_copied"), sem("soft_for_pe")
        s_ls = [sem(f"soft_lse_stored{i}") for i in range(4)]
        s_cnt = sem("soft_counts")
        d_i = m[:].bitcast(i32)
        C15 = CHUNKS - 1
        FULL = (GROUPS - 1) * TILES - C15 * CT
        REAL = E - C15 * CE
        SUB, NSUB = CE // 7, 7

        def lse_parts(k):
            return -(-min(4 * k + 4, CT) * P // SUB)

        n_loads = []

        with nc.allow_non_contiguous_dma(reason="rows of 512 bytes"), nc.Block() as block:
            @block.gpsimd
            def _(pool):
                nc.gpsimd.memset(x[96:P, REAL:CE], -BIG).then_inc(s_pre, 1)
                nc.gpsimd.memset(d_i[96:P, REAL + 1:CE + 1], -7).then_inc(s_pre, 1)
                nc.gpsimd.memset(d_i[0:32, 0:1], -7).then_inc(s_pre, 1)
                pool.wait_ge(s_pe, 3)
                for k in range(NSUB):
                    lo, hi = k * SUB, (k + 1) * SUB
                    nc.gpsimd.tensor_tensor(out=x[:, lo:hi], in0=x[:, lo:hi], in1=m[:, lo + 1:hi + 1], op=ALU.subtract).then_inc(s_neg, 1)

            @block.sync
            def _(sp):
                n = [0]

                def load(dst_ap, src_ap):
                    sp.dma_start(dst_ap, src_ap).then_inc((s_ld, s_ldx)[len(n_loads)], 16)
                    n[0] += 1

                sp.wait_ge(s_pre, 3)
                for c in range(CHUNKS):
                    rows = slice(H * c, H * c + H)
                    lo = 0 if c else 1
                    hi = CE + 1 if c < C15 else REAL + 1
                    load(d_i[rows, lo:hi], a["dst"][CE * c - 1 + lo:CE * c - 1 + hi].partition_broadcast(H))
                n_loads.append(n[0])
                n[0] = 0
                for c in range(CHUNKS):
                    rows = slice(H * c, H * c + H)
                    k = CT if c < C15 else FULL
                    load(x[rows, 0:k * P].rearrange("h (t e) -> h t e", e=P), qk_t[CT * c:CT * c + k, :, :].rearrange("t h e -> h t e"))
                at, tile0 = FULL * P, (GROUPS - 1) * TILES
                for k in range(DUP // P, TILES):
                    e0 = DUP % P if k == DUP // P else 0
                    load(x[H * C15:P, at:at + P - e0], qk_t[tile0 + k, :, e0:P])
                    at += P - e0
                assert at == REAL
                n_loads.append(n[0])
                sp.dma_start(t["counts"][:], t["sums_d"][:, :, AW - 1:AW].rearrange("b p o -> p (b o)")).then_inc(s_cnt, 16)
                for k in range(-(-CT // 4)):
                    tiles = min(4, CT - 4 * k)
                    sp.wait_ge(s_lc, k + 1)
                    sp.dma_start(t["lse_d"][4 * k * P:(4 * k + tiles) * P, :].rearrange("(t p) c -> p t c", p=P),
                                 lse_sb[:, k % 4, 0:tiles * P].rearrange("p (t c) -> p t c", c=P)).then_inc(s_ls[k % 4], 16)
                K = -(-CT // 4)
                for q in range(4):
                    sp.wait_ge(s_ls[q], 16 * len(range(q, K, 4)))
                sp.wait_ge(s_cnt, 16)

            @block.vector
            def _(dve):
                v = nc.vector
                done = [0]

                def link(ins):
                    done[0] += 1
                    ins.then_inc(s_ch, 1)
                    dve.wait_ge(s_ch, done[0])

                def carry(state, op0, op1, first, part):
                    v.tensor_copy(out=row[:], in_=bank[0][0:1, 0:2 * P].rearrange("o (r c) -> o r c", r=2)).then_inc(s_ch, 1)
                    done[0] += 1
                    dve.wait_ge(s_ch, done[0])
                    for h in range(H):
                        by_c = lambda ap: ap.rearrange("o (c h) -> o c h", h=H)[:, :, h]
                        v.tensor_tensor_scan(out=by_c(row_t[:]), data0=by_c(row[0:1, 1, :]), data1=by_c(row[0:1, 0, :]),
                                             initial=first, op0=op0, op1=op1).then_inc(s_ch, 1)
                        done[0] += 1
                    dve.wait_ge(s_ch, done[0])
                    link(v.memset(row_in[0:1, 0:H], first))
                    v.tensor_copy(out=row_in[0:1, H:P], in_=row_t[0:1, 0:P - H]).then_inc(s_ch, 1)
                    done[0] += 1
                    dve.wait_ge(s_ch, done[0])
                    v.tensor_copy(out=junk[0:1, 0, 0:1], in_=row_in[0:1, 0:1]).then_inc(s_pe, 1)

                dve.wait_ge(s_ld, 16 * n_loads[0])
                link(v.tensor_tensor(out=fresh[:], in0=d_i[:, 1:CE + 1], in1=d_i[:, 0:CE], op=ALU.not_equal))
                link(v.tensor_scalar(out=fresh[:], in0=fresh[:], scalar1=-BIG, scalar2=None, op0=ALU.mult))
                link(v.tensor_tensor(out=ends[:, 1:2], in0=d_i[:, CE:CE + 1], in1=d_i[:, 0:1], op=ALU.not_equal))
                link(v.tensor_scalar(out=ends[:, 1:2], in0=ends[:, 1:2], scalar1=-BIG, scalar2=None, op0=ALU.mult))
                dve.wait_ge(s_ldx, 16 * n_loads[1])
                link(v.tensor_tensor_scan(out=m[:, 1:CE + 1], data0=fresh[:], data1=x[:], initial=-BIG, op0=ALU.add, op1=ALU.max))
                v.tensor_copy(out=ends[:, 0:1], in_=m[:, CE:CE + 1]).then_inc(s_pe, 1)
                dve.wait_ge(s_tp, 1)
                carry(0, ALU.add, ALU.max, -BIG, 0)
                dve.wait_ge(s_tp, 2)
                link(v.tensor_copy(out=col_in[:, 0:1], in_=bank[1][:, 0:1]))
                link(v.tensor_copy(out=m[:, 0:1], in_=col_in[:, 0:1]))
                link(v.tensor_tensor_scan(out=m[:, 1:CE + 1], data0=fresh[:], data1=x[:], initial=col_in[:, 0:1], op0=ALU.add, op1=ALU.max))
                v.tensor_copy(out=junk[0:1, 1, 0:1], in_=m[0:1, CE:CE + 1]).then_inc(s_pe, 1)
                for k in range(NSUB):
                    lo, hi = k * SUB, (k + 1) * SUB
                    link(v.tensor_tensor(out=ratio[:, lo:hi], in0=m[:, lo:hi], in1=m[:, lo + 1:hi + 1], op=ALU.subtract))
                    v.tensor_tensor(out=ratio[:, lo:hi], in0=ratio[:, lo:hi], in1=fresh[:, lo:hi], op=ALU.add).then_inc(s_act, 1)
                link(v.tensor_tensor(out=ends[:, 0:1], in0=col_in[:, 0:1], in1=m[:, CE:CE + 1], op=ALU.subtract))
                v.tensor_tensor(out=ends[:, 1:2], in0=ends[:, 0:1], in1=ends[:, 1:2], op=ALU.add).then_inc(s_act, 1)
                for k in range(NSUB):
                    lo, hi = k * SUB, (k + 1) * SUB
                    dve.wait_ge(s_ex, 2 * (k + 1))
                    link(v.tensor_tensor_scan(out=junk[:, k % 2, :], data0=ratio[:, lo:hi], data1=x[:, lo:hi],
                                              initial=0.0 if k == 0 else junk[:, (k - 1) % 2, SUB - 1:SUB], op0=ALU.mult, op1=ALU.add))
                dve.wait_ge(s_ex, 2 * NSUB + 1)
                v.tensor_copy(out=ends[:, 0:1], in_=junk[:, (NSUB - 1) % 2, SUB - 1:SUB]).then_inc(s_pe, 1)
                dve.wait_ge(s_tp, 3)
                carry(1, ALU.mult, ALU.add, 0.0, 1)
                dve.wait_ge(s_tp, 4)
                link(v.tensor_copy(out=col_in[:, 1:2], in_=bank[1][:, 0:1]))
                for k in range(NSUB):
                    lo, hi = k * SUB, (k + 1) * SUB
                    v.tensor_tensor_scan(out=x[:, lo:hi], data0=ratio[:, lo:hi], data1=x[:, lo:hi],
                                         initial=col_in[:, 1:2] if k == 0 else junk[:, k % 2, 0:1], op0=ALU.mult, op1=ALU.add).then_inc(s_ch, 1)
                    done[0] += 1
                    dve.wait_ge(s_ch, done[0])
                    v.tensor_copy(out=junk[:, (k + 1) % 2, 0:1], in_=x[:, hi - 1:hi]).then_inc(s_act, 1)
                    dve.wait_ge(s_act, NSUB + 1 + k + 1)
                    if k >= 1:
                        dve.wait_ge(s_ex, 2 * NSUB + 1 + k)
                        v.tensor_tensor(out=x[:, lo - SUB:lo], in0=x[:, lo - SUB:lo], in1=m[:, lo - SUB + 1:lo + 1], op=ALU.add).then_inc(s_l, 1)
                dve.wait_ge(s_ex, 3 * NSUB + 1)
                v.tensor_tensor(out=x[:, CE - SUB:CE], in0=x[:, CE - SUB:CE], in1=m[:, CE - SUB + 1:CE + 1], op=ALU.add).then_inc(s_l, 1)

            @block.scalar
            def _(act):
                for k in range(NSUB):
                    lo, hi = k * SUB, (k + 1) * SUB
                    act.wait_ge(s_neg, k + 1)
                    nc.scalar.activation(x[:, lo:hi], x[:, lo:hi], ACT.Exp).then_inc(s_ex, 1)
                    act.wait_ge(s_act, k + 1)
                    nc.scalar.activation(ratio[:, lo:hi], ratio[:, lo:hi], ACT.Exp).then_inc(s_ex, 1)
                act.wait_ge(s_act, NSUB + 1)
                nc.scalar.activation(ends[:, 1:2], ends[:, 1:2], ACT.Exp).then_inc(s_ex, 1)
                copied = 0
                for k in range(NSUB + 1):
                    lo, hi = k * SUB, (k + 1) * SUB
                    if k < NSUB:
                        act.wait_ge(s_act, NSUB + 1 + k + 1)
                        nc.scalar.activation(x[:, lo:hi], x[:, lo:hi], ACT.Ln).then_inc(s_ex, 1)
                    while copied < -(-CT // 4) and (k == NSUB or lse_parts(copied) <= k - 1):
                        tiles = min(4, CT - 4 * copied)
                        act.wait_ge(s_lt, copied + 1)
                        if copied >= 4:
                            act.wait_ge(s_ls[copied % 4], 16 * (copied // 4))
                        nc.scalar.activation(lse_sb[:, copied % 4, 0:tiles * P], bank[2 + copied % 4][:, 0:tiles * P], ACT.Copy).then_inc(s_lc, 1)
                        copied += 1

            @block.tensor
            def _(pe):
                for part in range(2):
                    pe.wait_ge(s_pe, 3 * part + 1)
                    nc.tensor.transpose(bank[0][0:1, 0:P], ends[:, 0:1], t["ident"][:])
                    nc.tensor.transpose(bank[0][0:1, P:2 * P], ends[:, 1:2], t["ident"][:]).then_inc(s_tp, 1)
                    pe.wait_ge(s_pe, 3 * part + 2)
                    nc.tensor.matmul(bank[1][:, 0:1], row_in[0:1, :], t["one_c"][0:1, 0:1], start=True, stop=True).then_inc(s_tp, 1)
                for k in range(-(-CT // 4)):
                    tiles = min(4, CT - 4 * k)
                    pe.wait_ge(s_l, lse_parts(k))
                    if k >= 4:
                        pe.wait_ge(s_lc, k - 3)
                    for j in range(tiles):
                        last = nc.tensor.transpose(bank[2 + k % 4][:, j * P:(j + 1) * P], x[:, (4 * k + j) * P:(4 * k + j + 1) * P], t["ident"][:])
                    last.then_inc(s_lt, 1)


def finish(nc, a, sem, bank, t, out):
    f32, i32, u32 = mybir.dt.float32, mybir.dt.int32, mybir.dt.uint32
    ALU, ACT, AX = mybir.AluOpType, mybir.ActivationFunctionType, mybir.AxisListType
    ident, rows16 = t["ident"], t["rows16"]
    ZB, ZG, ZBETA = 4, 5, 6
    NBK = 2
    TURNS = BLOCKS // NBK
    assert TURNS % 2 == 0 and BLOCKS % NBK == 1
    with ExitStack() as scope:
        def sb(name, shape, dt=f32):
            return scope.enter_context(nc.sbuf_tensor(name, shape, dt))

        tri = sb("f_tri", [P, P])
        ones = sb("f_ones", [P, P])
        tot = sb("f_tot", [P, BLOCKS])
        pre = sb("f_pre", [P, BLOCKS])
        end = sb("f_end", [P, BLOCKS])
        thr_i = sb("f_thr_i", [P, CHUNKS + 1], i32)
        thr = sb("f_thr", [P, CHUNKS + 1])
        ge = sb("f_ge", [P, BLOCKS, CHUNKS + 1])
        oc = sb("f_oc", [P, BLOCKS, CHUNKS])
        nc_ = sb("f_nc", [P, BLOCKS])
        idx = sb("f_idx", [P, BLOCKS + 3], i32)
        idc = sb("f_idc", [P, 2, NBK], i32)
        sm = sb("f_sm", [P, 2, NBK, AW])
        xb = sb("f_x", [P, 2, NBK, F])
        lg = sb("f_lg", [P, 2, NBK, P])
        lt = sb("f_lt", [P, NBK, P])
        lse = sb("f_lse", [P, NBK, H])
        lc = sb("f_lc", [P, NBK, H])
        tq = sb("f_tq", [P, NBK, H])
        a1 = sb("f_a1", [P, NBK, F])
        ag = sb("f_ag", [P, NBK, F])
        agt = sb("f_agt", [P, 2, NBK, P])
        u = sb("f_u", [P, 2, NBK, F])
        z = sb("f_z", [P, NBK, F])
        zr = sb("f_zr", [P, NBK, F])
        mean = sb("f_mean", [P, NBK, H])
        zc = sb("f_zc", [P, 2, NBK, F])
        zn = sb("f_zn", [P, 2, NBK, F])
        zq = sb("f_zq", [P, NBK, F])
        var = sb("f_var", [P, NBK, H])
        lnv = sb("f_lnv", [P, NBK, H])
        r = sb("f_r", [P, 2, NBK, H])
        y = sb("f_y", [P, NBK, F])
        m1 = sb("f_m1", [P, NBK])
        yc = sb("f_yc", [P, 2, NBK, F])
        yq = sb("f_yq", [P, NBK, F])
        v1 = sb("f_v1", [P, NBK])
        l1 = sb("f_l1", [P, NBK])
        r1 = sb("f_r1", [P, 2, NBK])
        o = sb("f_o", [P, 2, NBK, F])
        s_k, s_ch, s_t = sem("fin_consts"), sem("fin_chain"), sem("fin_prefix")
        with nc.Block() as block:
            @block.gpsimd
            def _(pool):
                nc.gpsimd.memset(tri[:], 1.0).then_inc(s_k, 1)
                nc.gpsimd.memset(ones[:], 1.0).then_inc(s_k, 1)
                nc.gpsimd.iota(thr_i[:], pattern=[[CE, CHUNKS + 1]], base=0, channel_multiplier=0).then_inc(s_k, 1)
                pool.wait_ge(s_k, 1)
                nc.gpsimd.affine_select(out=tri[:], in_=tri[:], compare_op=ALU.is_ge, fill=0.0, base=0,
                                        pattern=[[1, P]], channel_multiplier=-1).then_inc(s_k, 1)

            @block.tensor
            def _(pe):
                pe.wait_ge(s_k, 4)
                nc.tensor.matmul(bank[0][:, 0:BLOCKS], tri[:], t["counts"][:], start=True, stop=True)
                nc.tensor.matmul(bank[1][:, 0:BLOCKS], ones[:], t["counts"][:], start=True, stop=True).then_inc(s_t, 1)

            @block.vector
            def _(dve):
                v = nc.vector
                done = [0]

                def link(ins):
                    done[0] += 1
                    ins.then_inc(s_ch, 1)
                    dve.wait_ge(s_ch, done[0])

                dve.wait_ge(s_k, 4)
                link(v.tensor_copy(out=thr[:], in_=thr_i[:]))
                link(v.memset(idx[:], 0))
                dve.wait_ge(s_t, 1)
                link(v.tensor_copy(out=tot[:], in_=bank[1][:, 0:BLOCKS]))
                link(v.memset(ge[:, :, 0], 0.0))
                link(v.tensor_tensor_scan(out=pre[:], data0=tot[:], data1=ge[:, :, 0], initial=0.0, op0=ALU.add, op1=ALU.add))
                link(v.tensor_tensor(out=pre[:], in0=pre[:], in1=tot[:], op=ALU.subtract))
                link(v.tensor_tensor(out=end[:], in0=pre[:], in1=bank[0][:, 0:BLOCKS], op=ALU.add))
                link(v.tensor_scalar(out=end[:], in0=end[:], scalar1=-1.0, scalar2=0.0, op0=ALU.add, op1=ALU.max))
                link(v.tensor_tensor(out=ge[:], in0=end[:].unsqueeze(2).to_broadcast([P, BLOCKS, CHUNKS + 1]),
                                     in1=thr[:].unsqueeze(1).to_broadcast([P, BLOCKS, CHUNKS + 1]), op=ALU.is_ge))
                link(v.tensor_tensor(out=oc[:], in0=ge[:, :, 0:CHUNKS], in1=ge[:, :, 1:CHUNKS + 1], op=ALU.subtract))
                link(v.tensor_reduce(out=nc_[:], in_=ge[:, :, 1:CHUNKS + 1], axis=AX.X, op=ALU.add))
                link(v.scalar_tensor_tensor(out=end[:], in0=nc_[:], scalar=-float(CE), in1=end[:], op0=ALU.mult, op1=ALU.add))
                link(v.tensor_copy(out=idx[:, 0:BLOCKS], in_=end[:]))

        LAG_A, LAG_B, LAG_C, LAG_D, LAG_O, FIRST = 1, 2, 3, 4, 5, 8
        s_in = [sem(f"fin_sums_loaded{i}") for i in range(2)]
        s_x = [sem(f"fin_x_loaded{i}") for i in range(2)]
        s_g = [sem(f"fin_lse_gathered{i}") for i in range(2)]
        s_o = [sem(f"fin_stored{i}") for i in range(2)]
        names = ("idc lt lse lc a1 ag tq agt_ps agt z_ps u z zb relu mean zc zq var lnv r zn zg zbeta y m1 yc yq v1 l1 r1 o").split()
        s = {n: sem("fin_" + n) for n in names}

        def every(eng, body, lag):
            for c in range(FIRST):
                body(c, 0, False)
            with eng.Fori(0, (TURNS - FIRST) // 2) as i:
                for u_ in range(2):
                    body(FIRST + u_, i, True)
            for c in range(TURNS, TURNS + 1 + lag):
                body(c, 0, False)

        def turn(x, i, loop):
            if not loop and not 0 <= x <= TURNS:
                return None
            n = x + 2 * i
            nb, rows = (NBK, P) if loop or x < TURNS else (1, LAST)
            return n, x % 2, nb, slice(0, rows), rows, loop or x >= 1, loop or x >= 2

        def use(x, i):
            return i + (x // 2 + 1)

        with nc.Block() as block:
            @block.sync
            def _(sp):
                def body(c, i, loop):
                    t_ = turn(c, i, loop)
                    if t_:
                        n, k, nb, rr, rows, _, two = t_
                        if two:
                            sp.wait_ge(s["ag"], n - 1)
                            sp.wait_ge(s["tq"], n - 1)
                        sp.dma_start(sm[rr, k, 0:nb, :], t["sums_d"][bass.ds(NBK * n, nb), rr, :].rearrange("b p c -> p b c")).then_inc(s_in[k], 16)
                    t_ = turn(c - LAG_C, i, loop)
                    if t_:
                        n, k, nb, rr, rows, _, two = t_
                        if two:
                            sp.wait_ge(s["y"], n - 1)
                        sp.dma_start(xb[rr, k, 0:nb, :],
                                     a["x"][bass.ds(P * NBK * n, nb * rows), :].rearrange("(b p) f -> p b f", p=rows)).then_inc(s_x[k], 16)
                    t_ = turn(c - LAG_O, i, loop)
                    if t_:
                        n, k, nb, rr, rows, _, _ = t_
                        sp.wait_ge(s["o"], n + 1)
                        sp.dma_start(out[bass.ds(P * NBK * n, nb * rows), :].rearrange("(b p) f -> p b f", p=rows), o[rr, k, 0:nb, :]).then_inc(s_o[k], 16)
                every(sp, body, LAG_O)
                sp.wait_ge(s_o[0], 16 * (TURNS // 2 + 1))
                sp.wait_ge(s_o[1], 16 * (TURNS // 2))

            @block.gpsimd
            def _(pool):
                g = nc.gpsimd
                last_row = pool.alloc_register("last_row")
                rows_less_2 = pool.to_reg(CE - 2)

                def body(c, i, loop):
                    t_ = turn(c, i, loop)
                    if t_:
                        n, k, nb, rr, rows, _, two = t_
                        if two:
                            pool.wait_ge(s["lt"], n - 1)
                        g.tensor_copy(out=idc[:, k, 0:nb], in_=idx[:, bass.ds(NBK * n, nb)]).then_inc(s["idc"], 1)
                        pool.wait_ge(s["idc"], n + 1)
                        pool.reg_add(last_row, rows_less_2, 1)
                        for b in range(nb):
                            pool.indirect_dma_start(out=lg[:, k, b, :], out_offset=None, in_=t["lse_d"],
                                                    in_offset=bass.IndirectOffsetOnAxis(ap=idc[:, k, b:b + 1].bitcast(u32), axis=0),
                                                    bounds_check=last_row, oob_is_err=True).then_inc(s_g[k], 16)
                    t_ = turn(c - LAG_C, i, loop)
                    if t_:
                        n, k, nb, rr, rows, _, _ = t_
                        r16 = lambda j: rows16[rr, j, :].unsqueeze(1).to_broadcast([rows, nb * H, D])
                        hd = lambda ap: ap.rearrange("p b (h d) -> p (b h) d", d=D)
                        pool.wait_ge(s["zn"], n + 1)
                        g.tensor_tensor(out=hd(zn[rr, k, 0:nb, :]), in0=hd(zn[rr, k, 0:nb, :]), in1=r16(ZG), op=ALU.mult).then_inc(s["zg"], 1)
                        pool.wait_ge(s["zg"], n + 1)
                        g.tensor_tensor(out=hd(zn[rr, k, 0:nb, :]), in0=hd(zn[rr, k, 0:nb, :]), in1=r16(ZBETA), op=ALU.add).then_inc(s["zbeta"], 1)
                every(pool, body, LAG_C)

            @block.tensor
            def _(pe):
                def body(c, i, loop):
                    t_ = turn(c - LAG_A, i, loop)
                    if t_:
                        n, k, nb, rr, rows, one, two = t_
                        pe.wait_ge(s["ag"], n + 1)
                        if one:
                            pe.wait_ge(s["agt"], n)
                        for b in range(nb):
                            last = nc.tensor.transpose(bank[0][:, b * P:b * P + rows], ag[rr, b, :], ident[rr, rr])
                        last.then_inc(s["agt_ps"], 1)
                        pe.wait_ge(s["agt"], n + 1)
                        if two:
                            pe.wait_ge(s["z"], n - 1)
                        for b in range(nb):
                            last = nc.tensor.matmul(bank[1 + k][rr, b * F:(b + 1) * F], agt[:, k, b, rr], t["z_w"][:], start=True, stop=True)
                        last.then_inc(s["z_ps"], 1)
                every(pe, body, LAG_A)

            @block.scalar
            def _(act):
                def body(c, i, loop):
                    sc = nc.scalar
                    B, A, Dd = turn(c - LAG_B, i, loop), turn(c - LAG_A, i, loop), turn(c - LAG_D, i, loop)
                    if B:
                        n, k, nb, rr, rows, one, _ = B
                        act.wait_ge(s["zb"], n + 1)
                        if one:
                            act.wait_ge(s["zc"], n)
                        sc.activation(zr[rr, 0:nb, :], z[rr, 0:nb, :], ACT.Relu).then_inc(s["relu"], 1)
                    if A:
                        n, k, nb, rr, rows, _, two = A
                        act.wait_ge(s["agt_ps"], n + 1)
                        if two:
                            act.wait_ge(s["z_ps"], n - 1)
                        sc.activation(agt[:, k, 0:nb, rr], bank[0][:, 0:nb * P].rearrange("p (b n) -> p b n", n=P)[:, :, rr], ACT.Copy).then_inc(s["agt"], 1)
                    if B:
                        n, k, nb, rr, rows, one, _ = B
                        act.wait_ge(s["zc"], n + 1)
                        if one:
                            act.wait_ge(s["var"], n)
                        sc.activation(zq[rr, 0:nb, :], zc[rr, k, 0:nb, :], ACT.Square).then_inc(s["zq"], 1)
                    if Dd:
                        n, k, nb, rr, rows, one, _ = Dd
                        act.wait_ge(s["yc"], n + 1)
                        if one:
                            act.wait_ge(s["v1"], n)
                        sc.activation(yq[rr, 0:nb, :], yc[rr, k, 0:nb, :], ACT.Square).then_inc(s["yq"], 1)
                    if B:
                        n, k, nb, rr, rows, one, _ = B
                        act.wait_ge(s["var"], n + 1)
                        if one:
                            act.wait_ge(s["r"], n)
                        sc.activation(lnv[rr, 0:nb, :], var[rr, 0:nb, :], ACT.Ln, bias=t["eps_c"][rr, 0:1], scale=1.0 / D).then_inc(s["lnv"], 1)
                    if Dd:
                        n, k, nb, rr, rows, one, _ = Dd
                        act.wait_ge(s["v1"], n + 1)
                        if one:
                            act.wait_ge(s["r1"], n)
                        sc.activation(l1[rr, 0:nb], v1[rr, 0:nb], ACT.Ln, bias=t["eps_c"][rr, 0:1], scale=1.0 / F).then_inc(s["l1"], 1)
                    if B:
                        n, k, nb, rr, rows, _, two = B
                        act.wait_ge(s["lnv"], n + 1)
                        if two:
                            act.wait_ge(s["zn"], n - 1)
                        sc.activation(r[rr, k, 0:nb, :], lnv[rr, 0:nb, :], ACT.Exp, scale=-0.5).then_inc(s["r"], 1)
                    if Dd:
                        n, k, nb, rr, rows, _, two = Dd
                        act.wait_ge(s["l1"], n + 1)
                        if two:
                            act.wait_ge(s["o"], n - 1)
                        sc.activation(r1[rr, k, 0:nb], l1[rr, 0:nb], ACT.Exp, scale=-0.5).then_inc(s["r1"], 1)
                every(act, body, LAG_D)

            @block.vector
            def _(dve):
                v = nc.vector
                hd = lambda ap: ap.rearrange("p b (h d) -> p b h d", d=D)
                hf = lambda ap: ap.rearrange("p b (h d) -> p (b h) d", d=D)

                def body(c, i, loop):
                    A, B, C, Dd, O = (turn(c - lag, i, loop) for lag in (LAG_A, LAG_B, LAG_C, LAG_D, LAG_O))
                    if C:
                        n, k, nb, rr, rows, _, two = C
                        dve.wait_ge(s["r"], n + 1)
                        dve.wait_ge(s["zc"], n + 1)
                        if two:
                            dve.wait_ge(s["y"], n - 1)
                        v.tensor_tensor(out=hd(zn[rr, k, 0:nb, :]), in0=hd(zc[rr, k, 0:nb, :]),
                                        in1=r[rr, k, 0:nb, :].unsqueeze(3).to_broadcast([rows, nb, H, D]), op=ALU.mult).then_inc(s["zn"], 1)
                    if B:
                        n, k, nb, rr, rows, one, _ = B
                        dve.wait_ge(s["u"], n + 1)
                        dve.wait_ge(s["z_ps"], n + 1)
                        if one:
                            dve.wait_ge(s["relu"], n)
                        v.tensor_tensor(out=z[rr, 0:nb, :], in0=bank[1 + k][rr, 0:nb * F].rearrange("p (b f) -> p b f", f=F),
                                        in1=u[rr, k, 0:nb, :], op=ALU.add).then_inc(s["z"], 1)
                    if A:
                        n, k, nb, rr, rows, one, _ = A
                        dve.wait_ge(s_g[k], 16 * NBK * (use(c - LAG_A, i) - 1) + 16 * nb)
                        if one:
                            dve.wait_ge(s["lse"], n)
                        v.tensor_tensor(out=lt[rr, 0:nb, :].rearrange("p b (c h) -> p b c h", h=H),
                                        in0=lg[rr, k, 0:nb, :].rearrange("p b (c h) -> p b c h", h=H),
                                        in1=oc[rr, bass.ds(NBK * n, nb), :].unsqueeze(3).to_broadcast([rows, nb, CHUNKS, H]), op=ALU.mult).then_inc(s["lt"], 1)
                    if B:
                        n, k, nb, rr, rows, _, _ = B
                        dve.wait_ge(s["z"], n + 1)
                        v.tensor_tensor(out=hf(z[rr, 0:nb, :]), in0=hf(z[rr, 0:nb, :]),
                                        in1=rows16[rr, ZB, :].unsqueeze(1).to_broadcast([rows, nb * H, D]), op=ALU.add).then_inc(s["zb"], 1)
                    if A:
                        n, k, nb, rr, rows, one, _ = A
                        dve.wait_ge(s["lt"], n + 1)
                        if one:
                            dve.wait_ge(s["lc"], n)
                            dve.wait_ge(s["a1"], n)
                        v.tensor_reduce(out=lse[rr, 0:nb, :], in_=lt[rr, 0:nb, :].rearrange("p b (c h) -> p b h c", h=H), axis=AX.X, op=ALU.add).then_inc(s["lse"], 1)
                    if Dd:
                        n, k, nb, rr, rows, one, _ = Dd
                        dve.wait_ge(s["zbeta"], n + 1)
                        dve.wait_ge(s_x[k], 16 * use(c - LAG_D, i))
                        if one:
                            dve.wait_ge(s["yc"], n)
                        v.tensor_tensor(out=y[rr, 0:nb, :], in0=zn[rr, k, 0:nb, :], in1=xb[rr, k, 0:nb, :], op=ALU.add).then_inc(s["y"], 1)
                    if B:
                        n, k, nb, rr, rows, _, _ = B
                        dve.wait_ge(s["relu"], n + 1)
                        v.tensor_reduce(out=mean[rr, 0:nb, :], in_=hd(zr[rr, 0:nb, :]), axis=AX.X, op=ALU.add).then_inc(s["mean"], 1)
                    if A:
                        n, k, nb, rr, rows, _, _ = A
                        dve.wait_ge(s["lse"], n + 1)
                        dve.wait_ge(s_in[k], 16 * use(c - LAG_A, i))
                        if one:
                            dve.wait_ge(s["tq"], n)
                            dve.wait_ge(s["ag"], n)
                        v.tensor_tensor(out=lc[rr, 0:nb, :], in0=lse[rr, 0:nb, :],
                                        in1=sm[rr, k, 0:nb, AW - 1:AW].to_broadcast([rows, nb, H]), op=ALU.mult).then_inc(s["lc"], 1)
                        v.tensor_tensor(out=hd(a1[rr, 0:nb, :]), in0=hd(sm[rr, k, 0:nb, 0:F]),
                                        in1=lse[rr, 0:nb, :].unsqueeze(3).to_broadcast([rows, nb, H, D]), op=ALU.mult).then_inc(s["a1"], 1)
                    if B:
                        n, k, nb, rr, rows, _, two = B
                        dve.wait_ge(s["mean"], n + 1)
                        if two:
                            dve.wait_ge(s["zn"], n - 1)
                            dve.wait_ge(s["zq"], n - 1)
                        v.scalar_tensor_tensor(out=hf(zc[rr, k, 0:nb, :]), in0=mean[rr, 0:nb, :].rearrange("p b h -> p (b h)").unsqueeze(2).to_broadcast([rows, nb * H, D]),
                                               scalar=-1.0 / D, in1=hf(zr[rr, 0:nb, :]), op0=ALU.mult, op1=ALU.add).then_inc(s["zc"], 1)
                    if A:
                        n, k, nb, rr, rows, one, _ = A
                        dve.wait_ge(s["a1"], n + 1)
                        if one:
                            dve.wait_ge(s["agt_ps"], n)
                        v.tensor_tensor(out=ag[rr, 0:nb, :], in0=sm[rr, k, 0:nb, F:2 * F], in1=a1[rr, 0:nb, :], op=ALU.subtract).then_inc(s["ag"], 1)
                    if Dd:
                        n, k, nb, rr, rows, _, _ = Dd
                        dve.wait_ge(s["y"], n + 1)
                        v.tensor_reduce(out=m1[rr, 0:nb], in_=y[rr, 0:nb, :], axis=AX.X, op=ALU.add).then_inc(s["m1"], 1)
                    if A:
                        n, k, nb, rr, rows, one, _ = A
                        dve.wait_ge(s["lc"], n + 1)
                        if one:
                            dve.wait_ge(s["u"], n)
                        v.tensor_tensor(out=tq[rr, 0:nb, :], in0=sm[rr, k, 0:nb, 2 * F:2 * F + H], in1=lc[rr, 0:nb, :], op=ALU.subtract).then_inc(s["tq"], 1)
                    if Dd:
                        n, k, nb, rr, rows, _, two = Dd
                        dve.wait_ge(s["m1"], n + 1)
                        if two:
                            dve.wait_ge(s["o"], n - 1)
                            dve.wait_ge(s["yq"], n - 1)
                        v.scalar_tensor_tensor(out=yc[rr, k, 0:nb, :], in0=m1[rr, 0:nb].unsqueeze(2).to_broadcast([rows, nb, F]), scalar=-1.0 / F,
                                               in1=y[rr, 0:nb, :], op0=ALU.mult, op1=ALU.add).then_inc(s["yc"], 1)
                    if A:
                        n, k, nb, rr, rows, _, two = A
                        dve.wait_ge(s["tq"], n + 1)
                        if two:
                            dve.wait_ge(s["z"], n - 1)
                        v.tensor_tensor(out=hd(u[rr, k, 0:nb, :]), in0=t["z_beta_w"][rr, :].rearrange("p (h d) -> p h d", d=D).unsqueeze(1).to_broadcast([rows, nb, H, D]),
                                        in1=tq[rr, 0:nb, :].unsqueeze(3).to_broadcast([rows, nb, H, D]), op=ALU.mult).then_inc(s["u"], 1)
                    if O:
                        n, k, nb, rr, rows, _, two = O
                        dve.wait_ge(s["r1"], n + 1)
                        dve.wait_ge(s["yc"], n + 1)
                        if two:
                            dve.wait_ge(s_o[k], 16 * (use(c - LAG_O, i) - 1))
                        v.tensor_tensor(out=o[rr, k, 0:nb, :], in0=yc[rr, k, 0:nb, :], in1=r1[rr, k, 0:nb].unsqueeze(2).to_broadcast([rows, nb, F]),
                                        op=ALU.mult).then_inc(s["o"], 1)
                    if B:
                        n, k, nb, rr, rows, one, _ = B
                        dve.wait_ge(s["zq"], n + 1)
                        if one:
                            dve.wait_ge(s["lnv"], n)
                        v.tensor_reduce(out=var[rr, 0:nb, :], in_=hd(zq[rr, 0:nb, :]), axis=AX.X, op=ALU.add).then_inc(s["var"], 1)
                    if Dd:
                        n, k, nb, rr, rows, one, _ = Dd
                        dve.wait_ge(s["yq"], n + 1)
                        if one:
                            dve.wait_ge(s["l1"], n)
                        v.tensor_reduce(out=v1[rr, 0:nb], in_=yq[rr, 0:nb, :], axis=AX.X, op=ALU.add).then_inc(s["v1"], 1)
                every(dve, body, LAG_O)


_WEIGHTS = ["Wq", "Wk", "Wv", "Wke", "Wve", "gq", "bq", "gk", "bk", "gv", "bv", "gke", "bke", "gve", "bve",
            "relk_W", "relk_b", "relk_g", "relk_beta", "relv_W", "relv_b", "relv_g", "relv_beta", "z_W", "z_b", "z_g", "z_beta"]


def kernel(**inputs):
    import concourse.bacc as _bacc
    from concourse.bass_utils import run_bass_kernel_spmd as _run

    nc = _bacc.Bacc("TRN2", target_bir_lowering=False, num_devices=1)
    arrays, aps = {}, {}
    names = {"x": "x", "src": "src", "dst": "dst", "edge_attr_128": "edge_attr_128"}
    names.update({w: "L0_gnn_" + w for w in _WEIGHTS})
    for short, name in names.items():
        arr = np.ascontiguousarray(inputs[name])
        arrays["in_" + short] = arr
        aps[short] = nc.dram_tensor("in_" + short, arr.shape, mybir.dt.from_np(arr.dtype), kind="ExternalInput").ap()
    out = nc.dram_tensor("out_0", (N, F), mybir.dt.float32, kind="ExternalOutput").ap()
    edge_attention(nc, aps, out)
    r = _run(nc, [arrays], core_ids=[0])
    return r.results[0]["out_0"]
```
